# Optimizing a Trainium2 kernel written in Bass

```python
import numpy as np
import jax
import jax.numpy as jnp

def _softmax(x, axis=-1):
    return jax.nn.softmax(x, axis=axis)

def _gelu(x):
    return jax.nn.gelu(x, approximate=True)

def _silu(x):
    return jax.nn.silu(x)

def _sigmoid(x):
    return jax.nn.sigmoid(x)

def _layernorm(x, axis=-1, eps=1e-05):
    m = jnp.mean(x, axis=axis, keepdims=True)
    v = jnp.var(x, axis=axis, keepdims=True)
    return (x - m) / jnp.sqrt(v + eps)

def _scatter_add(tgt, idx, src, axis=0):
    return tgt.at[idx].add(src)

def _segment_sum(src, seg, n):
    return jax.ops.segment_sum(src, seg, n)
kernel_name = 'mk_adj_ffn_d4_adj_r2_1bdf22'

def setup_inputs(seed: int=0):
    np.random.seed(seed)
    _w = jnp.asarray

    def _rec_inputs():
        import jax
        import jax.numpy as jnp
        _gk = jax.random.key(seed)
        x = -0.0002928 + 1 * jax.random.normal(jax.random.fold_in(_gk, 1), (16, 512, 128), jnp.float32)
        _a = jax.random.bernoulli(jax.random.fold_in(_gk, 2), 0.03125, (16, 512, 512))
        _a = jnp.logical_or(_a, jnp.swapaxes(_a, -1, -2))
        _a = jnp.logical_or(_a, jnp.eye(512, dtype=bool))
        adj = _a.astype(jnp.int32)
        _nm = jnp.ones((16, 512), dtype=bool)
        nodemask = jnp.where(_nm, 1.0, 0.0).astype(jnp.float32)
        return (x, adj, nodemask)
    x, adj, nodemask = _rec_inputs()

    def _L0_gnn_setup():
        import jax, jax.numpy as jnp
        import numpy as np
        ALPHA = 0.2
        NEG_BIG = -9000000000000000.0
        key = jax.random.key(seed)
        k1, k2, k3, k4 = jax.random.split(key, 4)
        B, N, Fin, Fout = (16, 512, 128, 128)
        h = jax.random.normal(k1, (B, N, Fin), dtype=jnp.float32)
        adj = jax.random.randint(k2, (B, N, N), 0, 2, dtype=jnp.int32)
        mask = jnp.ones((B, N), dtype=jnp.float32)
        gain = 1.414
        limW = gain * np.sqrt(6.0 / (Fin + Fout))
        W = jax.random.uniform(k3, (Fin, Fout), minval=-limW, maxval=limW, dtype=jnp.float32)
        lima = gain * np.sqrt(6.0 / (2 * Fout + 1))
        a = jax.random.uniform(k4, (2 * Fout, 1), minval=-lima, maxval=lima, dtype=jnp.float32)
        return {'h': h, 'adj': adj, 'mask': mask, 'W': W, 'a': a}
    _L0_gnn_all = _L0_gnn_setup()
    _L0_gnn_in = {k: v for k, v in _L0_gnn_all.items() if k in ('W', 'a')}
    del _L0_gnn_all

    def _L0_ffn_setup():
        import jax, jax.numpy as jnp
        import numpy as np
        D_MODEL = 128
        D_STATE = 64
        D_CONV = 4
        EXPAND = 2
        HEADDIM = 64
        D_INNER = EXPAND * D_MODEL
        NHEADS = D_INNER // HEADDIM
        CONV_DIM = D_INNER + 2 * D_STATE
        D_IN_PROJ = 2 * D_INNER + 2 * D_STATE + NHEADS
        CHUNK = 128
        EPS = 1e-05

        def segsum(a):
            T = a.shape[-1]
            cs = jnp.cumsum(a, axis=-1)
            ss = cs[..., :, None] - cs[..., None, :]
            mask = jnp.tril(jnp.ones((T, T), dtype=bool))
            return jnp.where(mask, ss, -jnp.inf)

        def mamba2_block(x, W_in, conv_w, conv_b, dt_bias, A_log, D, norm_w, W_out, W_lin, b_lin):
            Bsz, L, _ = x.shape
            zxbcdt = x @ W_in
            z, xBC, dt = jnp.split(zxbcdt, [D_INNER, D_INNER + CONV_DIM], axis=-1)
            xp = jnp.pad(xBC, ((0, 0), (D_CONV - 1, 0), (0, 0)))
            conv = conv_b + sum((xp[:, k:k + L, :] * conv_w[:, k] for k in range(D_CONV)))
            xBC = jax.nn.silu(conv)
            xh, Bmat, Cmat = jnp.split(xBC, [D_INNER, D_INNER + D_STATE], axis=-1)
            dt = jax.nn.softplus(dt + dt_bias)
            A = -jnp.exp(A_log)
            nc = L // CHUNK
            xh = xh.reshape(Bsz, nc, CHUNK, NHEADS, HEADDIM)
            Bc = Bmat.reshape(Bsz, nc, CHUNK, D_STATE)
            Cc = Cmat.reshape(Bsz, nc, CHUNK, D_STATE)
            dtc = dt.reshape(Bsz, nc, CHUNK, NHEADS)
            dA = jnp.einsum('bclh,h->bhcl', dtc, A)
            A_cum = jnp.cumsum(dA, axis=-1)
            Lmat = jnp.exp(segsum(dA))
            xdt = xh * dtc[..., None]
            Y_diag = jnp.einsum('bcln,bcsn,bhcls,bcshp->bclhp', Cc, Bc, Lmat, xdt)
            decay_states = jnp.exp(A_cum[..., -1:] - A_cum)
            states = jnp.einsum('bcln,bhcl,bclhp->bchpn', Bc, decay_states, xdt)
            chunk_decay = jnp.exp(A_cum[..., -1])

            def step(h, inp):
                s, d = inp
                return (h * d[..., None, None] + s, h)
            _, prevs = jax.lax.scan(step, jnp.zeros_like(states[:, 0]), (jnp.moveaxis(states, 1, 0), jnp.moveaxis(chunk_decay, 2, 0)))
            prevs = jnp.moveaxis(prevs, 0, 1)
            Y_off = jnp.einsum('bcln,bchpn,bhcl->bclhp', Cc, prevs, jnp.exp(A_cum))
            Y = (Y_diag + Y_off + xh * D[:, None]).reshape(Bsz, L, D_INNER)
            Y = Y * jax.nn.silu(z)
            Y = Y * jax.lax.rsqrt(jnp.mean(Y * Y, axis=-1, keepdims=True) + EPS) * norm_w
            out = Y @ W_out
            return out @ W_lin + b_lin
        key = jax.random.key(seed)
        ks = jax.random.split(key, 12)
        B, L = (8, 2048)

        def gauss(k, shape, scale):
            return jax.random.normal(k, shape, dtype=jnp.float32) * scale
        return {'x': gauss(ks[0], (B, L, D_MODEL), 1.0), 'W_in': gauss(ks[1], (D_MODEL, D_IN_PROJ), D_MODEL ** (-0.5)), 'conv_w': gauss(ks[2], (CONV_DIM, D_CONV), 0.3), 'conv_b': gauss(ks[3], (CONV_DIM,), 0.1), 'dt_bias': jax.random.uniform(ks[4], (NHEADS,), minval=-4.0, maxval=-1.0), 'A_log': jnp.log(jax.random.uniform(ks[5], (NHEADS,), minval=1.0, maxval=16.0)), 'D': jnp.ones((NHEADS,), jnp.float32), 'norm_w': jnp.ones((D_INNER,), jnp.float32), 'W_out': gauss(ks[6], (D_INNER, D_MODEL), D_INNER ** (-0.5)), 'W_lin': gauss(ks[7], (D_MODEL, D_MODEL), D_MODEL ** (-0.5)), 'b_lin': jnp.zeros((D_MODEL,), jnp.float32)}
    _L0_ffn_all = _L0_ffn_setup()
    _L0_ffn_in = {k: v for k, v in _L0_ffn_all.items() if k in ('W_in', 'conv_w', 'conv_b', 'dt_bias', 'A_log', 'D', 'norm_w', 'W_out', 'W_lin', 'b_lin')}
    del _L0_ffn_all

    def _L1_gnn_setup():
        import jax, jax.numpy as jnp
        import numpy as np
        NEG_BIG = -9000000000000000.0
        ALPHA = 0.2
        key = jax.random.key(seed)
        k1, k2, k3, k4 = jax.random.split(key, 4)
        B, N, Fin, Fout = (8, 1024, 128, 128)
        h = jax.random.normal(k1, (B, N, Fin), dtype=jnp.float32)
        adj = jax.random.randint(k2, (B, N, N), 0, 2, dtype=jnp.int32)
        limW = 1.414 * np.sqrt(6.0 / (Fin + Fout))
        W = jax.random.uniform(k3, (Fin, Fout), jnp.float32, -limW, limW)
        lima = 1.414 * np.sqrt(6.0 / (2 * Fout + 1))
        a = jax.random.uniform(k4, (2 * Fout, 1), jnp.float32, -lima, lima)
        return {'h': h, 'adj': adj, 'W': W, 'a': a}
    _L1_gnn_all = _L1_gnn_setup()
    _L1_gnn_in = {k: v for k, v in _L1_gnn_all.items() if k in ('W', 'a')}
    del _L1_gnn_all

    def _L1_ffn_setup():
        import jax, jax.numpy as jnp
        import numpy as np
        NUM_EXPERTS = 8
        TOP_K = 2
        B, S, D = (8, 4096, 128)

        def _moe(tokens, router_w, w1, b1, w2, b2):
            N = tokens.shape[0]
            E = router_w.shape[0]
            logits = tokens.astype(jnp.float32) @ router_w.astype(jnp.float32).T
            probs = jax.nn.softmax(logits, axis=-1)
            rw, re = jax.lax.top_k(probs, TOP_K)
            if TOP_K > 1:
                rw = rw / jnp.maximum(rw.sum(-1, keepdims=True), 1e-12)
            rw = rw.astype(tokens.dtype)
            combine = jnp.zeros((N, E), tokens.dtype).at[jnp.arange(N)[:, None], re].set(rw)
            out = tokens
            for e in range(E):
                h = jax.nn.gelu(tokens @ w1[e] + b1[e], approximate=False)
                y = h @ w2[e] + b2[e]
                out = out + combine[:, e:e + 1] * y
            return out
        key = jax.random.key(seed)
        ks = jax.random.split(key, 4)
        scale = 1.0 / np.sqrt(D).astype(np.float32)
        return {'input_embeddings': jax.random.normal(ks[0], (B, S, D), jnp.float32), 'router_w': jax.random.normal(ks[1], (NUM_EXPERTS, D), jnp.float32) * scale, 'w1': jax.random.normal(ks[2], (NUM_EXPERTS, D, D), jnp.float32) * scale, 'b1': jnp.zeros((NUM_EXPERTS, D), jnp.float32), 'w2': jax.random.normal(ks[3], (NUM_EXPERTS, D, D), jnp.float32) * scale, 'b2': jnp.zeros((NUM_EXPERTS, D), jnp.float32)}
    _L1_ffn_all = _L1_ffn_setup()
    _L1_ffn_in = {k: v for k, v in _L1_ffn_all.items() if k in ('router_w', 'w1', 'b1', 'w2', 'b2')}
    del _L1_ffn_all

    def _L2_gnn_setup():
        import jax, jax.numpy as jnp
        import numpy as np
        NEG_BIG = -9000000000000000.0
        LEAKY_SLOPE = 0.2
        key = jax.random.key(seed)
        k1, k2, k3, k4 = jax.random.split(key, 4)
        B, N, F_in, F_out = (8, 1024, 128, 128)
        h = jax.random.normal(k1, (B, N, F_in), dtype=jnp.float32)
        adj = jax.random.randint(k2, (B, N, N), 0, 2, dtype=jnp.int32)
        W = jax.random.normal(k3, (F_out, F_in), dtype=jnp.float32) * (1.414 * (6.0 / (F_in + F_out)) ** 0.5)
        a = jax.random.normal(k4, (2 * F_out, 1), dtype=jnp.float32) * 0.1
        return {'h': h, 'adj': adj, 'W': W, 'a': a}
    _L2_gnn_all = _L2_gnn_setup()
    _L2_gnn_in = {k: v for k, v in _L2_gnn_all.items() if k in ('W', 'a')}
    del _L2_gnn_all

    def _L2_ffn_setup():
        import jax, jax.numpy as jnp
        import numpy as np
        TOP_K = 2
        key = jax.random.key(seed)
        ks = jax.random.split(key, 4)
        B, L, D, H, E = (8, 2048, 128, 512, 8)
        s = 0.02
        return {'x': jax.random.normal(ks[0], (B, L, D), jnp.float32), 'Wg': jax.random.normal(ks[1], (D, E), jnp.float32) * s, 'bg': jnp.zeros((E,), jnp.float32), 'W1': jax.random.normal(ks[2], (E, D, H), jnp.float32) * s, 'b1': jnp.zeros((E, H), jnp.float32), 'W2': jax.random.normal(ks[3], (E, H, D), jnp.float32) * s, 'b2': jnp.zeros((E, D), jnp.float32)}
    _L2_ffn_all = _L2_ffn_setup()
    _L2_ffn_in = {k: v for k, v in _L2_ffn_all.items() if k in ('Wg', 'bg', 'W1', 'b1', 'W2', 'b2')}
    del _L2_ffn_all

    def _L3_gnn_setup():
        import jax, jax.numpy as jnp
        import numpy as np
        B, N, C_IN, H, C_OUT = (8, 512, 128, 4, 128)
        C = C_OUT // H
        ALPHA = 0.2
        NEG_INF = -9000000000000000.0
        key = jax.random.key(seed)
        k1, k2, k3, k4, k5 = jax.random.split(key, 5)
        node_feats = jax.random.normal(k1, (B, N, C_IN), dtype=jnp.float32)
        adj_matrix = jax.random.randint(k2, (B, N, N), 0, 2, dtype=jnp.int32)
        eye = jnp.eye(N, dtype=jnp.int32)[None]
        adj_matrix = jnp.maximum(adj_matrix, eye)

        def xavier(k, shape, fan_in, fan_out, gain=1.414):
            lim = gain * np.sqrt(6.0 / (fan_in + fan_out))
            return jax.random.uniform(k, shape, jnp.float32, -lim, lim)
        W = xavier(k3, (C_OUT, C_IN), C_IN, C_OUT)
        b = jnp.zeros((C_OUT,), dtype=jnp.float32)
        a = xavier(k4, (H, 2 * C), 2 * C, H)
        return {'node_feats': node_feats, 'adj_matrix': adj_matrix, 'W': W, 'b': b, 'a': a}
    _L3_gnn_all = _L3_gnn_setup()
    _L3_gnn_in = {k: v for k, v in _L3_gnn_all.items() if k in ('W', 'b', 'a')}
    del _L3_gnn_all

    def _L3_ffn_setup():
        import jax, jax.numpy as jnp
        import numpy as np
        TOP_K = 2
        LN_EPS = 1e-05
        key = jax.random.key(seed)
        ks = jax.random.split(key, 8)
        B, S, D, E, H = (16, 512, 128, 8, 512)
        x = jax.random.normal(ks[0], (B, S, D), dtype=jnp.float32)
        Wr = jax.random.normal(ks[1], (D, E), dtype=jnp.float32) * 0.1
        br = jnp.zeros((E,), dtype=jnp.float32)
        ln_g = jnp.ones((E, D), dtype=jnp.float32)
        ln_b = jnp.zeros((E, D), dtype=jnp.float32)
        W1 = jax.random.normal(ks[2], (E, D, H), dtype=jnp.float32) * (1.0 / np.sqrt(D))
        b1 = jnp.zeros((E, H), dtype=jnp.float32)
        W2 = jax.random.normal(ks[3], (E, H, D), dtype=jnp.float32) * (1.0 / np.sqrt(H))
        b2 = jnp.zeros((E, D), dtype=jnp.float32)
        return {'x': x, 'Wr': Wr, 'br': br, 'ln_g': ln_g, 'ln_b': ln_b, 'W1': W1, 'b1': b1, 'W2': W2, 'b2': b2}
    _L3_ffn_all = _L3_ffn_setup()
    _L3_ffn_in = {k: v for k, v in _L3_ffn_all.items() if k in ('Wr', 'br', 'ln_g', 'ln_b', 'W1', 'b1', 'W2', 'b2')}
    del _L3_ffn_all
    return {'x': x, 'adj': adj, 'nodemask': nodemask, 'L0_gnn_W': _L0_gnn_in['W'], 'L0_gnn_a': _L0_gnn_in['a'], 'L0_ffn_W_in': _L0_ffn_in['W_in'], 'L0_ffn_conv_w': _L0_ffn_in['conv_w'], 'L0_ffn_conv_b': _L0_ffn_in['conv_b'], 'L0_ffn_dt_bias': _L0_ffn_in['dt_bias'], 'L0_ffn_A_log': _L0_ffn_in['A_log'], 'L0_ffn_D': _L0_ffn_in['D'], 'L0_ffn_norm_w': _L0_ffn_in['norm_w'], 'L0_ffn_W_out': _L0_ffn_in['W_out'], 'L0_ffn_W_lin': _L0_ffn_in['W_lin'], 'L0_ffn_b_lin': _L0_ffn_in['b_lin'], 'L1_gnn_W': _L1_gnn_in['W'], 'L1_gnn_a': _L1_gnn_in['a'], 'L1_ffn_router_w': _L1_ffn_in['router_w'], 'L1_ffn_w1': _L1_ffn_in['w1'], 'L1_ffn_b1': _L1_ffn_in['b1'], 'L1_ffn_w2': _L1_ffn_in['w2'], 'L1_ffn_b2': _L1_ffn_in['b2'], 'L2_gnn_W': _L2_gnn_in['W'], 'L2_gnn_a': _L2_gnn_in['a'], 'L2_ffn_Wg': _L2_ffn_in['Wg'], 'L2_ffn_bg': _L2_ffn_in['bg'], 'L2_ffn_W1': _L2_ffn_in['W1'], 'L2_ffn_b1': _L2_ffn_in['b1'], 'L2_ffn_W2': _L2_ffn_in['W2'], 'L2_ffn_b2': _L2_ffn_in['b2'], 'L3_gnn_W': _L3_gnn_in['W'], 'L3_gnn_b': _L3_gnn_in['b'], 'L3_gnn_a': _L3_gnn_in['a'], 'L3_ffn_Wr': _L3_ffn_in['Wr'], 'L3_ffn_br': _L3_ffn_in['br'], 'L3_ffn_ln_g': _L3_ffn_in['ln_g'], 'L3_ffn_ln_b': _L3_ffn_in['ln_b'], 'L3_ffn_W1': _L3_ffn_in['W1'], 'L3_ffn_b1': _L3_ffn_in['b1'], 'L3_ffn_W2': _L3_ffn_in['W2'], 'L3_ffn_b2': _L3_ffn_in['b2']}

def reference(x, adj, nodemask, L0_gnn_W, L0_gnn_a, L0_ffn_W_in, L0_ffn_conv_w, L0_ffn_conv_b, L0_ffn_dt_bias, L0_ffn_A_log, L0_ffn_D, L0_ffn_norm_w, L0_ffn_W_out, L0_ffn_W_lin, L0_ffn_b_lin, L1_gnn_W, L1_gnn_a, L1_ffn_router_w, L1_ffn_w1, L1_ffn_b1, L1_ffn_w2, L1_ffn_b2, L2_gnn_W, L2_gnn_a, L2_ffn_Wg, L2_ffn_bg, L2_ffn_W1, L2_ffn_b1, L2_ffn_W2, L2_ffn_b2, L3_gnn_W, L3_gnn_b, L3_gnn_a, L3_ffn_Wr, L3_ffn_br, L3_ffn_ln_g, L3_ffn_ln_b, L3_ffn_W1, L3_ffn_b1, L3_ffn_W2, L3_ffn_b2):
    import jax
    import jax.numpy as jnp

    def _L0_gnn_ref(h, adj, mask, W, a):
        import jax, jax.numpy as jnp
        import numpy as np
        ALPHA = 0.2
        NEG_BIG = -9000000000000000.0
        Fout = W.shape[1]
        Wh = jnp.einsum('bni,io->bno', h, W)
        a1 = a[:Fout, 0]
        a2 = a[Fout:, 0]
        f1 = Wh @ a1
        f2 = Wh @ a2
        e = jax.nn.leaky_relu(f1[:, :, None] + f2[:, None, :], negative_slope=ALPHA)
        scores = jnp.where(adj > 0, e, NEG_BIG)
        attention = jax.nn.softmax(scores, axis=2)
        h_prime = jnp.einsum('bij,bjo->bio', attention, Wh)
        h_prime = h_prime * mask[:, :, None]
        return jax.nn.elu(h_prime)

    def _L0_ffn_ref(x, W_in, conv_w, conv_b, dt_bias, A_log, D, norm_w, W_out, W_lin, b_lin):
        import jax, jax.numpy as jnp
        import numpy as np
        D_MODEL = 128
        D_STATE = 64
        D_CONV = 4
        EXPAND = 2
        HEADDIM = 64
        D_INNER = EXPAND * D_MODEL
        NHEADS = D_INNER // HEADDIM
        CONV_DIM = D_INNER + 2 * D_STATE
        D_IN_PROJ = 2 * D_INNER + 2 * D_STATE + NHEADS
        CHUNK = 128
        EPS = 1e-05

        def segsum(a):
            T = a.shape[-1]
            cs = jnp.cumsum(a, axis=-1)
            ss = cs[..., :, None] - cs[..., None, :]
            mask = jnp.tril(jnp.ones((T, T), dtype=bool))
            return jnp.where(mask, ss, -jnp.inf)

        def mamba2_block(x, W_in, conv_w, conv_b, dt_bias, A_log, D, norm_w, W_out, W_lin, b_lin):
            Bsz, L, _ = x.shape
            zxbcdt = x @ W_in
            z, xBC, dt = jnp.split(zxbcdt, [D_INNER, D_INNER + CONV_DIM], axis=-1)
            xp = jnp.pad(xBC, ((0, 0), (D_CONV - 1, 0), (0, 0)))
            conv = conv_b + sum((xp[:, k:k + L, :] * conv_w[:, k] for k in range(D_CONV)))
            xBC = jax.nn.silu(conv)
            xh, Bmat, Cmat = jnp.split(xBC, [D_INNER, D_INNER + D_STATE], axis=-1)
            dt = jax.nn.softplus(dt + dt_bias)
            A = -jnp.exp(A_log)
            nc = L // CHUNK
            xh = xh.reshape(Bsz, nc, CHUNK, NHEADS, HEADDIM)
            Bc = Bmat.reshape(Bsz, nc, CHUNK, D_STATE)
            Cc = Cmat.reshape(Bsz, nc, CHUNK, D_STATE)
            dtc = dt.reshape(Bsz, nc, CHUNK, NHEADS)
            dA = jnp.einsum('bclh,h->bhcl', dtc, A)
            A_cum = jnp.cumsum(dA, axis=-1)
            Lmat = jnp.exp(segsum(dA))
            xdt = xh * dtc[..., None]
            Y_diag = jnp.einsum('bcln,bcsn,bhcls,bcshp->bclhp', Cc, Bc, Lmat, xdt)
            decay_states = jnp.exp(A_cum[..., -1:] - A_cum)
            states = jnp.einsum('bcln,bhcl,bclhp->bchpn', Bc, decay_states, xdt)
            chunk_decay = jnp.exp(A_cum[..., -1])

            def step(h, inp):
                s, d = inp
                return (h * d[..., None, None] + s, h)
            _, prevs = jax.lax.scan(step, jnp.zeros_like(states[:, 0]), (jnp.moveaxis(states, 1, 0), jnp.moveaxis(chunk_decay, 2, 0)))
            prevs = jnp.moveaxis(prevs, 0, 1)
            Y_off = jnp.einsum('bcln,bchpn,bhcl->bclhp', Cc, prevs, jnp.exp(A_cum))
            Y = (Y_diag + Y_off + xh * D[:, None]).reshape(Bsz, L, D_INNER)
            Y = Y * jax.nn.silu(z)
            Y = Y * jax.lax.rsqrt(jnp.mean(Y * Y, axis=-1, keepdims=True) + EPS) * norm_w
            out = Y @ W_out
            return out @ W_lin + b_lin
        return mamba2_block(x, W_in, conv_w, conv_b, dt_bias, A_log, D, norm_w, W_out, W_lin, b_lin)

    def _L1_gnn_ref(h, adj, W, a):
        import jax, jax.numpy as jnp
        import numpy as np
        NEG_BIG = -9000000000000000.0
        ALPHA = 0.2
        Fout = W.shape[1]
        wh = jnp.einsum('bni,io->bno', h, W)
        a1 = a[:Fout, 0]
        a2 = a[Fout:, 0]
        s1 = wh @ a1
        s2 = wh @ a2
        e = jax.nn.leaky_relu(s1[:, :, None] + s2[:, None, :], negative_slope=ALPHA)
        e = jnp.where(adj > 0, e, NEG_BIG)
        attention = jax.nn.softmax(e, axis=2)
        h_prime = jnp.einsum('bmn,bno->bmo', attention, wh)
        return h_prime

    def _L1_ffn_ref(input_embeddings, router_w, w1, b1, w2, b2):
        import jax, jax.numpy as jnp
        import numpy as np
        NUM_EXPERTS = 8
        TOP_K = 2
        B, S, D = (8, 4096, 128)

        def _moe(tokens, router_w, w1, b1, w2, b2):
            N = tokens.shape[0]
            E = router_w.shape[0]
            logits = tokens.astype(jnp.float32) @ router_w.astype(jnp.float32).T
            probs = jax.nn.softmax(logits, axis=-1)
            rw, re = jax.lax.top_k(probs, TOP_K)
            if TOP_K > 1:
                rw = rw / jnp.maximum(rw.sum(-1, keepdims=True), 1e-12)
            rw = rw.astype(tokens.dtype)
            combine = jnp.zeros((N, E), tokens.dtype).at[jnp.arange(N)[:, None], re].set(rw)
            out = tokens
            for e in range(E):
                h = jax.nn.gelu(tokens @ w1[e] + b1[e], approximate=False)
                y = h @ w2[e] + b2[e]
                out = out + combine[:, e:e + 1] * y
            return out
        b, s, d = input_embeddings.shape
        tokens = input_embeddings.reshape(b * s, d)
        return _moe(tokens, router_w, w1, b1, w2, b2).reshape(b, s, d)

    def _L2_gnn_ref(h, adj, W, a):
        import jax, jax.numpy as jnp
        import numpy as np
        NEG_BIG = -9000000000000000.0
        LEAKY_SLOPE = 0.2
        Wh = jnp.einsum('bnf,of->bno', h, W)
        F_out = W.shape[0]
        a1 = a[:F_out, 0]
        a2 = a[F_out:, 0]
        s1 = Wh @ a1
        s2 = Wh @ a2
        e = s1[:, :, None] + s2[:, None, :]
        e = jax.nn.leaky_relu(e, negative_slope=LEAKY_SLOPE)
        e = jnp.where(adj == 0, NEG_BIG, e)
        attention = jax.nn.softmax(e, axis=-1)
        h_prime = jnp.einsum('bij,bjf->bif', attention, Wh)
        return jax.nn.elu(h_prime)

    def _L2_ffn_ref(x, Wg, bg, W1, b1, W2, b2):
        import jax, jax.numpy as jnp
        import numpy as np
        TOP_K = 2
        B, L, D = x.shape
        E = W1.shape[0]
        xf = x.reshape(-1, D)
        gate_logits = xf @ Wg + bg
        top_w, top_i = jax.lax.top_k(gate_logits, TOP_K)
        top_w = jax.nn.softmax(top_w, axis=-1)
        w_dense = jnp.sum(jax.nn.one_hot(top_i, E, dtype=xf.dtype) * top_w[..., None], axis=1)
        out = jnp.zeros_like(xf)
        for e in range(E):
            h = jax.nn.gelu(xf @ W1[e] + b1[e], approximate=False)
            out = out + w_dense[:, e:e + 1] * (h @ W2[e] + b2[e])
        return out.reshape(B, L, D)

    def _L3_gnn_ref(node_feats, adj_matrix, W, b, a):
        import jax, jax.numpy as jnp
        import numpy as np
        B, N, C_IN, H, C_OUT = (8, 512, 128, 4, 128)
        C = C_OUT // H
        ALPHA = 0.2
        NEG_INF = -9000000000000000.0
        Bb, Nn, _ = node_feats.shape
        Hh, twoC = a.shape
        Cc = twoC // 2
        h = (node_feats @ W.T + b).reshape(Bb, Nn, Hh, Cc)
        a_src, a_dst = (a[:, :Cc], a[:, Cc:])
        l_src = jnp.einsum('bihc,hc->bih', h, a_src)
        l_dst = jnp.einsum('bjhc,hc->bjh', h, a_dst)
        logits = jax.nn.leaky_relu(l_src[:, :, None, :] + l_dst[:, None, :, :], ALPHA)
        logits = jnp.where(adj_matrix[..., None] == 1, logits, NEG_INF)
        probs = jax.nn.softmax(logits, axis=2)
        out = jnp.einsum('bijh,bjhc->bihc', probs, h)
        return out.reshape(Bb, Nn, Hh * Cc)

    def _L3_ffn_ref(x, Wr, br, ln_g, ln_b, W1, b1, W2, b2):
        import jax, jax.numpy as jnp
        import numpy as np
        TOP_K = 2
        LN_EPS = 1e-05
        B, S, D = x.shape
        N = B * S
        xt = x.reshape(N, D)
        logits = xt @ Wr + br
        probs = jax.nn.softmax(logits, axis=-1)
        top_p, top_idx = jax.lax.top_k(probs, TOP_K)
        weights = top_p / top_p.sum(axis=-1, keepdims=True)
        mu = xt.mean(axis=-1, keepdims=True)
        var = ((xt - mu) ** 2).mean(axis=-1, keepdims=True)
        xn = (xt - mu) * jax.lax.rsqrt(var + LN_EPS)
        xe = xn[None, :, :] * ln_g[:, None, :] + ln_b[:, None, :]
        h = jax.nn.gelu(jnp.einsum('end,edh->enh', xe, W1) + b1[:, None, :], approximate=False)
        y = jnp.einsum('enh,ehd->end', h, W2) + b2[:, None, :]
        y_tok = jnp.transpose(y, (1, 0, 2))
        sel = jnp.take_along_axis(y_tok, top_idx[:, :, None], axis=1)
        out = (weights[:, :, None] * sel).sum(axis=1)
        return out.reshape(B, S, D)
    x = x + _L0_gnn_ref(_layernorm(x, axis=-1), adj, nodemask, L0_gnn_W, L0_gnn_a)
    x = x + _L0_ffn_ref(_layernorm(x, axis=-1), L0_ffn_W_in, L0_ffn_conv_w, L0_ffn_conv_b, L0_ffn_dt_bias, L0_ffn_A_log, L0_ffn_D, L0_ffn_norm_w, L0_ffn_W_out, L0_ffn_W_lin, L0_ffn_b_lin)
    x = x + _L1_gnn_ref(_layernorm(x, axis=-1), adj, L1_gnn_W, L1_gnn_a)
    x = x + _L1_ffn_ref(_layernorm(x, axis=-1), L1_ffn_router_w, L1_ffn_w1, L1_ffn_b1, L1_ffn_w2, L1_ffn_b2)
    x = x + _L2_gnn_ref(_layernorm(x, axis=-1), adj, L2_gnn_W, L2_gnn_a)
    x = x + _L2_ffn_ref(_layernorm(x, axis=-1), L2_ffn_Wg, L2_ffn_bg, L2_ffn_W1, L2_ffn_b1, L2_ffn_W2, L2_ffn_b2)
    x = x + _L3_gnn_ref(_layernorm(x, axis=-1), adj, L3_gnn_W, L3_gnn_b, L3_gnn_a)
    x = x + _L3_ffn_ref(_layernorm(x, axis=-1), L3_ffn_Wr, L3_ffn_br, L3_ffn_ln_g, L3_ffn_ln_b, L3_ffn_W1, L3_ffn_b1, L3_ffn_W2, L3_ffn_b2)
    return x

_drawn_inputs = setup_inputs


def setup_inputs(seed=0):
    import zlib

    import numpy as np

    out = dict(_drawn_inputs(seed))
    spreads = {'L0_ffn_D': (1.0, 0.2),
     'L0_ffn_norm_w': (1.0, 0.2),
     'L0_ffn_b_lin': (0.0, 0.1),
     'L1_ffn_b1': (0.0, 0.319),
     'L1_ffn_b2': (0.0, 0.1),
     'L2_ffn_bg': (0.0, 0.363),
     'L2_ffn_b1': (0.0, 0.8),
     'L2_ffn_b2': (0.0, 0.31),
     'L3_gnn_b': (0.0, 0.1),
     'L3_ffn_br': (0.0, 0.1),
     'L3_ffn_ln_g': (1.0, 0.541),
     'L3_ffn_ln_b': (0.0, 0.555),
     'L3_ffn_b1': (0.0, 0.554),
     'L3_ffn_b2': (0.0, 0.403)}
    factors = {'L0_ffn_A_log': 29.376, 'L2_ffn_W1': 3.831, 'L2_ffn_W2': 3.578}
    for name, (base, spread) in spreads.items():
        noise = np.random.default_rng([zlib.crc32(name.encode()), seed]).standard_normal(out[name].shape)
        drawn = base * np.exp(spread * noise) if base else spread * noise
        out[name] = jnp.asarray(drawn.astype(out[name].dtype))
    for name, factor in factors.items():
        out[name] = (out[name] * factor).astype(out[name].dtype)
    return out
```

```python
import numpy as np
import concourse.bass as bass
from concourse import mybir
from contextlib import ExitStack

F32 = mybir.dt.float32
F32R = mybir.dt.float32r
BF16 = mybir.dt.bfloat16
I32 = mybir.dt.int32
U32 = mybir.dt.uint32
ALU = mybir.AluOpType
ACT = mybir.ActivationFunctionType
AX = mybir.AxisListType

B, N, D = 16, 512, 128
P = 128
R = N // P
PAIRS = B // 2
E = 8
LN_EPS = 1e-5
SLOPE = 0.2
MASKED = -float(2 ** 53)


def pairs(eng, body):
    body(0)
    with eng.Fori(1, PAIRS - 1) as pair:
        body(pair)
    body(PAIRS - 1)


def wait(eng, sem, value):
    if isinstance(value, int) and value <= 0:
        return
    eng.wait_ge(sem, value)


def layer_semaphores(nc, ctx, name):
    made = []

    def clear():
        nc.clear_and_free_semaphores(made)
        nc.all_engine_barrier()

    def sem(n):
        made.append(nc.alloc_semaphore(name=f"{name}_{n}"))
        return made[-1]
    ctx.callback(clear)
    return sem


def alone(eng, passed):
    eng.sem_inc(passed, 1)


class Chain:

    def __init__(self, eng, sem, per_pair):
        self.eng, self.sem, self.per_pair = eng, sem, per_pair
        self.base, self.count, self.before = 0, 0, 0

    def pair(self, pair):
        self.base, self.count = pair * self.per_pair + self.before, 0

    def end_pair(self):
        assert self.count == self.per_pair, f"chain {self.count}"

    def link(self, ins):
        self.count += 1
        ins.then_inc(self.sem, 1)
        self.eng.wait_ge(self.sem, self.base + self.count)

    def end_prologue(self):
        self.before, self.count = self.count, 0


def gnn_layer(nc, env, name, w, wt, a_cols, heads, elu=False, node_mask=None, bias=None, load=None):
    X, ident, mask_dram = env["X"], env["ident"], env["mask_dram"]
    C = D // heads
    ctx = ExitStack()
    with ctx:
        def sb(n, shape, dt=F32):
            return ctx.enter_context(nc.sbuf_tensor(f"{name}_{n}", shape, dt))

        def pb(n):
            return ctx.enter_context(nc.psum_tensor(f"{name}_{n}", [P, 512], F32))

        sem = layer_semaphores(nc, ctx, name)

        w_sb, wt_sb, a_sb = sb("w", [P, D]), sb("wt", [P, D]), sb("a", [P, 2 * heads])
        wa = sb("wa", [P, 2 * heads])
        wt_bc = sb("wt_bc", [P, heads, P])
        stats, aggr = sb("stats", [P, 2, R, 6]), sb("aggr", [P, 2, R, 2])
        rstd = sb("rstd", [P, 2, R])
        xn = sb("xn", [P, 2, R, P])
        xT = sb("xT", [P, 2, N])
        wh = sb("wh", [P, 2, R, D])
        s_col = sb("s_col", [P, 2, R, heads])
        tm = sb("tm", [P, 2, R, N])
        tmax = sb("tmax", [P, 2, R])
        z_max, top = sb("z_max", [P, R]), sb("top", [P, R])
        c1, c2 = sb("c1", [P, 2, R]), sb("c2", [P, 2, R])
        e1, e2 = sb("e1", [P, 2, N]), sb("e2", [P, 2, N])
        prob = sb("prob", [P, 2, N])
        probT = sb("probT", [P, 2, R, P])
        rowsum = sb("rowsum", [P, 2, R, heads])
        rinv = sb("rinv", [P, R, heads])
        att = sb("att", [P, 2, N])
        neg, eneg = sb("neg", [P, N]), sb("eneg", [P, N])
        if bias is not None:
            bias_col = sb("bias_col", [P, 1])
            bias_lhs = sb("bias_lhs", [P, P])
            bias_row = sb("bias_row", [P, R, D])
            st_const = sb("st_const", [P, 2 * heads])
            s_const = sb("s_const", [P, heads])
        mask = sb("mask", [P, 2, R * N], BF16)
        if load:
            adj_in = sb("adj_in", [P, 2, R, N], I32)
            nm_sb = sb("nm", [P, B * R])

        ps_xT, ps_wh, ps_s, ps_out = pb("ps_xT"), pb("ps_wh"), pb("ps_s"), pb("ps_out")
        ps_t = [pb(f"ps_t{i}") for i in range(2)]
        ps_pT = [pb(f"ps_pT{i}") for i in range(2)]

        w_loaded, wa_done, wa_copied, setup_done = sem("w_loaded"), sem("wa_done"), sem("wa_copied"), sem("setup_done")
        stats_ready, rstd_ready, xn_ready = sem("stats_ready"), sem("rstd_ready"), sem("xn_ready")
        xT_ready, xT_copied = sem("xT_ready"), sem("xT_copied")
        wh_ready, wh_copied = sem("wh_ready"), sem("wh_copied")
        t_ready, bias_ready, exps_ready = sem("t_ready"), sem("bias_ready"), sem("exps_ready")
        prob_ready, pT_ready, pT_copied = sem("prob_ready"), sem("pT_ready"), sem("pT_copied")
        out_done, out_used, neg_ready, eneg_ready = sem("out_done"), sem("out_used"), sem("neg_ready"), sem("eneg_ready")
        att_ready, x_done = sem("att_ready"), sem("x_done")
        dve_chain, pool_chain = sem("dve_chain"), sem("pool_chain")
        if load:
            x_loaded = [sem("x_loaded0"), sem("x_loaded1")]
            adj_loaded = [sem("adj_loaded0"), sem("adj_loaded1")]
            mask_done = sem("mask_done")
            mask_stored = [sem("mask_stored0"), sem("mask_stored1")]
        else:
            mask_loaded = [sem("mask_loaded0"), sem("mask_loaded1")]
            half_free = sem("half_free")

        block = ctx.enter_context(nc.Block())

        @block.sync
        def _(sp):
            if load:
                x_in, adj, nm = load
                x_v = x_in.rearrange("b (r p) d -> p (b r) d", p=P)
                adj_v = adj.rearrange("b (r p) j -> p (b r) j", p=P)
                sp.dma_start(X[:, 0:2 * N].rearrange("p (t d) -> p t d", d=D), x_v[:, 0:2 * R, :]).then_inc(x_loaded[0], 16)
            sp.dma_start(w_sb[:, :], w).then_inc(w_loaded, 16)
            sp.dma_start(wt_sb[:, :], wt).then_inc(w_loaded, 16)
            sp.dma_start(a_sb[:, :], a_cols).then_inc(w_loaded, 16)
            if bias is not None:
                sp.dma_start(bias_col[:, :], bias.rearrange("(p o) -> p o", o=1)).then_inc(w_loaded, 16)
                for r in range(R):
                    sp.dma_start(bias_row[:, r, :], bias.partition_broadcast(P)).then_inc(w_loaded, 16)
            if load:
                sp.dma_start(nm_sb[:, :], nm).then_inc(w_loaded, 16)

                def load_adj(pair, half):
                    wait(sp, mask_done, 2 * pair + half - 1)
                    sp.dma_start(adj_in[:, half, :, :], adj_v[:, bass.ds((2 * pair + half) * R, R), :])\
                      .then_inc(adj_loaded[half], 16)

                load_adj(0, 0)
                load_adj(0, 1)
                sp.dma_start(X[:, 2 * N:B * N].rearrange("p (t d) -> p t d", d=D), x_v[:, 2 * R:, :]).then_inc(x_loaded[1], 16)

                def store_mask(pair, half):
                    b = 2 * pair + half
                    sp.wait_ge(mask_done, b + 1)
                    sp.dma_start(mask_dram[bass.ds(b, 1)].rearrange("b p n -> p (b n)"), mask[:, half, :])\
                      .then_inc(mask_stored[half], 16)

                with sp.Fori(1, PAIRS) as pair:
                    for half in range(2):
                        store_mask(pair - 1, half)
                        load_adj(pair, half)
                for half in range(2):
                    store_mask(PAIRS - 1, half)
                for half in range(2):
                    sp.wait_ge(mask_stored[half], 16 * PAIRS)
            else:
                with sp.Fori(0, PAIRS) as pair:
                    for half in range(2):
                        b = 2 * pair + half
                        sp.wait_ge(half_free, b + 1)
                        sp.dma_start(mask[:, half, :], mask_dram[bass.ds(b, 1)].rearrange("b p n -> p (b n)"))\
                          .then_inc(mask_loaded[half], 16)

        n_loads = 16 * (3 + (1 + R if bias is not None else 0) + (1 if load else 0))

        @block.gpsimd
        def _(pool):
            def rstd_of(pair, half):
                b = 2 * pair + half
                pool.wait_ge(stats_ready, b + 1)
                chain.link(nc.gpsimd.tensor_tensor(rstd[:, half, :], aggr[:, half, :, 1], env["eps"][:, :], ALU.add))
                nc.gpsimd.tensor_tensor(rstd[:, half, :], rstd[:, half, :], env["minus_half"][:, :], ALU.pow)\
                  .then_inc(rstd_ready, 1)

            def residual(pair, half):
                b = 2 * pair + half
                pool.wait_ge(att_ready, b + 1)
                if bias is not None:
                    chain.link(nc.gpsimd.tensor_tensor(att[:, half, :], att[:, half, :],
                                                       bias_row[:, :, :].rearrange("p r d -> p (r d)"), ALU.add))
                alone(pool, env["pool_passed"])
                nc.gpsimd.tensor_tensor(X[:, bass.ts(b, N)], X[:, bass.ts(b, N)], att[:, half, :], ALU.add)\
                  .then_inc(x_done, 1)

            chain = Chain(pool, pool_chain, 0)
            if bias is not None:
                pool.wait_ge(w_loaded, n_loads)
            rstd_of(0, 0)
            rstd_of(0, 1)
            chain.end_prologue()
            chain.per_pair = 4 if bias is not None else 2

            def body(pair):
                last = isinstance(pair, int) and pair == PAIRS - 1
                chain.pair(pair)
                for half in range(2):
                    if not last:
                        rstd_of(pair + 1, half)
                    if not elu:
                        residual(pair, half)
                if not last:
                    chain.end_pair()
            pairs(pool, body)

        @block.scalar
        def _(act):
            def copy_xT(pair, half):
                act.wait_ge(xT_ready, 2 * pair + half + 1)
                nc.scalar.copy(xT[:, half, :], ps_xT[:, :]).then_inc(xT_copied, 1)

            def copy_wh(pair, half):
                b = 2 * pair + half
                act.wait_ge(wh_ready, b + 1)
                wait(act, bias_ready, heads * (b - 1))
                nc.scalar.copy(wh[:, half, :, :].rearrange("p r d -> p (r d)"), ps_wh[:, :])
                nc.scalar.copy(s_col[:, half, :, :].rearrange("p r h -> p (r h)"), ps_s[:, 0:R * heads])\
                  .then_inc(wh_copied, 1)

            def exps(unit, u2, r):
                if r == 0:
                    act.wait_ge(bias_ready, unit + 1)
                wait(act, prob_ready, unit * R + r - 1)
                nc.scalar.activation(e1[:, r % 2, :], tm[:, u2, r, :], ACT.Exp, bias=c1[:, u2, r:r + 1])
                nc.scalar.activation(e2[:, r % 2, :], tm[:, u2, r, :], ACT.Exp, bias=c2[:, u2, r:r + 1], scale=SLOPE)\
                  .then_inc(exps_ready, 1)

            def copy_pT(unit, r):
                n = unit * R + r
                act.wait_ge(pT_ready, n + 1)
                wait(act, out_done, n - 1)
                nc.scalar.copy(probT[:, r % 2, :, :].rearrange("p c i -> p (c i)"), ps_pT[r % 2][:, :])\
                  .then_inc(pT_copied, 1)

            def elu_exp(b):
                act.wait_ge(neg_ready, b + 1)
                nc.scalar.activation(eneg[:, :], neg[:, :], ACT.Exp).then_inc(eneg_ready, 1)

            act.wait_ge(wa_done, 1)
            nc.scalar.copy(wa[:, :], ps_s[:, 0:2 * heads]).then_inc(wa_copied, 1)
            copy_xT(0, 0)
            copy_wh(0, 0)

            def body(pair):
                first = isinstance(pair, int) and pair == 0
                last = isinstance(pair, int) and pair == PAIRS - 1
                for half in range(2):
                    b = 2 * pair + half
                    following = (pair, 1) if half == 0 else (pair + 1, 0)
                    for h in range(heads):
                        unit = b * heads + h
                        u2 = (half * heads + h) % 2
                        ahead = h == heads - 1 and not (last and half == 1)
                        if ahead:
                            copy_xT(*following)
                        exps(unit, u2, 0)
                        exps(unit, u2, 1)
                        if ahead:
                            copy_wh(*following)
                        if elu and h == 0 and not (first and half == 0):
                            elu_exp(b - 1)
                        copy_pT(unit, 0)
                        exps(unit, u2, 2)
                        copy_pT(unit, 1)
                        exps(unit, u2, 3)
                        copy_pT(unit, 2)
                        copy_pT(unit, 3)
            pairs(act, body)
            if elu:
                elu_exp(B - 1)

        @block.vector
        def _(dve):
            chain = Chain(dve, dve_chain, 0)

            def graph_stats(pair, half):
                b = 2 * pair + half
                wait(dve, xn_ready, b - 1)
                if load:
                    dve.wait_ge(x_loaded[0], 16)
                    if not (isinstance(pair, int) and pair == 0):
                        dve.wait_ge(x_loaded[1], 16)
                for r in range(R):
                    ins = nc.vector.bn_stats(stats[:, half, r, :], X[:, bass.ds(b * N + r * D, D)])
                chain.link(ins)
                alone(dve, env["dve_passed"])
                for r in range(R):
                    ins = nc.vector.bn_aggr(aggr[:, half, r, :], stats[:, half, r, :])
                ins.then_inc(stats_ready, 1)

            def make_mask(pair, half):
                dve.wait_ge(adj_loaded[half], 16 * (pair + 1))
                wait(dve, mask_stored[half], 16 * pair)
                nc.vector.tensor_scalar(mask[:, half, :], adj_in[:, half, :, :].rearrange("p r j -> p (r j)"),
                                        0.0, MASKED, ALU.is_le, ALU.mult).then_inc(mask_done, 1)

            def normalize(pair, half):
                b = 2 * pair + half
                dve.wait_ge(rstd_ready, b + 1)
                wait(dve, xT_ready, b - 1)
                for r in range(R):
                    ins = nc.vector.tensor_scalar(xn[:, half, r, :], X[:, bass.ds(b * N + r * D, D)],
                                                  aggr[:, half, r, 0:1], rstd[:, half, r:r + 1], ALU.subtract, ALU.mult)
                ins.then_inc(xn_ready, 1)


            def scores(pair, half, h, r):
                b = 2 * pair + half
                unit = b * heads + h
                u2 = (half * heads + h) % 2
                if r == 0:
                    dve.wait_ge(t_ready, unit + 1)
                if h == 0 and r == 0:
                    if load:
                        dve.wait_ge(mask_done, b + 1)
                    else:
                        dve.wait_ge(mask_loaded[half], 16 * (pair + 1))
                if r == 0:
                    alone(dve, env["dve_passed"])
                ins = nc.vector.tensor_tensor_reduce(out=tm[:, u2, r, :], in0=ps_t[u2][:, :],
                                                     in1=mask[:, half, r * N:(r + 1) * N],
                                                     scale=1.0, scalar=-3.0e38, op0=ALU.add, op1=ALU.max,
                                                     accum_out=tmax[:, u2, r:r + 1])
                return ins

            def shifts(pair, half, h, ins):
                b = 2 * pair + half
                u2 = (half * heads + h) % 2
                chain.link(ins)
                dve.wait_ge(wh_copied, b + 1)
                s = s_col[:, half, :, h]
                if bias is not None:
                    chain.link(nc.vector.tensor_scalar(s, s, s_const[:, h:h + 1], None, ALU.add))
                chain.link(nc.vector.tensor_tensor(z_max[:, :], tmax[:, u2, :], s, ALU.add))
                chain.link(nc.vector.scalar_tensor_tensor(top[:, :], z_max[:, :], SLOPE, z_max[:, :], ALU.mult, ALU.max))
                ins = nc.vector.tensor_tensor(c1[:, u2, :], s, top[:, :], ALU.subtract)
                if not load and h == heads - 1:
                    ins.then_inc(half_free, 1)
                nc.vector.scalar_tensor_tensor(c2[:, u2, :], s, SLOPE, top[:, :], ALU.mult, ALU.subtract)\
                  .then_inc(bias_ready, 1)

            def probs(pair, half, h, r):
                n = ((2 * pair + half) * heads + h) * R + r
                dve.wait_ge(exps_ready, n + 1)
                wait(dve, pT_ready, n - 1)
                nc.vector.scalar_tensor_tensor(prob[:, r % 2, :], e1[:, r % 2, :], 1.0, e2[:, r % 2, :], ALU.mult, ALU.max,
                                               accum_out=rowsum[:, half, r, h:h + 1]).then_inc(prob_ready, 1)

            def finish(pair, half):
                b = 2 * pair + half
                dve.wait_ge(prob_ready, (b + 1) * heads * R)
                chain.link(nc.vector.reciprocal(rinv[:, :, :], rowsum[:, half, :, :]))
                if node_mask is not None:
                    chain.link(nc.vector.tensor_tensor(rinv[:, :, 0], rinv[:, :, 0], nm_sb[:, bass.ds(b * R, R)], ALU.mult))
                dve.wait_ge(out_done, (b + 1) * heads * R)
                if not elu:
                    wait(dve, x_done, b - 1)
                ins = nc.vector.tensor_tensor(att[:, half, :].rearrange("p (r h c) -> p r h c", r=R, h=heads),
                                              ps_out[:, :].rearrange("p (r h c) -> p r h c", r=R, h=heads),
                                              rinv[:, :, :].unsqueeze(3).to_broadcast([P, R, heads, C]), ALU.mult)
                if elu:
                    ins.then_inc(out_used, 1)
                    dve.wait_ge(out_used, b + 1)
                    wait(dve, eneg_ready, b)
                    nc.vector.tensor_scalar(neg[:, :], att[:, half, :], 0.0, None, ALU.min).then_inc(neg_ready, 1)
                else:
                    ins.then_inc(att_ready, 1)

            def elu_finish(b, half):
                dve.wait_ge(eneg_ready, b + 1)
                chain.link(nc.vector.scalar_tensor_tensor(att[:, half, :], att[:, half, :], 0.0, eneg[:, :], ALU.max, ALU.add))
                nc.vector.scalar_tensor_tensor(X[:, bass.ts(b, N)], att[:, half, :], -1.0, X[:, bass.ts(b, N)],
                                               ALU.add, ALU.add).then_inc(x_done, 1)

            if not load:
                dve.sem_inc(half_free, 2)
            graph_stats(0, 0)
            graph_stats(0, 1)
            normalize(0, 0)
            if load:
                make_mask(0, 0)
            normalize(0, 1)
            if load:
                make_mask(0, 1)
            dve.wait_ge(w_loaded, n_loads)
            dve.wait_ge(wa_copied, 1)
            if bias is not None:
                nc.vector.tensor_copy(bias_lhs[:, :], bias_col[:, :].to_broadcast([P, P]))
            nc.vector.tensor_copy(wt_bc[:, :, :], wa[:, heads:2 * heads].unsqueeze(2).to_broadcast([P, heads, P]))\
              .then_inc(setup_done, 1)
            if bias is not None:
                dve.wait_ge(wa_done, 2)
                nc.vector.tensor_copy(st_const[:, :], ps_s[:, 64:64 + 2 * heads]).then_inc(setup_done, 1)
                dve.wait_ge(setup_done, 2)
                chain.link(nc.vector.tensor_tensor(s_const[:, :], st_const[:, 0:heads], st_const[:, heads:], ALU.add))
            for r in range(R):
                ins = scores(0, 0, 0, r)
            shifts(0, 0, 0, ins)
            chain.end_prologue()
            n_shift = 4 if bias is not None else 3
            chain.per_pair = 2 + 2 * heads * n_shift + 2 * (2 if node_mask is not None else 1) + (2 if elu else 0)

            def body(pair):
                first = isinstance(pair, int) and pair == 0
                last = isinstance(pair, int) and pair == PAIRS - 1
                chain.pair(pair)
                for half in range(2):
                    b = 2 * pair + half
                    for h in range(heads):
                        if h < heads - 1:
                            nxt = (pair, half, h + 1)
                        else:
                            nxt = (pair, 1, 0) if half == 0 else (pair + 1, 0, 0)
                        ahead = not (last and half == 1 and h == heads - 1)
                        probs(pair, half, h, 0)
                        if h == 0 and not last:
                            graph_stats(pair + 1, half)
                        probs(pair, half, h, 1)
                        if elu and h == 0 and not (first and half == 0):
                            elu_finish(b - 1, 1 - half)
                        if ahead:
                            scores(*nxt, 0)
                        probs(pair, half, h, 2)
                        if ahead:
                            scores(*nxt, 1)
                        probs(pair, half, h, 3)
                        if ahead:
                            scores(*nxt, 2)
                            shifts(*nxt, scores(*nxt, 3))
                    finish(pair, half)
                    if not last:
                        normalize(pair + 1, half)
                        if load:
                            make_mask(pair + 1, half)
                if not (first or last):
                    chain.end_pair()
                elif first:
                    chain.before -= chain.per_pair - chain.count
            pairs(dve, body)
            if elu:
                elu_finish(B - 1, 1)
                dve.wait_ge(x_done, B)
            else:
                dve.wait_ge(x_done, B)

        @block.tensor
        def _(pe):
            def front(pair, half):
                b = 2 * pair + half
                pe.wait_ge(xn_ready, b + 1)
                for r in range(R):
                    ins = nc.tensor.transpose(ps_xT[:, r * P:(r + 1) * P], xn[:, half, r, :], ident[:, :])
                ins.then_inc(xT_ready, 1)
                pe.wait_ge(xT_copied, b + 1)
                wait(pe, wh_copied, b)
                for r in range(R):
                    nc.tensor.matmul(ps_wh[:, r * P:(r + 1) * P], xT[:, half, r * P:(r + 1) * P], w_sb[:, :],
                                     start=True, stop=True)
                for r in range(R):
                    ins = nc.tensor.matmul(ps_s[:, r * heads:(r + 1) * heads], xT[:, half, r * P:(r + 1) * P],
                                           wa[:, 0:heads], start=True, stop=True)
                ins.then_inc(wh_ready, 1)

            def t_rows(pair, half, h):
                unit = (2 * pair + half) * heads + h
                wait(pe, bias_ready, unit - 1)
                nc.tensor.matmul(ps_t[(half * heads + h) % 2][:, :], wt_bc[:, h, :], xT[:, half, :],
                                 start=True, stop=True).then_inc(t_ready, 1)

            def transpose_probs(unit, r):
                n = unit * R + r
                pe.wait_ge(prob_ready, n + 1)
                wait(pe, pT_copied, n - 1)
                for c in range(R):
                    ins = nc.tensor.transpose(ps_pT[r % 2][:, c * P:(c + 1) * P], prob[:, r % 2, c * P:(c + 1) * P],
                                              ident[:, :])
                ins.then_inc(pT_ready, 1)

            def attend(pair, half, h, r):
                b = 2 * pair + half
                n = (b * heads + h) * R + r
                if h == 0 and r == 0:
                    wait(pe, out_used if elu else att_ready, b)
                pe.wait_ge(pT_copied, n + 1)
                for c in range(R):
                    ins = nc.tensor.matmul(ps_out[:, r * D + h * C:r * D + (h + 1) * C], probT[:, r % 2, c, :],
                                           wh[:, half, c, h * C:(h + 1) * C], start=c == 0, stop=c == R - 1)
                ins.then_inc(out_done, 1)

            pe.wait_ge(w_loaded, n_loads)
            nc.tensor.matmul(ps_s[:, 0:2 * heads], wt_sb[:, :], a_sb[:, :], start=True, stop=True).then_inc(wa_done, 1)
            pe.wait_ge(setup_done, 1)
            if bias is not None:
                nc.tensor.matmul(ps_s[:, 64:64 + 2 * heads], bias_lhs[:, :], a_sb[:, :], start=True, stop=True)\
                  .then_inc(wa_done, 1)
                pe.wait_ge(setup_done, 2)
            front(0, 0)
            t_rows(0, 0, 0)

            def body(pair):
                last = isinstance(pair, int) and pair == PAIRS - 1
                for half in range(2):
                    for h in range(heads):
                        unit = (2 * pair + half) * heads + h
                        if h < heads - 1:
                            t_rows(pair, half, h + 1)
                        elif not (last and half == 1):
                            following = (pair, 1) if half == 0 else (pair + 1, 0)
                            front(*following)
                            t_rows(*following, 0)
                        for r in range(R):
                            transpose_probs(unit, r)
                            if r >= 1:
                                attend(pair, half, h, r - 1)
                        attend(pair, half, h, R - 1)
            pairs(pe, body)


def moe_layer(nc, env, name, w1, b1, w2, b2, router, router_bias, hidden, keep_tokens=False, own_ln=None, split_h=True):
    X, ident = env["X"], env["ident"]
    HC = hidden // P
    NG = E * HC
    LAG = 2
    LATE = LAG + 1
    unit = NG // 8
    S_TRANSPOSE, S_LOGITS, S_TOP, S_TANH, S_COMBINE_W, S_COMB_T, S_COMB_SPLIT = [unit * k for k in range(7)]
    S_OUT = LATE + 2
    S_UPDATE = S_OUT + 1
    S_STATS, S_NORM, S_NORM2 = unit + 1, 5 * unit, 7 * unit
    Hs = F32R if split_h else F32
    HR = 2 if split_h else 4
    ctx = ExitStack()
    with ctx:
        def sb(n, shape, dt=F32):
            return ctx.enter_context(nc.sbuf_tensor(f"{name}_{n}", shape, dt))

        def pb(n):
            return ctx.enter_context(nc.psum_tensor(f"{name}_{n}", [P, 512], F32))

        sem = layer_semaphores(nc, ctx, name)

        w1h, w1l = sb("w1h", [P, E, hidden], F32R), sb("w1l", [P, E, hidden], F32R)
        w2h = sb("w2h", [P, E, HC, D], Hs)
        w2l = sb("w2l", [P, E, HC, D], F32R) if split_h else None
        b1_sb, b2_sb, wr_sb = sb("b1", [P, NG]), sb("b2", [P, E]), sb("wr", [P, E])
        iota = sb("iota", [P, R, E])
        sel = sb("sel", [64, E], F32R)
        comb_T = sb("comb_T", [64, 2, N], F32R)
        if router_bias is not None:
            rb_sb = sb("rb", [P, R, E])

        with ExitStack() as setup:
            def ssb(n, shape, dt=F32):
                return setup.enter_context(nc.sbuf_tensor(f"{name}_{n}", shape, dt))

            stage = ssb("stage", [P, 2, hidden])
            zero64 = ssb("zero64", [64, 2 * N])
            if own_ln:
                g_sb, lnb_sb = ssb("g", [P, E]), ssb("lnb", [P, E])
                ps_b = setup.enter_context(nc.psum_tensor(f"{name}_ps_b", [P, 512], F32))
            small_loaded, staged = sem("small_loaded"), [sem("staged0"), sem("staged1")]
            split_done, scaled, bias_mm, zeroed, w2_high = [sem(n) for n in ("w_split", "scaled", "bias_mm", "zeroed", "w2_high")]
            with nc.Block() as block:
                small = [(b1_sb[:, :], b1), (b2_sb[:, :], b2), (wr_sb[:, :], router)]
                if router_bias is not None:
                    small += [(rb_sb[:, r, :], router_bias.partition_broadcast(P)) for r in range(R)]
                if own_ln:
                    small += [(g_sb[:, :], own_ln[0]), (lnb_sb[:, :], own_ln[1])]

                @block.sync
                def _(sp):
                    for dst, src in small:
                        sp.dma_start(dst, src).then_inc(small_loaded, 16)
                    for e in range(E):
                        wait(sp, split_done, 2 * e - 1)
                        sp.dma_start(stage[:, 0, :], w1[e]).then_inc(staged[0], 16)
                        wait(sp, split_done, 2 * e)
                        sp.dma_start(stage[:, 1, :].rearrange("p (c d) -> p c d", d=D),
                                     w2[e].rearrange("(c p) d -> p c d", p=P)).then_inc(staged[1], 16)

                @block.gpsimd
                def _(pool):
                    nc.gpsimd.iota(iota[:, :, :], pattern=[[0, R], [1, E]], base=0, channel_multiplier=0,
                                   allow_small_or_imprecise_dtypes=True)
                    nc.gpsimd.memset(zero64[:, :], 0.0).then_inc(zeroed, 1)

                @block.vector
                def _(dve):
                    dve.wait_ge(small_loaded, 16 * len(small))
                    dve.wait_ge(zeroed, 1)
                    nc.vector.tensor_copy(comb_T[:, :, :].rearrange("k h n -> k (h n)"), zero64[:, :])
                    nc.vector.tensor_tensor(sel[:, :], ident[0:64, 0:E], ident[0:64, 32:32 + E], ALU.add)
                    for e in range(E):
                        dve.wait_ge(staged[0], 16 * (e + 1))
                        if own_ln:
                            dve.wait_ge(bias_mm, e + 1)
                            nc.vector.tensor_scalar(stage[:, 0, :], stage[:, 0, :], g_sb[:, e:e + 1], None, ALU.mult)\
                              .then_inc(scaled, 1)
                            dve.wait_ge(scaled, 2 * e + 1)
                        nc.vector.tensor_copy(w1h[:, e, :], stage[:, 0, :]).then_inc(scaled, 1)
                        dve.wait_ge(scaled, (2 * e + 2) if own_ln else (e + 1))
                        nc.vector.tensor_tensor(w1l[:, e, :], stage[:, 0, :], w1h[:, e, :].bitcast(F32), ALU.subtract)\
                          .then_inc(split_done, 1)
                        dve.wait_ge(staged[1], 16 * (e + 1))
                        w2v = w2h[:, e, :, :].rearrange("p c d -> p (c d)")
                        if split_h:
                            nc.vector.tensor_copy(w2v, stage[:, 1, :]).then_inc(w2_high, 1)
                            dve.wait_ge(w2_high, e + 1)
                            nc.vector.tensor_tensor(w2l[:, e, :, :].rearrange("p c d -> p (c d)"), stage[:, 1, :],
                                                    w2v.bitcast(F32), ALU.subtract).then_inc(split_done, 1)
                        else:
                            nc.vector.tensor_copy(w2v, stage[:, 1, :]).then_inc(split_done, 1)
                    if own_ln:
                        nc.vector.tensor_tensor(b1_sb[:, :], b1_sb[:, :], ps_b[:, 0:NG], ALU.add)

                if own_ln:
                    @block.tensor
                    def _(pe):
                        pe.wait_ge(small_loaded, 16 * len(small))
                        for e in range(E):
                            pe.wait_ge(staged[0], 16 * (e + 1))
                            for c in range(HC):
                                ins = nc.tensor.matmul(ps_b[:, e * HC + c:e * HC + c + 1],
                                                       stage[:, 0, c * P:(c + 1) * P], lnb_sb[:, e:e + 1],
                                                       start=True, stop=True)
                            ins.then_inc(bias_mm, 1)

        stats, aggr, rstd = sb("stats", [P, 2, R, 6]), sb("aggr", [P, 2, R, 2]), sb("rstd", [P, 2, R])
        xn = sb("xn", [P, 2, R, P])
        xT = sb("xT", [P, N])
        if own_ln:
            stats2, aggr2, rstd2 = sb("stats2", [P, R, 6]), sb("aggr2", [P, R, 2]), sb("rstd2", [P, R])
            xn2 = sb("xn2", [P, 2, R, P])
            xT2 = sb("xT2", [P, N])
        xe = xT2 if own_ln else xT
        xh, xl = sb("xh", [P, 2, N], F32R), sb("xl", [P, 2, N], F32R)
        logit, best, best_at = sb("logit", [P, R, E]), sb("best", [P, R, E]), sb("best_at", [P, R, E], U32)
        at_f = sb("at_f", [P, R, 2])
        gap, tanh_gap = sb("gap", [P, R]), sb("tanh_gap", [P, R])
        weight = sb("weight", [P, 2, R])
        hot = sb("hot", [P, 2, R, E])
        comb = sb("comb", [P, R, E])
        h = sb("h", [P, HR, N])
        hh = sb("hh", [P, HR, N], F32R) if split_h else None
        hl = sb("hl", [P, HR, N], F32R) if split_h else None
        w_rows = sb("w_rows", [P, 2, N])
        scaled_y = sb("scaled_y", [P, 2, N])
        acc = sb("acc", [P, 2, N])

        ps_h = [pb(f"ps_h{i}") for i in range(2)]
        ps_y = [pb(f"ps_y{i}") for i in range(2)]
        ps_w, ps_xT, ps_small, ps_out = pb("ps_w"), pb("ps_xT"), pb("ps_small"), pb("ps_out")

        stats_ready, rstd_ready, xn_ready = sem("stats_ready"), sem("rstd_ready"), sem("xn_ready")
        stats2_ready, rstd2_ready, xn2_ready = sem("stats2_ready"), sem("rstd2_ready"), sem("xn2_ready")
        xT_ready, xT_copied = sem("xT_ready"), sem("xT_copied")
        x_split, logits_ready, gap_ready, tanh_ready = sem("x_split"), sem("logits_ready"), sem("gap_ready"), sem("tanh_ready")
        comb_ready, combT_ready, combT_split = sem("comb_ready"), sem("combT_ready"), sem("combT_split")
        h_ready, gelu_done, h_split, y_chunk = sem("h_ready"), sem("gelu_done"), sem("h_split"), sem("y_chunk")
        w_ready, w_copied, y_scaled, added = sem("w_ready"), sem("w_copied"), sem("y_scaled"), sem("added")
        out_ready, x_done = sem("out_ready"), sem("x_done")
        dve_chain, pool_chain = sem("dve_chain"), sem("pool_chain")

        def steps(pair, half):
            first = isinstance(pair, int) and pair == 0 and half == 0
            last = isinstance(pair, int) and pair == PAIRS - 1 and half == 1
            nxt = (pair, 1) if half == 0 else (pair + 1, 0)
            prev = (pair, 0) if half == 1 else (pair - 1, 1)
            return first, last, nxt, prev

        def in_static(half, g, lag):
            return (half * NG + g - lag) % (2 * NG)

        block = ctx.enter_context(nc.Block())

        @block.gpsimd
        def _(pool):
            chain = Chain(pool, pool_chain, 0)

            def rstd_of(pair, half):
                b = 2 * pair + half
                pool.wait_ge(stats_ready, b + 1)
                chain.link(nc.gpsimd.tensor_tensor(rstd[:, half, :], aggr[:, half, :, 1], env["eps"][:, :], ALU.add))
                nc.gpsimd.tensor_tensor(rstd[:, half, :], rstd[:, half, :], env["minus_half"][:, :], ALU.pow)\
                  .then_inc(rstd_ready, 1)

            def add_tokens(pair, half):
                if keep_tokens:
                    b = 2 * pair + half
                    pool.wait_ge(xn_ready, b + 1)
                    alone(pool, env["pool_passed"])
                    chain.link(nc.gpsimd.tensor_tensor(X[:, bass.ts(b, N)], X[:, bass.ts(b, N)],
                                                       xn[:, half, :, :].rearrange("p r d -> p (r d)"), ALU.add))

            def rstd2_of(pair, half):
                pool.wait_ge(stats2_ready, 2 * pair + half + 1)
                chain.link(nc.gpsimd.tensor_tensor(rstd2[:, :], aggr2[:, :, 1], env["eps"][:, :], ALU.add))
                nc.gpsimd.tensor_tensor(rstd2[:, :], rstd2[:, :], env["minus_half"][:, :], ALU.pow).then_inc(rstd2_ready, 1)

            def add_expert(pair, half, e):
                n = (2 * pair + half) * E + e
                pool.wait_ge(y_scaled, n + 1)
                if e == 0:
                    wait(pool, out_ready, 2 * pair + half - 1)
                    alone(pool, env["pool_passed"])
                    nc.gpsimd.tensor_copy(acc[:, half, :], scaled_y[:, e % 2, :]).then_inc(added, 1)
                else:
                    pool.wait_ge(added, n)
                    nc.gpsimd.tensor_tensor(acc[:, half, :], acc[:, half, :], scaled_y[:, e % 2, :], ALU.add)\
                      .then_inc(added, 1)

            for half in range(2):
                rstd_of(0, half)
            for half in range(2):
                add_tokens(0, half)
                if own_ln:
                    rstd2_of(0, half)
            chain.end_prologue()
            chain.per_pair = 2 + (2 if own_ln else 0) + (2 if keep_tokens else 0)

            def body(pair):
                last_pair = isinstance(pair, int) and pair == PAIRS - 1
                chain.pair(pair)
                for half in range(2):
                    first, last, nxt, prev = steps(pair, half)
                    for e in range(E):
                        add_expert(pair, half, e)
                        if e == 1 and not last_pair:
                            rstd_of(pair + 1, half)
                        if e == 5 and not last_pair:
                            add_tokens(pair + 1, half)
                            if own_ln:
                                rstd2_of(pair + 1, half)
                if not last_pair:
                    chain.end_pair()
            pairs(pool, body)

        @block.scalar
        def _(act):
            def front(pair, half):
                b = 2 * pair + half
                act.wait_ge(xT_ready, b + 1)
                wait(act, logits_ready, b)
                if not own_ln:
                    wait(act, x_split, b)
                nc.scalar.copy(xT[:, :], ps_xT[:, :]).then_inc(xT_copied, 1)
                if own_ln:
                    act.wait_ge(xT_ready, b + 1)
                    wait(act, x_split, b)
                    nc.scalar.copy(xT2[:, :], ps_out[:, :]).then_inc(xT_copied, 1)

            def gap_tanh(pair, half):
                act.wait_ge(gap_ready, 2 * pair + half + 1)
                nc.scalar.activation(tanh_gap[:, :], gap[:, :], ACT.Tanh, scale=0.5).then_inc(tanh_ready, 1)

            def gelu(pair, half, g):
                n = (2 * pair + half) * NG + g
                act.wait_ge(h_ready, n + 1)
                wait(act, h_split if split_h else y_chunk, n - HR + 1)
                nc.scalar.activation(h[:, g % HR, :], ps_h[g % 2][:, :], ACT.Gelu,
                                     bias=b1_sb[:, g:g + 1]).then_inc(gelu_done, 1)

            def copy_w(n, e):
                act.wait_ge(w_ready, n + 1)
                wait(act, y_scaled, n - 1)
                nc.scalar.copy(w_rows[:, e % 2, :], ps_w[:, :]).then_inc(w_copied, 1)

            front(0, 0)
            gap_tanh(0, 0)

            def body(pair):
                for half in range(2):
                    first, last, nxt, prev = steps(pair, half)
                    for g in range(NG):
                        gelu(pair, half, g)
                        if (g - LAG) % HC == 0 and not (first and g < LAG):
                            copy_w((2 * pair + half) * E + (g - LAG) // HC, (g - LAG) // HC)
                        if not last and g == S_TRANSPOSE:
                            front(*nxt)
                        if not last and g == S_TANH:
                            gap_tanh(*nxt)
            pairs(act, body)
            for g in range(LAG):
                if (g - LAG) % HC == 0:
                    copy_w(B * E + (g - LAG) // HC, (g - LAG) // HC)

        @block.vector
        def _(dve):
            chain = Chain(dve, dve_chain, 0)

            def graph_stats(pair, half):
                b = 2 * pair + half
                wait(dve, xn_ready, b - 1)
                for r in range(R):
                    ins = nc.vector.bn_stats(stats[:, half, r, :], X[:, bass.ds(b * N + r * D, D)])
                chain.link(ins)
                alone(dve, env["dve_passed"])
                for r in range(R):
                    ins = nc.vector.bn_aggr(aggr[:, half, r, :], stats[:, half, r, :])
                ins.then_inc(stats_ready, 1)

            def graph_stats2(pair, half):
                b = 2 * pair + half
                dve.wait_ge(xn_ready, b + 1)
                wait(dve, xn2_ready, b)
                for r in range(R):
                    ins = nc.vector.bn_stats(stats2[:, r, :], xn[:, half, r, :])
                chain.link(ins)
                alone(dve, env["dve_passed"])
                for r in range(R):
                    ins = nc.vector.bn_aggr(aggr2[:, r, :], stats2[:, r, :])
                ins.then_inc(stats2_ready, 1)

            def normalize(pair, half):
                b = 2 * pair + half
                dve.wait_ge(rstd_ready, b + 1)
                wait(dve, xT_ready, b - 1)
                for r in range(R):
                    ins = nc.vector.tensor_scalar(xn[:, half, r, :], X[:, bass.ds(b * N + r * D, D)],
                                                  aggr[:, half, r, 0:1], rstd[:, half, r:r + 1], ALU.subtract, ALU.mult)
                ins.then_inc(xn_ready, 1)

            def normalize2(pair, half):
                b = 2 * pair + half
                dve.wait_ge(rstd2_ready, b + 1)
                for r in range(R):
                    ins = nc.vector.tensor_scalar(xn2[:, half, r, :], xn[:, half, r, :],
                                                  aggr2[:, r, 0:1], rstd2[:, r:r + 1], ALU.subtract, ALU.mult)
                ins.then_inc(xn2_ready, 1)

            def split_x(pair, half):
                b = 2 * pair + half
                dve.wait_ge(xT_copied, (b + 1) * (2 if own_ln else 1))
                wait(dve, h_ready, (b - 1) * NG)
                chain.link(nc.vector.tensor_copy(xh[:, half, :], xe[:, :]))
                nc.vector.tensor_tensor(xl[:, half, :], xe[:, :], xh[:, half, :].bitcast(F32), ALU.subtract)\
                  .then_inc(x_split, 1)

            def top_two(pair, half):
                b = 2 * pair + half
                dve.wait_ge(logits_ready, b + 1)
                lv = logit[:, :, :].rearrange("p r e -> p (r e)")
                if router_bias is not None:
                    ins = nc.vector.tensor_tensor(lv, ps_small[:, 0:R * E], rb_sb[:, :, :].rearrange("p r e -> p (r e)"),
                                                  ALU.add)
                else:
                    ins = nc.vector.tensor_copy(lv, ps_small[:, 0:R * E])
                chain.link(ins)
                alone(dve, env["dve_passed"])
                for r in range(R):
                    ins = nc.vector.max(best[:, r, :], logit[:, r, :])
                chain.link(ins)
                alone(dve, env["dve_passed"])
                for r in range(R):
                    ins = nc.vector.max_index(best_at[:, r, :], best[:, r, :], logit[:, r, :])
                nc.vector.tensor_tensor(gap[:, :], best[:, :, 0], best[:, :, 1], ALU.subtract).then_inc(gap_ready, 1)

            def weights(pair, half):
                b = 2 * pair + half
                dve.wait_ge(gap_ready, b + 1)
                chain.link(nc.vector.tensor_copy(at_f[:, :, :], best_at[:, :, 0:2]))
                dve.wait_ge(tanh_ready, b + 1)
                nc.vector.tensor_scalar(weight[:, 0, :], tanh_gap[:, :], 0.5, 0.5, ALU.mult, ALU.add)
                nc.vector.tensor_scalar(weight[:, 1, :], tanh_gap[:, :], -0.5, 0.5, ALU.mult, ALU.add)
                for k in range(2):
                    ins = nc.vector.tensor_tensor(hot[:, k, :, :], iota[:, :, :],
                                                  at_f[:, :, k:k + 1].to_broadcast([P, R, E]), ALU.is_equal)
                chain.link(ins)
                for k in range(2):
                    ins = nc.vector.tensor_tensor(hot[:, k, :, :], hot[:, k, :, :],
                                                  weight[:, k, :].unsqueeze(2).to_broadcast([P, R, E]), ALU.mult)
                chain.link(ins)
                nc.vector.tensor_tensor(comb[:, :, :], hot[:, 0, :, :], hot[:, 1, :, :], ALU.add).then_inc(comb_ready, 1)

            def split_comb(pair, half):
                b = 2 * pair + half
                dve.wait_ge(combT_ready, b + 1)
                wait(dve, w_ready, (b - 1) * E)
                chain.link(nc.vector.tensor_copy(comb_T[0:E, half, :], ps_small[0:E, :]))
                nc.vector.tensor_tensor(comb_T[32:32 + E, half, :], ps_small[0:E, :], comb_T[0:E, half, :].bitcast(F32),
                                        ALU.subtract).then_inc(combT_split, 1)

            def split_hidden(pair, half, g):
                n = (2 * pair + half) * NG + g
                slot = g % HR
                dve.wait_ge(gelu_done, n + 1)
                wait(dve, y_chunk, n - HR + 1)
                chain.link(nc.vector.tensor_copy(hh[:, slot, :], h[:, g % 2, :]))
                nc.vector.tensor_tensor(hl[:, slot, :], h[:, g % 2, :], hh[:, slot, :].bitcast(F32), ALU.subtract)\
                  .then_inc(h_split, 1)

            def combine(n, e):
                dve.wait_ge(y_chunk, (n + 1) * HC)
                dve.wait_ge(w_copied, n + 1)
                wait(dve, added, n - 1)
                nc.vector.scalar_tensor_tensor(scaled_y[:, e % 2, :], ps_y[e % 2][:, :], b2_sb[:, e:e + 1],
                                               w_rows[:, e % 2, :], ALU.add, ALU.mult).then_inc(y_scaled, 1)

            def update(pair, half):
                b = 2 * pair + half
                dve.wait_ge(out_ready, b + 1)
                nc.vector.tensor_tensor(X[:, bass.ts(b, N)], X[:, bass.ts(b, N)], ps_out[:, :], ALU.add)\
                  .then_inc(x_done, 1)

            graph_stats(0, 0)
            graph_stats(0, 1)
            for half in range(2):
                normalize(0, half)
                if own_ln:
                    graph_stats2(0, half)
                    normalize2(0, half)
            split_x(0, 0)
            top_two(0, 0)
            weights(0, 0)
            split_comb(0, 0)
            chain.end_prologue()
            chain.per_pair = 2 + (2 if own_ln else 0) + 2 * (1 + 2 + 3 + 1) + (2 * NG if split_h else 0)

            def body(pair):
                last_pair = isinstance(pair, int) and pair == PAIRS - 1
                chain.pair(pair)
                for half in range(2):
                    first, last, nxt, prev = steps(pair, half)
                    for g in range(NG):
                        if split_h:
                            split_hidden(pair, half, g)
                        else:
                            dve.wait_ge(gelu_done, (2 * pair + half) * NG + g + 1)
                        done = g - LATE + 1
                        if done % HC == 0 and not (first and done <= 0):
                            combine((2 * pair + half) * E + done // HC - 1, (done // HC - 1) % E)
                        if g == S_UPDATE and not first:
                            update(*prev)
                        if not last:
                            if g == S_TRANSPOSE:
                                split_x(*nxt)
                            if g == S_TOP:
                                top_two(*nxt)
                            if g == S_COMBINE_W:
                                weights(*nxt)
                            if g == S_COMB_SPLIT:
                                split_comb(*nxt)
                        if g == S_STATS and not last_pair:
                            graph_stats(pair + 1, half)
                        if g == S_NORM and not last_pair:
                            normalize(pair + 1, half)
                            if own_ln:
                                graph_stats2(pair + 1, half)
                        if g == S_NORM2 and own_ln and not last_pair:
                            normalize2(pair + 1, half)
                if not last_pair:
                    chain.end_pair()
            pairs(dve, body)
            for done in range(NG - LATE + 1, NG + 1):
                if done % HC == 0:
                    combine((B - 1) * E + done // HC - 1, done // HC - 1)
            update(PAIRS - 1, 1)
            dve.wait_ge(x_done, B)

        @block.tensor
        def _(pe):
            def transposes(pair, half):
                b = 2 * pair + half
                pe.wait_ge(xn_ready, b + 1)
                for r in range(R):
                    ins = nc.tensor.transpose(ps_xT[:, r * P:(r + 1) * P], xn[:, half, r, :], ident[:, :])
                if own_ln:
                    pe.wait_ge(xn2_ready, b + 1)
                    wait(pe, x_done, b - 2)
                    for r in range(R):
                        ins = nc.tensor.transpose(ps_out[:, r * P:(r + 1) * P], xn2[:, half, r, :], ident[:, :])
                ins.then_inc(xT_ready, 1)

            def logits(pair, half):
                b = 2 * pair + half
                pe.wait_ge(xT_copied, (b + 1) * (2 if own_ln else 1))
                wait(pe, combT_split, b)
                for r in range(R):
                    ins = nc.tensor.matmul(ps_small[:, r * E:(r + 1) * E], xT[:, r * P:(r + 1) * P], wr_sb[:, :],
                                           start=True, stop=True)
                ins.then_inc(logits_ready, 1)

            def transpose_comb(pair, half):
                pe.wait_ge(comb_ready, 2 * pair + half + 1)
                for r in range(R):
                    ins = nc.tensor.transpose(ps_small[0:E, r * P:(r + 1) * P], comb[:, r, :], ident[:, :])
                ins.then_inc(combT_ready, 1)

            def first_product(pair, half, g):
                n = (2 * pair + half) * NG + g
                if g == 0:
                    pe.wait_ge(x_split, 2 * pair + half + 1)
                wait(pe, gelu_done, n - 1)
                e, c = g // HC, g % HC
                cols = slice(c * P, (c + 1) * P)
                nc.tensor.matmul(ps_h[g % 2][:, :], w1h[:, e, cols], xh[:, half, :], start=True, stop=False)
                nc.tensor.matmul(ps_h[g % 2][:, :], w1h[:, e, cols], xl[:, half, :], start=False, stop=False)
                nc.tensor.matmul(ps_h[g % 2][:, :], w1l[:, e, cols], xh[:, half, :], start=False, stop=True)\
                  .then_inc(h_ready, 1)

            def second_product(n, g, half):
                e, c = g // HC, g % HC
                slot = g % HR
                y = ps_y[e % 2]
                if split_h:
                    pe.wait_ge(h_split, n + 1)
                    nc.tensor.matmul(y[:, :], w2h[:, e, c, :], hh[:, slot, :], start=c == 0, stop=False)
                    nc.tensor.matmul(y[:, :], w2h[:, e, c, :], hl[:, slot, :], start=False, stop=False)
                    nc.tensor.matmul(y[:, :], w2l[:, e, c, :], hh[:, slot, :], start=False, stop=c == HC - 1)\
                      .then_inc(y_chunk, 1)
                else:
                    pe.wait_ge(gelu_done, n + 1)
                    nc.tensor.matmul(y[:, :], w2h[:, e, c, :], h[:, slot, :], start=c == 0, stop=c == HC - 1)\
                      .then_inc(y_chunk, 1)

            def lagged(pair, half, g):
                b = 2 * pair + half
                lg = g - LAG
                n = b * NG + lg
                if lg < 0:
                    lg, lb, lh = lg + NG, b - 1, 1 - half
                else:
                    lb, lh = b, half
                e = lg // HC
                if lg % HC == 0:
                    if e == 0:
                        pe.wait_ge(combT_split, lb + 1)
                    en = lb * E + e
                    wait(pe, w_copied, en)
                    nc.tensor.matmul(ps_w[:, :], sel[:, e:e + 1].to_broadcast([64, P]), comb_T[:, lh, :], start=True, stop=True)\
                      .then_inc(w_ready, 1)
                    wait(pe, y_scaled, en - 1)
                second_product(n, lg, lh)

            def transpose_out(pair, half):
                b = 2 * pair + half
                pe.wait_ge(added, (b + 1) * E)
                wait(pe, x_done, b)
                for r in range(R):
                    ins = nc.tensor.transpose(ps_out[:, r * P:(r + 1) * P], acc[:, half, r * P:(r + 1) * P], ident[:, :])
                ins.then_inc(out_ready, 1)

            transposes(0, 0)
            logits(0, 0)
            transpose_comb(0, 0)

            def body(pair):
                for half in range(2):
                    first, last, nxt, prev = steps(pair, half)
                    for g in range(NG):
                        first_product(pair, half, g)
                        if not (first and g < LAG):
                            lagged(pair, half, g)
                        if g == S_OUT and not first:
                            transpose_out(*prev)
                        if not last:
                            if g == S_TRANSPOSE:
                                transposes(*nxt)
                            if g == S_LOGITS:
                                logits(*nxt)
                            if g == S_COMB_T:
                                transpose_comb(*nxt)
            pairs(pe, body)
            for g in range(LAG):
                lagged(PAIRS, 0, g)
            transpose_out(PAIRS - 1, 1)


def mamba_layer(nc, env, name, w_in, conv_w, conv_b, dt_bias, a_log, d_skip, norm_w, w_out_t, w_lin, b_lin):
    X, ident = env["X"], env["ident"]
    INNER, STATE, HEADS, HEAD, TAPS = 256, 64, 4, 64, 4
    XBC = INNER + 2 * STATE
    CC = XBC // P
    RMS_EPS = 1e-5
    PAD = 4
    RH = R * HEADS
    ctx = ExitStack()
    with ctx:
        def sb(n, shape, dt=F32):
            return ctx.enter_context(nc.sbuf_tensor(f"{name}_{n}", shape, dt))

        def pb(n):
            return ctx.enter_context(nc.psum_tensor(f"{name}_{n}", [P, 512], F32))

        sem = layer_semaphores(nc, ctx, name)

        wch, wcl = sb("wch", [P, TAPS, XBC], F32R), sb("wcl", [P, TAPS, XBC], F32R)
        wz, wdt_sb = sb("wz", [P, INNER]), sb("wdt", [P, HEADS])
        wo = sb("wo", [P, 2, D])
        half_cb = sb("half_cb", [P, CC])
        dtb, a_neg = sb("dtb", [P, R, HEADS]), sb("a_neg", [P, R, HEADS])
        d_row = sb("d_row", [P, HEADS, HEAD])
        b_row = sb("b_row", [P, R, D])
        rms_eps = sb("rms_eps", [P, 1])
        ones, tri, strict = sb("ones", [P, P]), sb("tri", [P, P]), sb("strict", [P, P])
        xh, xl = sb("xh", [P, PAD + N], F32R), sb("xl", [P, PAD + N], F32R)

        with ExitStack() as setup:
            def ssb(n, shape, dt=F32):
                return setup.enter_context(nc.sbuf_tensor(f"{name}_{n}", shape, dt))

            w_xbc, cw_row, w_tap = ssb("w_xbc", [P, XBC]), ssb("cw_row", [P, TAPS, XBC]), ssb("w_tap", [P, TAPS, XBC])
            wot, wlin, nw = ssb("wot", [P, INNER]), ssb("wlin", [P, D]), ssb("nw", [P, 2])
            d_in, cb_in = ssb("d_in", [P, HEADS]), ssb("cb_in", [P, CC])
            zeros = ssb("zeros", [P, PAD])
            ps_w = setup.enter_context(nc.psum_tensor(f"{name}_ps_w", [P, 512], F32))
            loaded, masks, prep, wo_mm, a_exp = [sem(n) for n in ("loaded", "masks", "prep", "wo_mm", "a_exp")]
            loads = [(w_xbc[:, :], w_in[:, INNER:INNER + XBC]), (wz[:, :], w_in[:, 0:INNER]),
                     (wdt_sb[:, :], w_in[:, INNER + XBC:]), (wot[:, :], w_out_t), (wlin[:, :], w_lin),
                     (nw[:, :], norm_w), (cb_in[:, :], conv_b), (d_in[:, :], d_skip.partition_broadcast(P))]
            loads += [(cw_row[:, k, :], conv_w[k].partition_broadcast(P)) for k in range(TAPS)]
            for r in range(R):
                loads += [(dtb[:, r, :], dt_bias.partition_broadcast(P)), (a_neg[:, r, :], a_log.partition_broadcast(P)),
                          (b_row[:, r, :], b_lin.partition_broadcast(P))]
            with nc.Block() as block:
                @block.sync
                def _(sp):
                    for dst, src in loads:
                        sp.dma_start(dst, src).then_inc(loaded, 16)

                @block.gpsimd
                def _(pool):
                    nc.gpsimd.memset(zeros[:, :], 0.0)
                    nc.gpsimd.memset(rms_eps[:, :], RMS_EPS * INNER)
                    nc.gpsimd.memset(ones[:, :], 1.0).then_inc(masks, 1)
                    pool.wait_ge(masks, 1)
                    nc.gpsimd.affine_select(out=tri[:, :], in_=ones[:, :], compare_op=ALU.is_ge, fill=0.0,
                                            base=0, pattern=[[1, P]], channel_multiplier=-1).then_inc(masks, 1)

                @block.scalar
                def _(act):
                    act.wait_ge(loaded, 16 * len(loads))
                    nc.scalar.activation(a_neg[:, :, :], a_neg[:, :, :], ACT.Exp).then_inc(a_exp, 1)
                    nc.scalar.mul(half_cb[:, :], cb_in[:, :], 0.5)

                @block.tensor
                def _(pe):
                    pe.wait_ge(loaded, 16 * len(loads))
                    for k in range(2):
                        ins = nc.tensor.matmul(ps_w[:, k * D:(k + 1) * D], wot[:, k * P:(k + 1) * P], wlin[:, :],
                                               start=True, stop=True)
                    ins.then_inc(wo_mm, 1)

                @block.vector
                def _(dve):
                    dve.wait_ge(masks, 2)
                    nc.vector.tensor_tensor(strict[:, :], tri[:, :], ident[:, :], ALU.subtract)
                    nc.vector.tensor_copy(xh[:, 0:PAD], zeros[:, :])
                    nc.vector.tensor_copy(xl[:, 0:PAD], zeros[:, :])
                    dve.wait_ge(loaded, 16 * len(loads))
                    for k in range(TAPS):
                        ins = nc.vector.tensor_tensor(w_tap[:, k, :], w_xbc[:, :], cw_row[:, k, :], ALU.mult)
                    ins.then_inc(prep, 1)
                    dve.wait_ge(prep, 1)
                    nc.vector.tensor_copy(wch[:, :, :], w_tap[:, :, :]).then_inc(prep, 1)
                    dve.wait_ge(prep, 2)
                    nc.vector.tensor_tensor(wcl[:, :, :], w_tap[:, :, :], wch[:, :, :].bitcast(F32), ALU.subtract)
                    nc.vector.tensor_copy(d_row[:, :, :], d_in[:, :].unsqueeze(2).to_broadcast([P, HEADS, HEAD]))
                    dve.wait_ge(wo_mm, 1)
                    for k in range(2):
                        nc.vector.tensor_scalar(wo[:, k, :], ps_w[:, k * D:(k + 1) * D], nw[:, k:k + 1], float(INNER) ** 0.5,
                                                ALU.mult, ALU.mult)
                    dve.wait_ge(a_exp, 1)
                    nc.vector.tensor_scalar(a_neg[:, :, :], a_neg[:, :, :], -1.0, None, ALU.mult)

        stats, aggr, rstd = sb("stats", [P, 2, R, 6]), sb("aggr", [P, 2, R, 2]), sb("rstd", [P, 2, R])
        xn = sb("xn", [P, 2, R, P])
        xT = sb("xT", [P, N])
        th, hv = sb("th", [P, 2, N]), sb("hv", [P, 2, N])
        xc = sb("xc", [P, 2, 2, N])
        BT, CT = sb("BT", [STATE, 2, N]), sb("CT", [STATE, 2, N])
        zg = sb("zg", [P, 2, R, INNER])
        dt_raw, dt_abs, dt_exp, dt_ln = [sb(n, [P, RH]) for n in ("dt_raw", "dt_abs", "dt_exp", "dt_ln")]
        dt, dA = sb("dt", [P, 2, RH]), sb("dA", [P, 2, RH])
        acum, exp_acum = sb("acum", [P, 2, RH]), sb("exp_acum", [P, 2, RH])
        rest, exp_rest = sb("rest", [P, RH]), sb("exp_rest", [P, RH])
        exp_total, dt_rest = sb("exp_total", [P, 2, RH]), sb("dt_rest", [P, 2, RH])
        diff, ediff = sb("diff", [P, HEADS, P]), sb("ediff", [P, HEADS, P])
        cb_m = sb("cb_m", [P, P])
        mix = sb("mix", [P, 2, HEADS, P])
        xB = sb("xB", [P, 2, INNER + STATE])
        xdt, xrest, xD = sb("xdt", [P, 2, INNER]), sb("xrest", [P, 2, INNER]), sb("xD", [P, 2, INNER])
        state, decayed = sb("state", [STATE, INNER]), sb("decayed", [STATE, INNER])
        y_part, y, gated = sb("y_part", [P, INNER]), sb("y", [P, INNER]), sb("gated", [P, 2, INNER])
        squares = sb("squares", [P, INNER])
        sumsq, rms = sb("sumsq", [P, 2]), sb("rms", [P, 2])
        gT = sb("gT", [P, 2, INNER])
        minus_half1 = env["minus_half"][:, 0:1]

        ps_f = [pb("ps_f0"), pb("ps_f1")]
        ps_bc, ps_c1, ps_c2, ps_s, ps_small, ps_c3 = [pb(n) for n in ("ps_bc", "ps_c1", "ps_c2", "ps_s", "ps_small", "ps_c3")]

        (stats_ready, rstd_ready, xn_ready, f_ready, f_read, x_split, conv_act, silu_done, dtm_ready, dt_pre, dt_ln_done, dA_ready,
         cum_ready, cum_act, cum_dve, rest_exp, front_done, c1_ready, c1_copied, diff_ready, ediff_ready, mix_ready,
         c2_ready, state_done, decay_done, gated_ready, sq_done, rms_ready, gT_ready, gT_copied, o_ready, x_done, xD_ready,
         z_act, zg_ready, dve_chain, pool_chain) = [sem(n) for n in (
             "stats_ready rstd_ready xn_ready f_ready f_read x_split conv_act silu_done dtm_ready dt_pre dt_ln_done dA_ready "
             "cum_ready cum_act cum_dve rest_exp front_done c1_ready c1_copied diff_ready ediff_ready mix_ready "
             "c2_ready state_done decay_done gated_ready sq_done rms_ready gT_ready gT_copied o_ready x_done xD_ready "
             "z_act zg_ready dve_chain pool_chain").split()]
        FU = 1 + CC + 2

        block = ctx.enter_context(nc.Block())

        def schedule(body_of):
            def body(pair):
                for half in range(2):
                    first = isinstance(pair, int) and pair == 0 and half == 0
                    last = isinstance(pair, int) and pair == PAIRS - 1 and half == 1
                    nxt = (pair, 1) if half == 0 else (pair + 1, 0)
                    for r in range(R):
                        body_of(pair, half, r, first, last, nxt)
            return body

        @block.gpsimd
        def _(pool):
            chain = Chain(pool, pool_chain, 0)

            def rstd_of(pair, half):
                b = 2 * pair + half
                pool.wait_ge(stats_ready, b + 1)
                chain.link(nc.gpsimd.tensor_tensor(rstd[:, half, :], aggr[:, half, :, 1], env["eps"][:, :], ALU.add))
                nc.gpsimd.tensor_tensor(rstd[:, half, :], rstd[:, half, :], env["minus_half"][:, :], ALU.pow)\
                  .then_inc(rstd_ready, 1)

            def add_bias(pair, half):
                b = 2 * pair + half
                pool.wait_ge(xn_ready, b + 1)
                alone(pool, env["pool_passed"])
                chain.link(nc.gpsimd.tensor_tensor(X[:, bass.ts(b, N)], X[:, bass.ts(b, N)],
                                                   b_row[:, :, :].rearrange("p r d -> p (r d)"), ALU.add))

            def skip(n, s):
                pool.wait_ge(c1_copied, n + 1)
                wait(pool, gated_ready, n - 1)
                nc.gpsimd.tensor_tensor(xD[:, s, :], xB[:, s, 0:INNER], d_row[:, :, :].rearrange("p h c -> p (h c)"), ALU.mult)\
                    .then_inc(xD_ready, 1)

            def rms_of(n, s):
                pool.wait_ge(sq_done, n + 1)
                chain.link(nc.gpsimd.tensor_tensor(rms[:, s:s + 1], sumsq[:, s:s + 1], rms_eps[:, :], ALU.add))
                nc.gpsimd.tensor_tensor(rms[:, s:s + 1], rms[:, s:s + 1], minus_half1, ALU.pow).then_inc(rms_ready, 1)

            rstd_of(0, 0)
            rstd_of(0, 1)
            add_bias(0, 0)
            add_bias(0, 1)
            skip(0, 0)
            chain.end_prologue()
            chain.per_pair = 2 * 2 + 2 * R

            def step(pair, half, r, first, last, nxt):
                n = (2 * pair + half) * R + r
                rms_of(n, r % 2)
                if not (last and r == R - 1):
                    skip(n + 1, (r + 1) % 2)
                if not (isinstance(pair, int) and pair == PAIRS - 1):
                    if r == 1:
                        rstd_of(pair + 1, half)
                    if r == 3:
                        add_bias(pair + 1, half)
            inner = schedule(step)

            def body(pair):
                chain.pair(pair)
                inner(pair)
                if not (isinstance(pair, int) and pair == PAIRS - 1):
                    chain.end_pair()
            pairs(pool, body)


        @block.scalar
        def _(act):
            def copy_xT(b):
                act.wait_ge(f_ready, b * FU + 1)
                wait(act, x_split, b)
                wait(act, f_ready, (b - 1) * FU + FU)
                nc.scalar.copy(xT[:, :], ps_f[0][:, :]).then_inc(f_read, 1)

            def conv_act_of(b, c):
                u = 1 + c
                act.wait_ge(f_ready, b * FU + u + 1)
                wait(act, silu_done, b * CC + c - 1 if c >= 2 else b * CC)
                if c < 2:
                    wait(act, zg_ready, b * 2)
                nc.scalar.activation(th[:, c % 2, :], ps_f[u % 2][:, :], ACT.Tanh, bias=half_cb[:, c:c + 1], scale=0.5)
                nc.scalar.activation(hv[:, c % 2, :], ps_f[u % 2][:, :], ACT.Identity, bias=half_cb[:, c:c + 1], scale=0.5)\
                    .then_inc(f_read, 1)

            def z_act_of(b, k):
                u = 1 + CC + k
                act.wait_ge(f_ready, b * FU + u + 1)
                wait(act, silu_done, (b + 1) * CC)
                s = (k + 1) % 2
                nc.scalar.activation(th[:, s, :], ps_f[u % 2][:, :], ACT.Tanh, scale=0.5)
                nc.scalar.activation(hv[:, s, :], ps_f[u % 2][:, :], ACT.Identity, scale=0.5).then_inc(f_read, 1)

            def dt_act(b):
                act.wait_ge(dt_pre, b + 1)
                nc.scalar.activation(dt_abs[:, :], dt_raw[:, :], ACT.Abs).then_inc(dt_ln_done, 1)
                act.wait_ge(dt_ln_done, 3 * b + 1)
                nc.scalar.activation(dt_exp[:, :], dt_abs[:, :], ACT.Exp, scale=-1.0).then_inc(dt_ln_done, 1)
                act.wait_ge(dt_ln_done, 3 * b + 2)
                nc.scalar.activation(dt_ln[:, :], dt_exp[:, :], ACT.Ln, bias=1.0).then_inc(dt_ln_done, 1)

            def cum_act_of(b, half):
                act.wait_ge(cum_dve, b + 1)
                nc.scalar.activation(exp_acum[:, half, :], acum[:, half, :], ACT.Exp)
                nc.scalar.activation(exp_total[:, half, :], ps_small[:, 2 * RH:3 * RH], ACT.Exp)
                nc.scalar.activation(exp_rest[:, :], rest[:, :], ACT.Exp).then_inc(rest_exp, 1)

            def exp_diff(n):
                act.wait_ge(diff_ready, n + 1)
                wait(act, mix_ready, n)
                nc.scalar.activation(ediff[:, :, :], diff[:, :, :], ACT.Exp).then_inc(ediff_ready, 1)

            def copy_c1(n, s):
                act.wait_ge(c1_ready, n + 1)
                wait(act, c2_ready, n - 1)
                wait(act, diff_ready, n - 1)
                nc.scalar.copy(xB[:, s, :], ps_c1[:, P:P + INNER + STATE]).then_inc(c1_copied, 1)

            def square(n, s):
                act.wait_ge(gated_ready, n + 1)
                nc.scalar.activation(squares[:, :], gated[:, s, :], ACT.Square, accum_out=sumsq[:, s:s + 1]).then_inc(sq_done, 1)

            def copy_gT(n, s):
                act.wait_ge(gT_ready, n + 1)
                nc.scalar.copy(gT[:, s, :], ps_c3[:, 0:INNER]).then_inc(gT_copied, 1)

            def front_step(b, half, r):
                if r == 0:
                    copy_xT(b)
                if r == 1:
                    conv_act_of(b, 0)
                    conv_act_of(b, 1)
                    conv_act_of(b, 2)
                if r == 2:
                    dt_act(b)
                    cum_act_of(b, half)
                if r == 3:
                    z_act_of(b, 0)
                    z_act_of(b, 1)

            for r in range(3):
                front_step(0, 0, r)
            copy_c1(0, 0)
            exp_diff(0)
            front_step(0, 0, 3)

            def step(pair, half, r, first, last, nxt):
                n = (2 * pair + half) * R + r
                if not (first and r == 0):
                    copy_gT(n - 1, (r + 1) % 2)
                if not last and r < 3:
                    front_step(2 * nxt[0] + nxt[1], nxt[1], r)
                square(n, r % 2)
                if not (last and r == R - 1):
                    copy_c1(n + 1, (r + 1) % 2)
                    exp_diff(n + 1)
                if not last and r == 3:
                    front_step(2 * nxt[0] + nxt[1], nxt[1], 3)
            pairs(act, schedule(step))
            copy_gT(B * R - 1, 1)

        @block.vector
        def _(dve):
            chain = Chain(dve, dve_chain, 0)

            def graph_stats(pair, half):
                b = 2 * pair + half
                wait(dve, xn_ready, b - 1)
                for r in range(R):
                    ins = nc.vector.bn_stats(stats[:, half, r, :], X[:, bass.ds(b * N + r * D, D)])
                chain.link(ins)
                alone(dve, env["dve_passed"])
                for r in range(R):
                    ins = nc.vector.bn_aggr(aggr[:, half, r, :], stats[:, half, r, :])
                ins.then_inc(stats_ready, 1)

            def normalize(pair, half):
                b = 2 * pair + half
                dve.wait_ge(rstd_ready, b + 1)
                wait(dve, f_ready, FU * (b - 2) + 1)
                for r in range(R):
                    ins = nc.vector.tensor_scalar(xn[:, half, r, :], X[:, bass.ds(b * N + r * D, D)],
                                                  aggr[:, half, r, 0:1], rstd[:, half, r:r + 1], ALU.subtract, ALU.mult)
                ins.then_inc(xn_ready, 1)

            def split_x(b):
                dve.wait_ge(f_read, b * FU + 1)
                wait(dve, f_ready, (b - 1) * FU + 1 + CC)
                chain.link(nc.vector.tensor_copy(xh[:, PAD:], xT[:, :]))
                nc.vector.tensor_tensor(xl[:, PAD:], xT[:, :], xh[:, PAD:].bitcast(F32), ALU.subtract).then_inc(x_split, 1)

            def silu(b, half, c):
                dve.wait_ge(f_read, b * FU + 1 + c + 1)
                wait(dve, c1_ready, (b - 1) * R)
                if c < 2:
                    nc.vector.scalar_tensor_tensor(xc[:, half, c, :], th[:, c % 2, :], 1.0, hv[:, c % 2, :], ALU.add, ALU.mult)\
                        .then_inc(silu_done, 1)
                else:
                    wait(dve, c2_ready, (b - 1) * R)
                    nc.vector.scalar_tensor_tensor(BT[:, half, :], th[0:STATE, 0, :], 1.0, hv[0:STATE, 0, :], ALU.add, ALU.mult)
                    nc.vector.scalar_tensor_tensor(CT[:, half, :], th[STATE:, 0, :], 1.0, hv[STATE:, 0, :], ALU.add, ALU.mult)\
                        .then_inc(silu_done, 1)

            def z_silu(b, half, k):
                dve.wait_ge(f_read, b * FU + 1 + CC + k + 1)
                s = (k + 1) % 2
                nc.vector.scalar_tensor_tensor(zg[:, half, 2 * k:2 * k + 2, :].rearrange("p r c -> p (r c)"), th[:, s, :], 1.0,
                                               hv[:, s, :], ALU.add, ALU.mult).then_inc(zg_ready, 1)

            def dt_first(b):
                dve.wait_ge(dtm_ready, b + 1)
                nc.vector.tensor_tensor(dt_raw[:, :], ps_small[:, 0:RH], dtb[:, :, :].rearrange("p r h -> p (r h)"), ALU.add)\
                    .then_inc(dt_pre, 1)

            def dt_second(b, half):
                dve.wait_ge(dt_ln_done, 3 * b + 3)
                dve.wait_ge(dt_pre, b + 1)
                wait(dve, c1_ready, (b - 1) * R)
                chain.link(nc.vector.scalar_tensor_tensor(dt[:, half, :], dt_raw[:, :], 0.0, dt_ln[:, :], ALU.max, ALU.add))
                nc.vector.tensor_tensor(dA[:, half, :], dt[:, half, :], a_neg[:, :, :].rearrange("p r h -> p (r h)"), ALU.mult)\
                    .then_inc(dA_ready, 1)

            def cum_first(b, half):
                dve.wait_ge(cum_ready, b + 1)
                chain.link(nc.vector.tensor_copy(acum[:, half, :], ps_small[:, RH:2 * RH]))
                wait(dve, rest_exp, b)
                nc.vector.tensor_tensor(rest[:, :], ps_small[:, 2 * RH:3 * RH], acum[:, half, :], ALU.subtract)\
                    .then_inc(cum_dve, 1)

            def cum_second(b, half):
                dve.wait_ge(rest_exp, b + 1)
                nc.vector.tensor_tensor(dt_rest[:, half, :], exp_rest[:, :], dt[:, half, :], ALU.mult).then_inc(front_done, 1)

            def by_head(v, half, r):
                return v[:, half, r * HEADS:(r + 1) * HEADS].unsqueeze(2).to_broadcast([P, HEADS, HEAD])

            def chunk_first(n, b, half, r):
                s = r % 2
                dve.wait_ge(c1_ready, n + 1)
                wait(dve, ediff_ready, n)
                dve.wait_ge(front_done, b + 1)
                for h in range(HEADS):
                    ins = nc.vector.scalar_tensor_tensor(diff[:, h, :], ps_bc[:, h * P:(h + 1) * P],
                                                         acum[:, half, r * HEADS + h:r * HEADS + h + 1], strict[:, :],
                                                         ALU.subtract, ALU.mult)
                ins.then_inc(diff_ready, 1)
                dve.wait_ge(c1_copied, n + 1)
                wait(dve, mix_ready, n)
                chain.link(nc.vector.tensor_tensor(cb_m[:, :], ps_c1[:, 0:P], tri[:, :], ALU.mult))
                wait(dve, c2_ready, n - 1)
                x_v = xB[:, s, 0:INNER].rearrange("p (h c) -> p h c", c=HEAD)
                nc.vector.tensor_tensor(xdt[:, s, :].rearrange("p (h c) -> p h c", c=HEAD), x_v, by_head(dt, half, r), ALU.mult)
                nc.vector.tensor_tensor(xrest[:, s, :].rearrange("p (h c) -> p h c", c=HEAD), x_v, by_head(dt_rest, half, r),
                                        ALU.mult)
                dve.wait_ge(ediff_ready, n + 1)
                nc.vector.scalar_tensor_tensor(mix[:, s, :, :], ediff[:, :, :], 1.0, cb_m[:, :].unsqueeze(1).to_broadcast([P, HEADS, P]),
                                               ALU.min, ALU.mult).then_inc(mix_ready, 1)

            def chunk_second(n, half, r):
                s = r % 2
                dve.wait_ge(c2_ready, n + 1)
                if r == 0:
                    nc.vector.tensor_copy(state[:, :], ps_s[0:STATE, 0:INNER]).then_inc(state_done, 1)
                else:
                    chain.link(nc.vector.tensor_tensor(
                        decayed[:, :].rearrange("p (h c) -> p h c", c=HEAD), state[:, :].rearrange("p (h c) -> p h c", c=HEAD),
                        exp_total[0:STATE, half, r * HEADS:(r + 1) * HEADS].unsqueeze(2).to_broadcast([STATE, HEADS, HEAD]),
                        ALU.mult))
                    nc.vector.tensor_tensor(state[:, :], decayed[:, :], ps_s[0:STATE, 0:INNER], ALU.add).then_inc(state_done, 1)
                dve.wait_ge(xD_ready, n + 1)
                if r == 0:
                    chain.link(nc.vector.tensor_tensor(y[:, :], ps_c2[:, 0:INNER], xD[:, s, :], ALU.add))
                else:
                    for h in range(HEADS):
                        cols = slice(h * HEAD, (h + 1) * HEAD)
                        ins = nc.vector.scalar_tensor_tensor(y_part[:, cols], ps_c2[:, INNER + h * HEAD:INNER + (h + 1) * HEAD],
                                                             exp_acum[:, half, r * HEADS + h:r * HEADS + h + 1], xD[:, s, cols],
                                                             ALU.mult, ALU.add)
                    chain.link(ins)
                    chain.link(nc.vector.tensor_tensor(y[:, :], y_part[:, :], ps_c2[:, 0:INNER], ALU.add))
                wait(dve, gT_ready, n - 1)
                wait(dve, sq_done, n - 1)
                nc.vector.tensor_tensor(gated[:, s, :], y[:, :], zg[:, half, r, :], ALU.mult).then_inc(gated_ready, 1)

            def update(n, col, s):
                dve.wait_ge(o_ready, n + 1)
                dve.wait_ge(rms_ready, n + 1)
                nc.vector.scalar_tensor_tensor(X[:, bass.ds(col, D)], ps_c3[:, INNER:INNER + D], rms[:, s:s + 1],
                                               X[:, bass.ds(col, D)], ALU.mult, ALU.add).then_inc(x_done, 1)

            def front_step(b, half, r):
                if r == 0:
                    split_x(b)
                if r == 1:
                    silu(b, half, 0)
                    silu(b, half, 1)
                    silu(b, half, 2)
                    dt_first(b)
                if r == 2:
                    dt_second(b, half)
                    cum_first(b, half)
                    cum_second(b, half)
                if r == 3:
                    z_silu(b, half, 0)
                    z_silu(b, half, 1)

            graph_stats(0, 0)
            graph_stats(0, 1)
            normalize(0, 0)
            normalize(0, 1)
            for r in range(3):
                front_step(0, 0, r)
            chunk_first(0, 0, 0, 0)
            front_step(0, 0, 3)
            chain.end_prologue()
            chain.per_pair = 2 * (1 + 1 + 1 + 1 + R + 1 + 3 * (R - 1))

            def step(pair, half, r, first, last, nxt):
                b = 2 * pair + half
                n = b * R + r
                chunk_second(n, half, r)
                if not last and r < 3:
                    front_step(2 * nxt[0] + nxt[1], nxt[1], r)
                if not (last and r == R - 1):
                    if r < R - 1:
                        chunk_first(n + 1, b, half, r + 1)
                    else:
                        chunk_first(n + 1, b + 1, 1 - half, 0)
                if not last and r == 3:
                    front_step(2 * nxt[0] + nxt[1], nxt[1], 3)
                if not (first and r == 0):
                    update(n - 1, (n - 1) * D, (r + 1) % 2)
                if not (isinstance(pair, int) and pair == PAIRS - 1):
                    if r == 1:
                        graph_stats(pair + 1, half)
                    if r == 3:
                        normalize(pair + 1, half)
            inner = schedule(step)

            def body(pair):
                chain.pair(pair)
                inner(pair)
                if not (isinstance(pair, int) and pair == PAIRS - 1):
                    chain.end_pair()
            pairs(dve, body)
            update(B * R - 1, (B * R - 1) * D, 1)
            dve.wait_ge(x_done, B * R)

        @block.tensor
        def _(pe):
            def transposes(b, half):
                pe.wait_ge(xn_ready, b + 1)
                wait(pe, f_read, b * FU - 1)
                for r in range(R):
                    ins = nc.tensor.transpose(ps_f[0][:, r * P:(r + 1) * P], xn[:, half, r, :], ident[:, :])
                ins.then_inc(f_ready, 1)

            def conv(b, c):
                u = 1 + c
                if c == 0:
                    pe.wait_ge(x_split, b + 1)
                wait(pe, f_read, b * FU + u - 1)
                cols = slice(c * P, (c + 1) * P)
                for k in range(TAPS):
                    shift = slice(PAD - (TAPS - 1) + k, PAD - (TAPS - 1) + k + N)
                    nc.tensor.matmul(ps_f[u % 2][:, :], wch[:, k, cols], xh[:, shift], start=k == 0, stop=False)
                    nc.tensor.matmul(ps_f[u % 2][:, :], wch[:, k, cols], xl[:, shift], start=False, stop=False)
                    ins = nc.tensor.matmul(ps_f[u % 2][:, :], wcl[:, k, cols], xh[:, shift], start=False, stop=k == TAPS - 1)
                ins.then_inc(f_ready, 1)

            def z_of(b, k):
                u = 1 + CC + k
                wait(pe, f_read, b * FU + u - 1)
                for j in range(2):
                    r = 2 * k + j
                    ins = nc.tensor.matmul(ps_f[u % 2][:, j * INNER:(j + 1) * INNER], xT[:, r * P:(r + 1) * P], wz[:, :],
                                           start=True, stop=True)
                ins.then_inc(f_ready, 1)

            def dt_of(b):
                wait(pe, rest_exp, b)
                for r in range(R):
                    ins = nc.tensor.matmul(ps_small[:, r * HEADS:(r + 1) * HEADS], xT[:, r * P:(r + 1) * P], wdt_sb[:, :],
                                           start=True, stop=True)
                ins.then_inc(dtm_ready, 1)

            def sums(b, half):
                pe.wait_ge(dA_ready, b + 1)
                nc.tensor.matmul(ps_small[:, RH:2 * RH], tri[:, :], dA[:, half, :], start=True, stop=True)
                nc.tensor.matmul(ps_small[:, 2 * RH:3 * RH], ones[:, :], dA[:, half, :], start=True, stop=True)\
                    .then_inc(cum_ready, 1)

            def chunk_prep(n, b, half, r):
                wait(pe, diff_ready, n)
                wait(pe, c1_copied, n)
                wait(pe, mix_ready, n)
                if r == 0:
                    pe.wait_ge(silu_done, (b + 1) * CC)
                for h in range(HEADS):
                    col = r * HEADS + h
                    nc.tensor.matmul(ps_bc[:, h * P:(h + 1) * P], dA[:, half, col:col + 1].to_broadcast([P, P]), tri[:, :],
                                     start=True, stop=True)
                tile = slice(r * P, (r + 1) * P)
                nc.tensor.matmul(ps_c1[:, 0:P], BT[:, half, tile], CT[:, half, tile], start=True, stop=True)
                for k in range(2):
                    nc.tensor.transpose(ps_c1[:, P + k * P:P + (k + 1) * P], xc[:, half, k, tile], ident[:, :])
                nc.tensor.transpose(ps_c1[:, P + INNER:P + INNER + STATE], BT[:, half, tile], ident[0:STATE, 0:STATE])\
                    .then_inc(c1_ready, 1)

            def chunk_products(n, half, r):
                s = r % 2
                pe.wait_ge(mix_ready, n + 1)
                wait(pe, gated_ready, n)
                wait(pe, state_done, n)
                for h in range(HEADS):
                    nc.tensor.matmul(ps_c2[:, h * HEAD:(h + 1) * HEAD], mix[:, s, h, :], xdt[:, s, h * HEAD:(h + 1) * HEAD],
                                     start=True, stop=True)
                if r > 0:
                    nc.tensor.matmul(ps_c2[:, INNER:2 * INNER], CT[:, half, r * P:(r + 1) * P], state[:, :],
                                     start=True, stop=True)
                nc.tensor.matmul(ps_s[0:STATE, 0:INNER], xB[:, s, INNER:INNER + STATE], xrest[:, s, :],
                                 start=True, stop=True).then_inc(c2_ready, 1)

            def transpose_gated(n, s):
                pe.wait_ge(gated_ready, n + 1)
                wait(pe, x_done, n)
                for k in range(2):
                    ins = nc.tensor.transpose(ps_c3[:, k * P:(k + 1) * P], gated[:, s, k * P:(k + 1) * P], ident[:, :])
                ins.then_inc(gT_ready, 1)

            def project(n, s):
                pe.wait_ge(gT_copied, n + 1)
                for k in range(2):
                    ins = nc.tensor.matmul(ps_c3[:, INNER:INNER + D], gT[:, s, k * P:(k + 1) * P], wo[:, k, :],
                                           start=k == 0, stop=k == 1)
                ins.then_inc(o_ready, 1)

            def front_step(b, half, r):
                if r == 0:
                    transposes(b, half)
                if r == 1:
                    conv(b, 0)
                    conv(b, 1)
                    conv(b, 2)
                    dt_of(b)
                if r == 2:
                    sums(b, half)
                if r == 3:
                    z_of(b, 0)
                    z_of(b, 1)

            for r in range(3):
                front_step(0, 0, r)
            chunk_prep(0, 0, 0, 0)
            front_step(0, 0, 3)

            def step(pair, half, r, first, last, nxt):
                b = 2 * pair + half
                n = b * R + r
                if not (first and r == 0):
                    transpose_gated(n - 1, (r + 1) % 2)
                chunk_products(n, half, r)
                if not last and r < 3:
                    front_step(2 * nxt[0] + nxt[1], nxt[1], r)
                if not (last and r == R - 1):
                    if r < R - 1:
                        chunk_prep(n + 1, b, half, r + 1)
                    else:
                        chunk_prep(n + 1, b + 1, 1 - half, 0)
                if not last and r == 3:
                    front_step(2 * nxt[0] + nxt[1], nxt[1], 3)
                if not (first and r == 0):
                    project(n - 1, (r + 1) % 2)
            pairs(pe, schedule(step))
            transpose_gated(B * R - 1, 1)
            project(B * R - 1, 1)


def build(nc, a, out, layers=range(8), only_load=None):
    ctx = ExitStack()
    with ctx:
        X = ctx.enter_context(nc.sbuf_tensor("X", [P, B * N], F32))
        ident = ctx.enter_context(nc.sbuf_tensor("ident", [P, P], F32))
        minus_half = ctx.enter_context(nc.sbuf_tensor("minus_half", [P, R], F32))
        ident_zero, ident_done = (ctx.enter_context(nc.semaphore(n)) for n in ("ident_zero", "ident_done"))
        dve_passed, pool_passed = (ctx.enter_context(nc.semaphore(n)) for n in ("dve_passed", "pool_passed"))
        out_stored = ctx.enter_context(nc.semaphore("out_stored"))
        mask_dram = nc.dram_tensor("mask_dram", [B, P, R * N], BF16, kind="Internal").ap()
        eps = ctx.enter_context(nc.sbuf_tensor("eps", [P, R], F32))
        env = {"X": X, "ident": ident, "minus_half": minus_half, "eps": eps, "mask_dram": mask_dram,
               "dve_passed": dve_passed, "pool_passed": pool_passed}

        with nc.Block() as block:
            @block.gpsimd
            def _(pool):
                nc.gpsimd.memset(minus_half[:, :], -0.5)
                nc.gpsimd.memset(eps[:, :], LN_EPS)
                nc.gpsimd.memset(ident[:, :], 0.0).then_inc(ident_zero, 1)
                pool.wait_ge(ident_zero, 1)
                nc.gpsimd.affine_select(out=ident[:, :], in_=ident[:, :], compare_op=ALU.not_equal, fill=1.0,
                                        base=0, pattern=[[-1, P]], channel_multiplier=1).then_inc(ident_done, 1)
                pool.wait_ge(ident_done, 1)

        if 0 not in layers:
            only_load(nc, env, a)
        else:
            gnn_layer(nc, env, "g0", a["L0_gnn_W"], a["L0_gnn_Wt"], a["L0_gnn_A"], 1, elu=True,
                      node_mask=True, load=(a["x"], a["adj"], a["nodemask"]))
        if 1 in layers:
            f = {k: a[f"L0_ffn_{k}"] for k in ("W_in", "conv_w", "conv_b", "dt_bias", "A_log", "D", "norm_w", "W_out_t",
                                               "W_lin", "b_lin")}
            mamba_layer(nc, env, "f0", f["W_in"], f["conv_w"], f["conv_b"], f["dt_bias"], f["A_log"], f["D"],
                        f["norm_w"], f["W_out_t"], f["W_lin"], f["b_lin"])
        if 2 in layers:
            gnn_layer(nc, env, "g1", a["L1_gnn_W"], a["L1_gnn_Wt"], a["L1_gnn_A"], 1)
        if 3 in layers:
            moe_layer(nc, env, "f1", a["L1_ffn_w1"], a["L1_ffn_b1"], a["L1_ffn_w2"], a["L1_ffn_b2"],
                      a["L1_ffn_router_w"], None, 128, keep_tokens=True, split_h=False)
        if 4 in layers:
            gnn_layer(nc, env, "g2", a["L2_gnn_W"], a["L2_gnn_Wt"], a["L2_gnn_A"], 1, elu=True)
        if 5 in layers:
            moe_layer(nc, env, "f2", a["L2_ffn_W1"], a["L2_ffn_b1"], a["L2_ffn_W2"], a["L2_ffn_b2"],
                      a["L2_ffn_Wg"], a["L2_ffn_bg"], 512)
        if 6 in layers:
            gnn_layer(nc, env, "g3", a["L3_gnn_W"], a["L3_gnn_Wt"], a["L3_gnn_A"], 4, bias=a["L3_gnn_b"])
        if 7 in layers:
            moe_layer(nc, env, "f3", a["L3_ffn_W1"], a["L3_ffn_b1"], a["L3_ffn_W2"], a["L3_ffn_b2"],
                      a["L3_ffn_Wr"], a["L3_ffn_br"], 512, own_ln=(a["L3_ffn_ln_g"], a["L3_ffn_ln_b"]))

        with nc.Block() as block:
            @block.sync
            def _(sp):
                out_v = out.rearrange("b (r p) d -> p (b r) d", p=P)
                sp.dma_start(out_v, X[:, :].rearrange("p (t d) -> p t d", d=D)).then_inc(out_stored, 16)
                sp.wait_ge(out_stored, 16)


def _layout(inputs):
    arrays = {k: np.ascontiguousarray(v) for k, v in inputs.items()}
    arrays["nodemask"] = np.ascontiguousarray(inputs["nodemask"].reshape(B * R, P).T)
    for l in range(4):
        w, a = arrays.pop(f"L{l}_gnn_W"), arrays.pop(f"L{l}_gnn_a")
        if l >= 2:
            w = w.T
        arrays[f"L{l}_gnn_W"], arrays[f"L{l}_gnn_Wt"] = np.ascontiguousarray(w), np.ascontiguousarray(w.T)
        heads = a.shape[0] if l == 3 else 1
        a = a.reshape(heads, 2, D // heads)
        cols = np.zeros((D, 2 * heads), a.dtype)
        for h in range(heads):
            for side in range(2):
                cols[h * (D // heads):(h + 1) * (D // heads), side * heads + h] = a[h, side]
        arrays[f"L{l}_gnn_A"] = cols
    for name in ("L0_ffn_conv_b", "L0_ffn_norm_w"):
        arrays[name] = np.ascontiguousarray(arrays[name].reshape(-1, P).T)
    arrays["L0_ffn_conv_w"] = np.ascontiguousarray(arrays["L0_ffn_conv_w"].T)
    arrays["L0_ffn_W_out_t"] = np.ascontiguousarray(arrays.pop("L0_ffn_W_out").T)
    arrays["L1_ffn_router_w"] = np.ascontiguousarray(arrays["L1_ffn_router_w"].T)
    for l in (1, 2, 3):
        name = f"L{l}_ffn_b1"
        arrays[name] = np.ascontiguousarray(arrays[name].reshape(-1, P).T)
        arrays[f"L{l}_ffn_b2"] = np.ascontiguousarray(arrays[f"L{l}_ffn_b2"].T)
    for name in ("L3_ffn_ln_g", "L3_ffn_ln_b"):
        arrays[name] = np.ascontiguousarray(arrays[name].T)
    return arrays


def kernel(**inputs):
    import concourse.bacc as bacc
    from concourse.bass_utils import run_bass_kernel_spmd

    arrays = {f"in_{k}": v for k, v in _layout(inputs).items()}
    nc = bacc.Bacc("TRN2", target_bir_lowering=False, num_devices=1)
    aps = {k[3:]: nc.dram_tensor(k, v.shape, mybir.dt.from_np(v.dtype), kind="ExternalInput").ap()
           for k, v in arrays.items()}
    out = nc.dram_tensor("out", [B, N, D], F32, kind="ExternalOutput").ap()
    build(nc, aps, out)
    r = run_bass_kernel_spmd(nc, [arrays], core_ids=[0])
    return r.results[0]["out"]
```

```python
import numpy as np
import concourse.bass as bass
from concourse import mybir
from contextlib import ExitStack

F32 = mybir.dt.float32
F32R = mybir.dt.float32r
BF16 = mybir.dt.bfloat16
I32 = mybir.dt.int32
U32 = mybir.dt.uint32
ALU = mybir.AluOpType
ACT = mybir.ActivationFunctionType
AX = mybir.AxisListType

B, N, D = 16, 512, 128
P = 128
R = N // P
PAIRS = B // 2
E = 8
LN_EPS = 1e-5
SLOPE = 0.2
MASKED = -float(2 ** 53)


def pairs(eng, body):
    body(0)
    with eng.Fori(1, PAIRS - 1) as pair:
        body(pair)
    body(PAIRS - 1)


def wait(eng, sem, value):
    if isinstance(value, int) and value <= 0:
        return
    eng.wait_ge(sem, value)


def layer_semaphores(nc, ctx, name):
    made = []

    def clear():
        nc.clear_and_free_semaphores(made)
        nc.all_engine_barrier()

    def sem(n):
        made.append(nc.alloc_semaphore(name=f"{name}_{n}"))
        return made[-1]
    ctx.callback(clear)
    return sem


def alone(eng, passed):
    eng.sem_inc(passed, 1)


class Chain:

    def __init__(self, eng, sem, per_pair):
        self.eng, self.sem, self.per_pair = eng, sem, per_pair
        self.base, self.count, self.before = 0, 0, 0

    def pair(self, pair):
        self.base, self.count = pair * self.per_pair + self.before, 0

    def end_pair(self):
        assert self.count == self.per_pair, f"chain {self.count}"

    def link(self, ins):
        self.count += 1
        ins.then_inc(self.sem, 1)
        self.eng.wait_ge(self.sem, self.base + self.count)

    def end_prologue(self):
        self.before, self.count = self.count, 0


def gnn_layer(nc, env, name, w, wt, a_pad, heads, elu=False, node_mask=None, bias=None, load=None):
    X, ident, mask_dram = env["X"], env["ident"], env["mask_dram"]
    C = D // heads
    T = heads * R
    Z_AT, SCORE_AT, LEAKY_AT, TRANS_AT, COPY_AT = 7, 6, 5, -1, -2
    ATTEND_AT = COPY_AT - R
    if heads == 1:
        G = 4
        STATS_AT, NORM_AT, XT_AT, ROWS_AT, SPLIT_AT, SIDES_AT = 14, 12, 11, 10, 9, 8
    else:
        G = 2
        STATS_AT, NORM_AT, XT_AT, ROWS_AT, SPLIT_AT, SIDES_AT = 20, 18, 16, 15, 13, 12
    MASK_AT, WH_AT, COPY_WH_AT = 8, -2, -3
    OUT_AT, BACK_AT, FINISH_AT, ELU_AT, UPDATE_AT = [-(T + R + 2 + i) for i in range(5)]
    TAIL = -UPDATE_AT
    TURNS = B // G
    LAG = -(-(WH_AT - BACK_AT) // T)
    ctx = ExitStack()
    with ctx:
        def sb(n, shape, dt=F32):
            return ctx.enter_context(nc.sbuf_tensor(f"{name}_{n}", shape, dt))

        def pb(n):
            return ctx.enter_context(nc.psum_tensor(f"{name}_{n}", [P, 512], F32))

        sem = layer_semaphores(nc, ctx, name)

        w_sb, wt_sb, a_sb = sb("w", [P, D]), sb("wt", [P, D]), sb("a", [P, P])
        wa = sb("wa", [P, P])
        st_const = sb("st_const", [P, 1])
        row_lo, row_hi = sb("row_lo", [P, 1]), sb("row_hi", [P, 1])
        head_lo, head_hi = sb("head_lo", [P, heads]), sb("head_hi", [P, heads])
        stats, aggr, rstd = sb("stats", [P, 2, R, 6]), sb("aggr", [P, 2, R, 2]), sb("rstd", [P, 2, R])
        xn = sb("xn", [P, 2, R, P])
        xT = sb("xT", [P, G, N])
        wh = sb("wh", [P, 2, R, D])
        rows = sb("rows", [P, N], F32R)
        lhs, rhs = sb("lhs", [P, 2, heads, N], F32R), sb("rhs", [P, 2, N], F32R)
        score = sb("score", [P, 2, R, N])
        z_max, z_low, neg_top = sb("z_max", [P, 2, R]), sb("z_low", [P, R]), sb("neg_top", [P, 2, R])
        prob, probT = sb("prob", [P, R, N]), sb("probT", [P, 2, R, R, P])
        outT = sb("outT", [P, N])
        rowsum, rinv = sb("rowsum", [P, G, R, heads]), sb("rinv", [P, R, heads])
        att = sb("att", [P, 2, N])
        neg, eneg = sb("neg", [P, N]), sb("eneg", [P, N])
        mask = sb("mask", [P, 2, R * N], BF16)
        if bias is not None:
            bias_col, bias_row = sb("bias_col", [P, 1]), sb("bias_row", [P, R, D])
        if load:
            adj_in, nm_sb = sb("adj_in", [P, 2, R, N], I32), sb("nm", [P, B * R])

        ps_xT, ps_wh = pb("ps_xT"), pb("ps_wh")
        ps_outT = [pb(f"ps_outT{i}") for i in range(2)]
        ps_z = [pb(f"ps_z{i}") for i in range(2)]
        ps_pT = [pb(f"ps_pT{i}") for i in range(2)]

        w_loaded, wa_done, wa_copied, consts = [sem(n) for n in ("w_loaded", "wa_done", "wa_copied", "consts")]
        stats_ready, rstd_ready, xn_ready = sem("stats_ready"), sem("rstd_ready"), sem("xn_ready")
        xT_ready, xT_copied, wh_ready, wh_copied = [sem(n) for n in ("xT_ready", "xT_copied", "wh_ready", "wh_copied")]
        rows_ready, rows_split, sides_ready = sem("rows_ready"), sem("rows_split"), sem("sides_ready")
        z_ready, scored, leaky_done, top_ready = sem("z_ready"), sem("scored"), sem("leaky_done"), sem("top_ready")
        prob_ready, pT_ready, pT_copied, out_done = [sem(n) for n in ("prob_ready", "pT_ready", "pT_copied", "out_done")]
        outT_copied, back_ready = sem("outT_copied"), sem("back_ready")
        out_used, neg_ready, eneg_ready, att_ready, x_done = [
            sem(n) for n in ("out_used", "neg_ready", "eneg_ready", "att_ready", "x_done")]
        dve_chain, pool_chain = sem("dve_chain"), sem("pool_chain")
        if load:
            x_loaded, adj_loaded = [sem("x_loaded0"), sem("x_loaded1")], [sem("adj_loaded0"), sem("adj_loaded1")]
            mask_done, mask_stored = sem("mask_done"), [sem("mask_stored0"), sem("mask_stored1")]
        else:
            mask_loaded = [sem("mask_loaded0"), sem("mask_loaded1")]

        def tile_at(turn, g, k, ahead):
            turns, rest = divmod(g * T + k + ahead, G * T)
            if isinstance(turn, int) and not 0 <= turn + turns < TURNS:
                return None
            return turn + turns, rest // T, rest % T // R, rest % R

        def graph_at(turn, g, k, ahead):
            t = tile_at(turn, g, k, ahead)
            return t[:2] if t and t[2:] == (0, 0) else None

        def tile_number(turn, g, h, r):
            return (G * turn + g) * T + h * R + r

        def walk(eng, step):
            before = -(-STATS_AT // T)
            for k in range(-before * T, 0):
                step(0, 0, k)
            for k in range(G * T):
                step(0, k // T, k % T)
            with eng.Fori(1, TURNS - 1) as turn:
                for k in range(G * T):
                    step(turn, k // T, k % T)
            for k in range(G * T):
                step(TURNS - 1, k // T, k % T)
            for k in range(TAIL - T + 1):
                step(TURNS, 0, k)

        block = ctx.enter_context(nc.Block())

        @block.sync
        def _(sp):
            if load:
                x_in, adj, nm = load
                x_v = x_in.rearrange("b (r p) d -> p (b r) d", p=P)
                adj_v = adj.rearrange("b (r p) j -> p (b r) j", p=P)
                sp.dma_start(X[:, 0:2 * N].rearrange("p (t d) -> p t d", d=D), x_v[:, 0:2 * R, :]).then_inc(x_loaded[0], 16)
            sp.dma_start(w_sb[:, :], w).then_inc(w_loaded, 16)
            sp.dma_start(wt_sb[:, :], wt).then_inc(w_loaded, 16)
            sp.dma_start(a_sb[:, :], a_pad).then_inc(w_loaded, 16)
            if bias is not None:
                sp.dma_start(bias_col[:, :], bias.rearrange("(p o) -> p o", o=1)).then_inc(w_loaded, 16)
                for r in range(R):
                    sp.dma_start(bias_row[:, r, :], bias.partition_broadcast(P)).then_inc(w_loaded, 16)
            if load:
                sp.dma_start(nm_sb[:, :], nm).then_inc(w_loaded, 16)

                def load_adj(pair, half):
                    wait(sp, mask_done, 2 * pair + half - 1)
                    sp.dma_start(adj_in[:, half, :, :], adj_v[:, bass.ds((2 * pair + half) * R, R), :])\
                      .then_inc(adj_loaded[half], 16)

                def store_mask(pair, half):
                    b = 2 * pair + half
                    sp.wait_ge(mask_done, b + 1)
                    sp.dma_start(mask_dram[bass.ds(b, 1)].rearrange("b p n -> p (b n)"), mask[:, half, :])\
                      .then_inc(mask_stored[half], 16)

                load_adj(0, 0)
                load_adj(0, 1)
                sp.dma_start(X[:, 2 * N:B * N].rearrange("p (t d) -> p t d", d=D), x_v[:, 2 * R:, :]).then_inc(x_loaded[1], 16)
                with sp.Fori(1, PAIRS) as pair:
                    for half in range(2):
                        store_mask(pair - 1, half)
                        load_adj(pair, half)
                for half in range(2):
                    store_mask(PAIRS - 1, half)
                for half in range(2):
                    sp.wait_ge(mask_stored[half], 16 * PAIRS)
            else:
                def load_mask(pair, half):
                    wait(sp, scored, (2 * pair + half - 1) * T)
                    sp.dma_start(mask[:, half, :], mask_dram[bass.ds(2 * pair + half, 1)].rearrange("b p n -> p (b n)"))\
                      .then_inc(mask_loaded[half], 16)

                load_mask(0, 0)
                load_mask(0, 1)
                with sp.Fori(1, PAIRS) as pair:
                    load_mask(pair, 0)
                    load_mask(pair, 1)

        n_loads = 16 * (3 + (1 + R if bias is not None else 0) + (1 if load else 0))

        @block.gpsimd
        def _(pool):
            def rstd_of(turn, g):
                b = G * turn + g
                pool.wait_ge(stats_ready, b + 1)
                nc.gpsimd.tensor_tensor(rstd[:, g % 2, :], aggr[:, g % 2, :, 1], env["eps"][:, :], ALU.add)\
                  .then_inc(pool_chain, 1)
                pool.wait_ge(pool_chain, b + 1)
                nc.gpsimd.tensor_tensor(rstd[:, g % 2, :], rstd[:, g % 2, :], env["minus_half"][:, :], ALU.pow)\
                  .then_inc(rstd_ready, 1)

            def sides(turn, g):
                b = G * turn + g
                pool.wait_ge(rows_split, 3 * b + 3)
                alone(pool, env["pool_passed"])
                wait(pool, z_ready, (b - 1) * T)
                alone(pool, env["pool_passed"])
                for h in range(heads):
                    nc.gpsimd.tensor_scalar(lhs[:, g % 2, h, :], rows[:, :].bitcast(F32), head_lo[:, h:h + 1], head_hi[:, h:h + 1],
                                            ALU.mult, ALU.add)
                nc.gpsimd.tensor_scalar(rhs[:, g % 2, :], rows[:, :].bitcast(F32), row_hi[:, :], row_lo[:, :], ALU.mult, ALU.add)\
                    .then_inc(sides_ready, 1)

            def residual(turn, g):
                b = G * turn + g
                pool.wait_ge(out_used if bias is None else att_ready, b + 1)
                alone(pool, env["pool_passed"])
                nc.gpsimd.tensor_tensor(X[:, bass.ts(b, N)], X[:, bass.ts(b, N)], att[:, g % 2, :], ALU.add)\
                    .then_inc(x_done, 1)

            nc.gpsimd.memset(row_lo[0:64, :], 1.0)
            nc.gpsimd.memset(row_lo[64:P, :], 0.0)
            nc.gpsimd.memset(row_hi[0:64, :], 0.0)
            nc.gpsimd.memset(row_hi[64:P, :], 1.0)
            nc.gpsimd.memset(head_hi[0:64, :], 0.0)
            nc.gpsimd.memset(head_lo[64:P, :], 0.0).then_inc(consts, 1)
            pool.wait_ge(consts, 1)
            nc.gpsimd.tensor_tensor(head_lo[0:64, :], ident[0:64, 0:heads], ident[0:64, 32:32 + heads], ALU.add)
            nc.gpsimd.tensor_tensor(head_hi[64:P, :], ident[64:P, 64:64 + heads], ident[64:P, 96:96 + heads], ALU.add)\
                .then_inc(consts, 1)
            pool.wait_ge(consts, 2)

            def step(turn, g, k):
                if b := graph_at(turn, g, k, STATS_AT):
                    rstd_of(*b)
                if b := graph_at(turn, g, k, SIDES_AT):
                    sides(*b)
                if not elu and (b := graph_at(turn, g, k, UPDATE_AT)):
                    residual(*b)
            walk(pool, step)

        @block.scalar
        def _(act):
            def copy_xT(turn, g):
                act.wait_ge(xT_ready, G * turn + g + 1)
                nc.scalar.copy(xT[:, g, :], ps_xT[:, :]).then_inc(xT_copied, 1)

            def copy_wh(turn, g):
                b = G * turn + g
                act.wait_ge(wh_ready, b + 1)
                wait(act, out_done, (b - 1) * T)
                nc.scalar.copy(wh[:, g % 2, :, :].rearrange("p r d -> p (r d)"), ps_wh[:, :]).then_inc(wh_copied, 1)

            def copy_outT(turn, g):
                b = G * turn + g
                act.wait_ge(out_done, (b + 1) * T)
                wait(act, back_ready, b)
                nc.scalar.copy(outT[:, :], ps_outT[g % 2][:, :]).then_inc(outT_copied, 1)

            def exp(turn, g, h, r):
                n = tile_number(turn, g, h, r)
                if r == 0:
                    act.wait_ge(top_ready, (G * turn + g) * heads + h + 1)
                wait(act, pT_ready, n - R + 1)
                if h == 0 and r == 0:
                    wait(act, out_used, G * turn + g - G + 1)
                nc.scalar.activation(prob[:, r, :], score[:, (g * heads + h) % 2, r, :], ACT.Exp,
                                     bias=neg_top[:, (g * heads + h) % 2, r:r + 1],
                                     accum_out=rowsum[:, g, r, h:h + 1]).then_inc(prob_ready, 1)

            def copy_pT(turn, g, h, r):
                n = tile_number(turn, g, h, r)
                act.wait_ge(pT_ready, n + 1)
                if r == 0:
                    wait(act, out_done, n - R)
                nc.scalar.copy(probT[:, (g * heads + h) % 2, :, r, :], ps_pT[r % 2][:, :].rearrange("p (c i) -> p c i", c=R))\
                    .then_inc(pT_copied, 1)

            def elu_exp(turn, g):
                act.wait_ge(neg_ready, G * turn + g + 1)
                nc.scalar.activation(eneg[:, :], neg[:, :], ACT.Exp).then_inc(eneg_ready, 1)

            act.wait_ge(wa_done, 1)
            nc.scalar.copy(wa[:, :], ps_wh[:, 0:P]).then_inc(wa_copied, 1)
            nc.scalar.copy(st_const[:, :], ps_wh[:, P:P + 1]).then_inc(wa_copied, 1)

            def step(turn, g, k):
                if b := graph_at(turn, g, k, XT_AT):
                    copy_xT(*b)
                if t := tile_at(turn, g, k, 0):
                    exp(*t)
                if b := graph_at(turn, g, k, COPY_WH_AT):
                    copy_wh(*b)
                if b := graph_at(turn, g, k, OUT_AT):
                    copy_outT(*b)
                if t := tile_at(turn, g, k, COPY_AT):
                    copy_pT(*t)
                if elu and (b := graph_at(turn, g, k, ELU_AT)):
                    elu_exp(*b)
            walk(act, step)

        @block.vector
        def _(dve):
            def graph_stats(turn, g):
                b = G * turn + g
                wait(dve, xn_ready, b - 1)
                if load:
                    dve.wait_ge(x_loaded[0], 16)
                    if not (isinstance(turn, int) and turn == 0 and g < 2):
                        dve.wait_ge(x_loaded[1], 16)
                for r in range(R):
                    ins = nc.vector.bn_stats(stats[:, g % 2, r, :], X[:, bass.ds(b * N + r * D, D)])
                ins.then_inc(dve_chain, 1)
                dve.wait_ge(dve_chain, b + 1)
                alone(dve, env["dve_passed"])
                for r in range(R):
                    ins = nc.vector.bn_aggr(aggr[:, g % 2, r, :], stats[:, g % 2, r, :])
                ins.then_inc(stats_ready, 1)

            def normalize(turn, g):
                b = G * turn + g
                dve.wait_ge(rstd_ready, b + 1)
                wait(dve, xT_ready, b - 1)
                for r in range(R):
                    ins = nc.vector.tensor_scalar(xn[:, g % 2, r, :], X[:, bass.ds(b * N + r * D, D)],
                                                  aggr[:, g % 2, r, 0:1], rstd[:, g % 2, r:r + 1], ALU.subtract, ALU.mult)
                ins.then_inc(xn_ready, 1)

            def make_mask(turn, g):
                before = G // 2 * turn + g // 2
                dve.wait_ge(adj_loaded[g % 2], 16 * (before + 1))
                wait(dve, mask_stored[g % 2], 16 * before)
                nc.vector.tensor_scalar(mask[:, g % 2, :], adj_in[:, g % 2, :, :].rearrange("p r j -> p (r j)"),
                                        0.0, MASKED, ALU.is_le, ALU.mult).then_inc(mask_done, 1)

            def split_rows(turn, g):
                b = G * turn + g
                dve.wait_ge(rows_ready, b + 1)
                wait(dve, sides_ready, b)
                nc.vector.tensor_scalar(rows[:, :], ps_xT[:, :], st_const[:, :], None, ALU.add).then_inc(rows_split, 1)
                dve.wait_ge(rows_split, 3 * b + 1)
                for q in (32, 96):
                    nc.vector.scalar_tensor_tensor(rows[q:q + 32, :], ps_xT[q:q + 32, :], st_const[q:q + 32, :],
                                                   rows[q:q + 32, :].bitcast(F32), ALU.add, ALU.subtract)\
                        .then_inc(rows_split, 1)

            def scores(turn, g, h, r):
                n = tile_number(turn, g, h, r)
                dve.wait_ge(z_ready, n + 1)
                if h == 0 and r == 0:
                    if load:
                        dve.wait_ge(mask_done, G * turn + g + 1)
                    else:
                        dve.wait_ge(mask_loaded[g % 2], 16 * (G // 2 * turn + g // 2 + 1))
                wait(dve, prob_ready, n - 2 * R + 1)
                alone(dve, env["dve_passed"])
                u2 = (g * heads + h) % 2
                nc.vector.tensor_tensor_reduce(out=score[:, u2, r, :], in0=ps_z[r % 2][:, :],
                                               in1=mask[:, g % 2, r * N:(r + 1) * N],
                                               scale=1.0, scalar=-3.0e38, op0=ALU.add, op1=ALU.max,
                                               accum_out=z_max[:, u2, r:r + 1]).then_inc(scored, 1)

            def leaky(turn, g, h, r):
                n = tile_number(turn, g, h, r)
                u2 = (g * heads + h) % 2
                dve.wait_ge(scored, n + 1)
                nc.vector.scalar_tensor_tensor(score[:, u2, r, :], score[:, u2, r, :], SLOPE, score[:, u2, r, :],
                                               ALU.mult, ALU.max).then_inc(leaky_done, 1)

            def top(turn, g, h):
                u = (G * turn + g) * heads + h
                u2 = (g * heads + h) % 2
                nc.vector.tensor_scalar(z_low[:, :], z_max[:, u2, :], -SLOPE, None, ALU.mult).then_inc(leaky_done, 1)
                dve.wait_ge(leaky_done, (u + 1) * (R + 1))
                nc.vector.scalar_tensor_tensor(neg_top[:, u2, :], z_max[:, u2, :], -1.0, z_low[:, :], ALU.mult, ALU.min)\
                    .then_inc(top_ready, 1)

            def finish(turn, g):
                b = G * turn + g
                dve.wait_ge(prob_ready, (b + 1) * T)
                nc.vector.reciprocal(rinv[:, :, :], rowsum[:, g, :, :]).then_inc(finish_chain, 1)
                dve.wait_ge(finish_chain, links * b + 1)
                if node_mask is not None:
                    nc.vector.tensor_tensor(rinv[:, :, 0], rinv[:, :, 0], nm_sb[:, bass.ds(b * R, R)], ALU.mult)\
                        .then_inc(finish_chain, 1)
                    dve.wait_ge(finish_chain, links * b + 2)
                dve.wait_ge(back_ready, b + 1)
                if not elu:
                    wait(dve, x_done, b - 1)
                nc.vector.tensor_tensor(att[:, g % 2, :].rearrange("p (r h c) -> p r h c", r=R, h=heads),
                                        ps_wh[:, :].rearrange("p (r h c) -> p r h c", r=R, h=heads),
                                        rinv[:, :, :].unsqueeze(3).to_broadcast([P, R, heads, C]), ALU.mult)\
                    .then_inc(out_used, 1)
                dve.wait_ge(out_used, b + 1)
                if elu:
                    wait(dve, eneg_ready, b)
                    nc.vector.tensor_scalar(neg[:, :], att[:, g % 2, :], 0.0, None, ALU.min).then_inc(neg_ready, 1)
                elif bias is not None:
                    nc.vector.tensor_tensor(att[:, g % 2, :], att[:, g % 2, :], bias_row[:, :, :].rearrange("p r d -> p (r d)"),
                                            ALU.add).then_inc(att_ready, 1)

            def elu_update(turn, g):
                b = G * turn + g
                dve.wait_ge(eneg_ready, b + 1)
                nc.vector.scalar_tensor_tensor(att[:, g % 2, :], att[:, g % 2, :], 0.0, eneg[:, :], ALU.max, ALU.add)\
                    .then_inc(att_ready, 1)
                dve.wait_ge(att_ready, b + 1)
                nc.vector.scalar_tensor_tensor(X[:, bass.ts(b, N)], att[:, g % 2, :], -1.0, X[:, bass.ts(b, N)],
                                               ALU.add, ALU.add).then_inc(x_done, 1)

            finish_chain = sem("finish_chain")
            links = 2 if node_mask is not None else 1
            dve.wait_ge(w_loaded, n_loads)
            dve.wait_ge(wa_copied, 2)

            def step(turn, g, k):
                if b := graph_at(turn, g, k, STATS_AT):
                    graph_stats(*b)
                if t := tile_at(turn, g, k, SCORE_AT):
                    scores(*t)
                if b := graph_at(turn, g, k, NORM_AT):
                    normalize(*b)
                if load and (b := graph_at(turn, g, k, MASK_AT)):
                    make_mask(*b)
                if t := tile_at(turn, g, k, LEAKY_AT):
                    leaky(*t)
                    if t[3] == R - 1:
                        top(*t[:3])
                if b := graph_at(turn, g, k, SPLIT_AT):
                    split_rows(*b)
                if b := graph_at(turn, g, k, FINISH_AT):
                    finish(*b)
                if elu and (b := graph_at(turn, g, k, UPDATE_AT)):
                    elu_update(*b)
            walk(dve, step)
            dve.wait_ge(x_done, B)

        @block.tensor
        def _(pe):
            def transpose_x(turn, g):
                b = G * turn + g
                pe.wait_ge(xn_ready, b + 1)
                wait(pe, rows_split, 3 * b)
                for r in range(R):
                    ins = nc.tensor.transpose(ps_xT[:, r * P:(r + 1) * P], xn[:, g % 2, r, :], ident[:, :])
                ins.then_inc(xT_ready, 1)

            def rows_of(turn, g):
                b = G * turn + g
                pe.wait_ge(xT_copied, b + 1)
                nc.tensor.matmul(ps_xT[:, :], wa[:, :], xT[:, g, :], start=True, stop=True).then_inc(rows_ready, 1)

            def wh_of(turn, g):
                b = G * turn + g
                wait(pe, out_used, b - LAG + 1)
                for r in range(R):
                    ins = nc.tensor.matmul(ps_wh[:, r * P:(r + 1) * P], xT[:, g, r * P:(r + 1) * P], w_sb[:, :],
                                           start=True, stop=True)
                ins.then_inc(wh_ready, 1)

            def z_of(turn, g, h, r):
                n = tile_number(turn, g, h, r)
                if h == 0 and r == 0:
                    pe.wait_ge(sides_ready, G * turn + g + 1)
                wait(pe, scored, n - 1)
                nc.tensor.matmul(ps_z[r % 2][:, :], lhs[:, g % 2, h, r * P:(r + 1) * P], rhs[:, g % 2, :],
                                 start=True, stop=True).then_inc(z_ready, 1)

            def transpose_probs(turn, g, h, r):
                n = tile_number(turn, g, h, r)
                pe.wait_ge(prob_ready, n + 1)
                wait(pe, pT_copied, n - 1)
                for c in range(R):
                    ins = nc.tensor.transpose(ps_pT[r % 2][:, c * P:(c + 1) * P], prob[:, r, c * P:(c + 1) * P], ident[:, :])
                ins.then_inc(pT_ready, 1)

            def attend(turn, g, h, c):
                n = tile_number(turn, g, h, c)
                if h == 0 and c == 0:
                    wait(pe, outT_copied, G * turn + g - 1)
                    pe.wait_ge(wh_copied, G * turn + g + 1)
                if c == 0:
                    pe.wait_ge(pT_copied, n + R)
                nc.tensor.matmul(ps_outT[g % 2][h * C:(h + 1) * C, :], wh[:, g % 2, c, h * C:(h + 1) * C],
                                 probT[:, (g * heads + h) % 2, c, :, :].rearrange("p r i -> p (r i)"),
                                 start=c == 0, stop=c == R - 1).then_inc(out_done, 1)

            def turn_back(turn, g):
                b = G * turn + g
                pe.wait_ge(outT_copied, b + 1)
                wait(pe, out_used, b)
                copied = b + LAG
                pe.wait_ge(wh_copied, min(B, copied) if isinstance(copied, int) else copied)
                for r in range(R):
                    ins = nc.tensor.transpose(ps_wh[:, r * P:(r + 1) * P], outT[:, r * P:(r + 1) * P], ident[:, :])
                ins.then_inc(back_ready, 1)

            pe.wait_ge(w_loaded, n_loads)
            nc.tensor.matmul(ps_wh[:, 0:P], wt_sb[:, :], a_sb[:, :], start=True, stop=True)
            nc.tensor.matmul(ps_wh[:, P:P + 1], a_sb[:, :], bias_col[:, :] if bias is not None else a_sb[:, P - 1:P],
                             start=True, stop=True).then_inc(wa_done, 1)
            pe.wait_ge(wa_copied, 2)
            pe.wait_ge(consts, 2)

            def step(turn, g, k):
                if t := tile_at(turn, g, k, Z_AT):
                    z_of(*t)
                if b := graph_at(turn, g, k, ROWS_AT):
                    rows_of(*b)
                if t := tile_at(turn, g, k, ATTEND_AT):
                    attend(*t)
                if b := graph_at(turn, g, k, WH_AT):
                    wh_of(*b)
                if b := graph_at(turn, g, k, XT_AT):
                    transpose_x(*b)
                if b := graph_at(turn, g, k, BACK_AT):
                    turn_back(*b)
                if t := tile_at(turn, g, k, TRANS_AT):
                    transpose_probs(*t)
            walk(pe, step)


def moe_layer(nc, env, name, w1, b1, w2, b2, router, router_bias, hidden, keep_tokens=False, own_ln=None, split_h=True):
    X, ident = env["X"], env["ident"]
    HC = hidden // P
    NG = E * HC
    LAG = 4 if split_h else 2
    LATE = LAG + 1
    unit = NG // 8
    S_TRANSPOSE, S_LOGITS, S_TOP, S_TANH, S_COMBINE_W, S_COMB_T, S_COMB_SPLIT = [unit * k for k in range(7)]
    S_OUT = LATE + 2
    S_UPDATE = S_OUT + 1
    S_STATS, S_NORM, S_NORM2 = unit + 1, 5 * unit, 7 * unit
    Hs = F32R if split_h else F32
    HB, HR = (4, 8) if split_h else (4, 4)
    ctx = ExitStack()
    with ctx:
        def sb(n, shape, dt=F32):
            return ctx.enter_context(nc.sbuf_tensor(f"{name}_{n}", shape, dt))

        def pb(n):
            return ctx.enter_context(nc.psum_tensor(f"{name}_{n}", [P, 512], F32))

        sem = layer_semaphores(nc, ctx, name)

        w1h, w1l = sb("w1h", [P, E, hidden], F32R), sb("w1l", [P, E, hidden], F32R)
        w2h = sb("w2h", [P, E, HC, D], Hs)
        w2l = sb("w2l", [P, E, HC, D], F32R) if split_h else None
        b1_sb, b2_sb, wr_sb = sb("b1", [P, NG]), sb("b2", [P, E]), sb("wr", [P, E])
        iota = sb("iota", [P, R, E])
        sel = sb("sel", [64, E], F32R)
        comb_T = sb("comb_T", [64, 2, N], F32R)
        if router_bias is not None:
            rb_sb = sb("rb", [P, R, E])

        with ExitStack() as setup:
            def ssb(n, shape, dt=F32):
                return setup.enter_context(nc.sbuf_tensor(f"{name}_{n}", shape, dt))

            stage = ssb("stage", [P, 2, hidden])
            zero64 = ssb("zero64", [64, 2 * N])
            if own_ln:
                g_sb, lnb_sb = ssb("g", [P, E]), ssb("lnb", [P, E])
                ps_b = setup.enter_context(nc.psum_tensor(f"{name}_ps_b", [P, 512], F32))
            small_loaded, staged = sem("small_loaded"), [sem("staged0"), sem("staged1")]
            split_done, scaled, bias_mm, zeroed, w2_high = [sem(n) for n in ("w_split", "scaled", "bias_mm", "zeroed", "w2_high")]
            with nc.Block() as block:
                small = [(b1_sb[:, :], b1), (b2_sb[:, :], b2), (wr_sb[:, :], router)]
                if router_bias is not None:
                    small += [(rb_sb[:, r, :], router_bias.partition_broadcast(P)) for r in range(R)]
                if own_ln:
                    small += [(g_sb[:, :], own_ln[0]), (lnb_sb[:, :], own_ln[1])]

                @block.sync
                def _(sp):
                    for dst, src in small:
                        sp.dma_start(dst, src).then_inc(small_loaded, 16)
                    for e in range(E):
                        wait(sp, split_done, 2 * e - 1)
                        sp.dma_start(stage[:, 0, :], w1[e]).then_inc(staged[0], 16)
                        wait(sp, split_done, 2 * e)
                        sp.dma_start(stage[:, 1, :].rearrange("p (c d) -> p c d", d=D),
                                     w2[e].rearrange("(c p) d -> p c d", p=P)).then_inc(staged[1], 16)

                @block.gpsimd
                def _(pool):
                    nc.gpsimd.iota(iota[:, :, :], pattern=[[0, R], [1, E]], base=0, channel_multiplier=0,
                                   allow_small_or_imprecise_dtypes=True)
                    nc.gpsimd.memset(zero64[:, :], 0.0).then_inc(zeroed, 1)

                @block.vector
                def _(dve):
                    dve.wait_ge(small_loaded, 16 * len(small))
                    dve.wait_ge(zeroed, 1)
                    nc.vector.tensor_copy(comb_T[:, :, :].rearrange("k h n -> k (h n)"), zero64[:, :])
                    nc.vector.tensor_tensor(sel[:, :], ident[0:64, 0:E], ident[0:64, 32:32 + E], ALU.add)
                    for e in range(E):
                        dve.wait_ge(staged[0], 16 * (e + 1))
                        if own_ln:
                            dve.wait_ge(bias_mm, e + 1)
                            nc.vector.tensor_scalar(stage[:, 0, :], stage[:, 0, :], g_sb[:, e:e + 1], None, ALU.mult)\
                              .then_inc(scaled, 1)
                            dve.wait_ge(scaled, 2 * e + 1)
                        nc.vector.tensor_copy(w1h[:, e, :], stage[:, 0, :]).then_inc(scaled, 1)
                        dve.wait_ge(scaled, (2 * e + 2) if own_ln else (e + 1))
                        nc.vector.tensor_tensor(w1l[:, e, :], stage[:, 0, :], w1h[:, e, :].bitcast(F32), ALU.subtract)\
                          .then_inc(split_done, 1)
                        dve.wait_ge(staged[1], 16 * (e + 1))
                        w2v = w2h[:, e, :, :].rearrange("p c d -> p (c d)")
                        if split_h:
                            nc.vector.tensor_copy(w2v, stage[:, 1, :]).then_inc(w2_high, 1)
                            dve.wait_ge(w2_high, e + 1)
                            nc.vector.tensor_tensor(w2l[:, e, :, :].rearrange("p c d -> p (c d)"), stage[:, 1, :],
                                                    w2v.bitcast(F32), ALU.subtract).then_inc(split_done, 1)
                        else:
                            nc.vector.tensor_copy(w2v, stage[:, 1, :]).then_inc(split_done, 1)
                    if own_ln:
                        nc.vector.tensor_tensor(b1_sb[:, :], b1_sb[:, :], ps_b[:, 0:NG], ALU.add)

                if own_ln:
                    @block.tensor
                    def _(pe):
                        pe.wait_ge(small_loaded, 16 * len(small))
                        for e in range(E):
                            pe.wait_ge(staged[0], 16 * (e + 1))
                            for c in range(HC):
                                ins = nc.tensor.matmul(ps_b[:, e * HC + c:e * HC + c + 1],
                                                       stage[:, 0, c * P:(c + 1) * P], lnb_sb[:, e:e + 1],
                                                       start=True, stop=True)
                            ins.then_inc(bias_mm, 1)

        stats, aggr, rstd = sb("stats", [P, 2, R, 6]), sb("aggr", [P, 2, R, 2]), sb("rstd", [P, 2, R])
        xn = sb("xn", [P, 2, R, P])
        xT = sb("xT", [P, N])
        if own_ln:
            stats2, aggr2, rstd2 = sb("stats2", [P, R, 6]), sb("aggr2", [P, R, 2]), sb("rstd2", [P, R])
            xn2 = sb("xn2", [P, 2, R, P])
            xT2 = sb("xT2", [P, N])
        xe = xT2 if own_ln else xT
        xh, xl = sb("xh", [P, 2, N], F32R), sb("xl", [P, 2, N], F32R)
        logit, best, best_at = sb("logit", [P, R, E]), sb("best", [P, R, E]), sb("best_at", [P, R, E], U32)
        at_f = sb("at_f", [P, R, 2])
        gap, tanh_gap = sb("gap", [P, R]), sb("tanh_gap", [P, R])
        weight = sb("weight", [P, 2, R])
        hot = sb("hot", [P, 2, R, E])
        comb = sb("comb", [P, R, E])
        h = sb("h", [P, HB, N])
        hh = sb("hh", [P, HR, N], F32R) if split_h else None
        hl = sb("hl", [P, HR, N], F32R) if split_h else None
        w_rows = sb("w_rows", [P, 2, N])
        scaled_y = sb("scaled_y", [P, 2, N])
        acc = sb("acc", [P, 2, N])

        ps_h = [pb(f"ps_h{i}") for i in range(2)]
        ps_y = [pb(f"ps_y{i}") for i in range(2)]
        ps_w, ps_xT, ps_small, ps_out = pb("ps_w"), pb("ps_xT"), pb("ps_small"), pb("ps_out")

        high_done = sem("high_done")
        stats_ready, rstd_ready, xn_ready = sem("stats_ready"), sem("rstd_ready"), sem("xn_ready")
        stats2_ready, rstd2_ready, xn2_ready = sem("stats2_ready"), sem("rstd2_ready"), sem("xn2_ready")
        xT_ready, xT_copied = sem("xT_ready"), sem("xT_copied")
        x_split, logits_ready, gap_ready, tanh_ready = sem("x_split"), sem("logits_ready"), sem("gap_ready"), sem("tanh_ready")
        comb_ready, combT_ready, combT_split = sem("comb_ready"), sem("combT_ready"), sem("combT_split")
        h_ready, gelu_done, h_split, y_chunk = sem("h_ready"), sem("gelu_done"), sem("h_split"), sem("y_chunk")
        w_ready, w_copied, y_scaled, added = sem("w_ready"), sem("w_copied"), sem("y_scaled"), sem("added")
        out_ready, x_done = sem("out_ready"), sem("x_done")
        dve_chain, pool_chain = sem("dve_chain"), sem("pool_chain")

        def steps(pair, half):
            first = isinstance(pair, int) and pair == 0 and half == 0
            last = isinstance(pair, int) and pair == PAIRS - 1 and half == 1
            nxt = (pair, 1) if half == 0 else (pair + 1, 0)
            prev = (pair, 0) if half == 1 else (pair - 1, 1)
            return first, last, nxt, prev

        def in_static(half, g, lag):
            return (half * NG + g - lag) % (2 * NG)

        block = ctx.enter_context(nc.Block())

        @block.gpsimd
        def _(pool):
            chain = Chain(pool, pool_chain, 0)

            def rstd_of(pair, half):
                b = 2 * pair + half
                pool.wait_ge(stats_ready, b + 1)
                chain.link(nc.gpsimd.tensor_tensor(rstd[:, half, :], aggr[:, half, :, 1], env["eps"][:, :], ALU.add))
                nc.gpsimd.tensor_tensor(rstd[:, half, :], rstd[:, half, :], env["minus_half"][:, :], ALU.pow)\
                  .then_inc(rstd_ready, 1)

            def add_tokens(pair, half):
                if keep_tokens:
                    b = 2 * pair + half
                    pool.wait_ge(xn_ready, b + 1)
                    alone(pool, env["pool_passed"])
                    chain.link(nc.gpsimd.tensor_tensor(X[:, bass.ts(b, N)], X[:, bass.ts(b, N)],
                                                       xn[:, half, :, :].rearrange("p r d -> p (r d)"), ALU.add))

            def rstd2_of(pair, half):
                pool.wait_ge(stats2_ready, 2 * pair + half + 1)
                chain.link(nc.gpsimd.tensor_tensor(rstd2[:, :], aggr2[:, :, 1], env["eps"][:, :], ALU.add))
                nc.gpsimd.tensor_tensor(rstd2[:, :], rstd2[:, :], env["minus_half"][:, :], ALU.pow).then_inc(rstd2_ready, 1)

            def add_expert(pair, half, e):
                n = (2 * pair + half) * E + e
                pool.wait_ge(y_scaled, n + 1)
                if e == 0:
                    wait(pool, out_ready, 2 * pair + half - 1)
                    alone(pool, env["pool_passed"])
                    nc.gpsimd.tensor_copy(acc[:, half, :], scaled_y[:, e % 2, :]).then_inc(added, 1)
                else:
                    pool.wait_ge(added, n)
                    nc.gpsimd.tensor_tensor(acc[:, half, :], acc[:, half, :], scaled_y[:, e % 2, :], ALU.add)\
                      .then_inc(added, 1)

            for half in range(2):
                rstd_of(0, half)
            for half in range(2):
                add_tokens(0, half)
                if own_ln:
                    rstd2_of(0, half)
            chain.end_prologue()
            chain.per_pair = 2 + (2 if own_ln else 0) + (2 if keep_tokens else 0)

            def body(pair):
                last_pair = isinstance(pair, int) and pair == PAIRS - 1
                chain.pair(pair)
                for half in range(2):
                    first, last, nxt, prev = steps(pair, half)
                    for e in range(E):
                        add_expert(pair, half, e)
                        if e == 1 and not last_pair:
                            rstd_of(pair + 1, half)
                        if e == 4 and not last_pair:
                            add_tokens(pair + 1, half)
                            if own_ln:
                                rstd2_of(pair + 1, half)
                if not last_pair:
                    chain.end_pair()
            pairs(pool, body)

        @block.scalar
        def _(act):
            def front(pair, half):
                b = 2 * pair + half
                act.wait_ge(xT_ready, b + 1)
                wait(act, logits_ready, b)
                if not own_ln:
                    wait(act, x_split, b)
                nc.scalar.copy(xT[:, :], ps_xT[:, :]).then_inc(xT_copied, 1)
                if own_ln:
                    act.wait_ge(xT_ready, b + 1)
                    wait(act, x_split, b)
                    nc.scalar.copy(xT2[:, :], ps_out[:, :]).then_inc(xT_copied, 1)

            def gap_tanh(pair, half):
                act.wait_ge(gap_ready, 2 * pair + half + 1)
                nc.scalar.activation(tanh_gap[:, :], gap[:, :], ACT.Tanh, scale=0.5).then_inc(tanh_ready, 1)

            def gelu(pair, half, g):
                n = (2 * pair + half) * NG + g
                act.wait_ge(h_ready, n + 1)
                wait(act, h_split if split_h else y_chunk, n - HB + 1)
                nc.scalar.activation(h[:, g % HB, :], ps_h[g % 2][:, :], ACT.Gelu,
                                     bias=b1_sb[:, g:g + 1]).then_inc(gelu_done, 1)

            def copy_w(n, e):
                act.wait_ge(w_ready, n + 1)
                wait(act, y_scaled, n - 1)
                nc.scalar.copy(w_rows[:, e % 2, :], ps_w[:, :]).then_inc(w_copied, 1)

            front(0, 0)
            gap_tanh(0, 0)

            def body(pair):
                for half in range(2):
                    first, last, nxt, prev = steps(pair, half)
                    for g in range(NG):
                        gelu(pair, half, g)
                        if (g - LAG) % HC == 0 and not (first and g < LAG):
                            copy_w((2 * pair + half) * E + (g - LAG) // HC, (g - LAG) // HC)
                        if not last and g == S_TRANSPOSE:
                            front(*nxt)
                        if not last and g == S_TANH:
                            gap_tanh(*nxt)
            pairs(act, body)
            for g in range(LAG):
                if (g - LAG) % HC == 0:
                    copy_w(B * E + (g - LAG) // HC, (g - LAG) // HC)

        @block.vector
        def _(dve):
            chain = Chain(dve, dve_chain, 0)

            def graph_stats(pair, half):
                b = 2 * pair + half
                wait(dve, xn_ready, b - 1)
                for r in range(R):
                    ins = nc.vector.bn_stats(stats[:, half, r, :], X[:, bass.ds(b * N + r * D, D)])
                chain.link(ins)
                alone(dve, env["dve_passed"])
                for r in range(R):
                    ins = nc.vector.bn_aggr(aggr[:, half, r, :], stats[:, half, r, :])
                ins.then_inc(stats_ready, 1)

            def graph_stats2(pair, half):
                b = 2 * pair + half
                dve.wait_ge(xn_ready, b + 1)
                wait(dve, xn2_ready, b)
                for r in range(R):
                    ins = nc.vector.bn_stats(stats2[:, r, :], xn[:, half, r, :])
                chain.link(ins)
                alone(dve, env["dve_passed"])
                for r in range(R):
                    ins = nc.vector.bn_aggr(aggr2[:, r, :], stats2[:, r, :])
                ins.then_inc(stats2_ready, 1)

            def normalize(pair, half):
                b = 2 * pair + half
                dve.wait_ge(rstd_ready, b + 1)
                wait(dve, xT_ready, b - 1)
                for r in range(R):
                    ins = nc.vector.tensor_scalar(xn[:, half, r, :], X[:, bass.ds(b * N + r * D, D)],
                                                  aggr[:, half, r, 0:1], rstd[:, half, r:r + 1], ALU.subtract, ALU.mult)
                ins.then_inc(xn_ready, 1)

            def normalize2(pair, half):
                b = 2 * pair + half
                dve.wait_ge(rstd2_ready, b + 1)
                for r in range(R):
                    ins = nc.vector.tensor_scalar(xn2[:, half, r, :], xn[:, half, r, :],
                                                  aggr2[:, r, 0:1], rstd2[:, r:r + 1], ALU.subtract, ALU.mult)
                ins.then_inc(xn2_ready, 1)

            def split_x(pair, half):
                b = 2 * pair + half
                dve.wait_ge(xT_copied, (b + 1) * (2 if own_ln else 1))
                wait(dve, h_ready, (b - 1) * NG)
                chain.link(nc.vector.tensor_copy(xh[:, half, :], xe[:, :]))
                nc.vector.tensor_tensor(xl[:, half, :], xe[:, :], xh[:, half, :].bitcast(F32), ALU.subtract)\
                  .then_inc(x_split, 1)

            def top_two(pair, half):
                b = 2 * pair + half
                dve.wait_ge(logits_ready, b + 1)
                lv = logit[:, :, :].rearrange("p r e -> p (r e)")
                if router_bias is not None:
                    ins = nc.vector.tensor_tensor(lv, ps_small[:, 0:R * E], rb_sb[:, :, :].rearrange("p r e -> p (r e)"),
                                                  ALU.add)
                else:
                    ins = nc.vector.tensor_copy(lv, ps_small[:, 0:R * E])
                chain.link(ins)
                alone(dve, env["dve_passed"])
                for r in range(R):
                    ins = nc.vector.max(best[:, r, :], logit[:, r, :])
                chain.link(ins)
                alone(dve, env["dve_passed"])
                for r in range(R):
                    ins = nc.vector.max_index(best_at[:, r, :], best[:, r, :], logit[:, r, :])
                nc.vector.tensor_tensor(gap[:, :], best[:, :, 0], best[:, :, 1], ALU.subtract).then_inc(gap_ready, 1)

            def weights(pair, half):
                b = 2 * pair + half
                dve.wait_ge(gap_ready, b + 1)
                chain.link(nc.vector.tensor_copy(at_f[:, :, :], best_at[:, :, 0:2]))
                dve.wait_ge(tanh_ready, b + 1)
                nc.vector.tensor_scalar(weight[:, 0, :], tanh_gap[:, :], 0.5, 0.5, ALU.mult, ALU.add)
                nc.vector.tensor_scalar(weight[:, 1, :], tanh_gap[:, :], -0.5, 0.5, ALU.mult, ALU.add)
                for k in range(2):
                    ins = nc.vector.tensor_tensor(hot[:, k, :, :], iota[:, :, :],
                                                  at_f[:, :, k:k + 1].to_broadcast([P, R, E]), ALU.is_equal)
                chain.link(ins)
                for k in range(2):
                    ins = nc.vector.tensor_tensor(hot[:, k, :, :], hot[:, k, :, :],
                                                  weight[:, k, :].unsqueeze(2).to_broadcast([P, R, E]), ALU.mult)
                chain.link(ins)
                nc.vector.tensor_tensor(comb[:, :, :], hot[:, 0, :, :], hot[:, 1, :, :], ALU.add).then_inc(comb_ready, 1)

            def split_comb(pair, half):
                b = 2 * pair + half
                dve.wait_ge(combT_ready, b + 1)
                wait(dve, w_ready, (b - 1) * E)
                chain.link(nc.vector.tensor_copy(comb_T[0:E, half, :], ps_small[0:E, :]))
                nc.vector.tensor_tensor(comb_T[32:32 + E, half, :], ps_small[0:E, :], comb_T[0:E, half, :].bitcast(F32),
                                        ALU.subtract).then_inc(combT_split, 1)

            def high_part(pair, half, g):
                n = (2 * pair + half) * NG + g
                dve.wait_ge(gelu_done, n + 1)
                wait(dve, y_chunk, n - HR + 1)
                nc.vector.tensor_copy(hh[:, g % HR, :], h[:, g % HB, :]).then_inc(high_done, 1)

            def low_part(n, g):
                dve.wait_ge(high_done, n + 1)
                nc.vector.tensor_tensor(hl[:, g % HR, :], h[:, g % HB, :], hh[:, g % HR, :].bitcast(F32), ALU.subtract)\
                  .then_inc(h_split, 1)

            def combine(n, e):
                dve.wait_ge(y_chunk, (n + 1) * HC)
                dve.wait_ge(w_copied, n + 1)
                wait(dve, added, n - 1)
                nc.vector.scalar_tensor_tensor(scaled_y[:, e % 2, :], ps_y[e % 2][:, :], b2_sb[:, e:e + 1],
                                               w_rows[:, e % 2, :], ALU.add, ALU.mult).then_inc(y_scaled, 1)

            def update(pair, half):
                b = 2 * pair + half
                dve.wait_ge(out_ready, b + 1)
                nc.vector.tensor_tensor(X[:, bass.ts(b, N)], X[:, bass.ts(b, N)], ps_out[:, :], ALU.add)\
                  .then_inc(x_done, 1)

            graph_stats(0, 0)
            graph_stats(0, 1)
            for half in range(2):
                normalize(0, half)
                if own_ln:
                    graph_stats2(0, half)
                    normalize2(0, half)
            split_x(0, 0)
            top_two(0, 0)
            weights(0, 0)
            split_comb(0, 0)
            chain.end_prologue()
            chain.per_pair = 2 + (2 if own_ln else 0) + 2 * (1 + 2 + 3 + 1)

            def body(pair):
                last_pair = isinstance(pair, int) and pair == PAIRS - 1
                chain.pair(pair)
                for half in range(2):
                    first, last, nxt, prev = steps(pair, half)
                    for g in range(NG):
                        if split_h:
                            high_part(pair, half, g)
                            if not (first and g == 0):
                                low_part((2 * pair + half) * NG + g - 1, (g - 1) % NG)
                        else:
                            dve.wait_ge(gelu_done, (2 * pair + half) * NG + g + 1)
                        done = g - LATE + 1
                        if done % HC == 0 and not (first and done <= 0):
                            combine((2 * pair + half) * E + done // HC - 1, (done // HC - 1) % E)
                        if g == S_UPDATE and not first:
                            update(*prev)
                        if not last:
                            if g == S_TRANSPOSE:
                                split_x(*nxt)
                            if g == S_TOP:
                                top_two(*nxt)
                            if g == S_COMBINE_W:
                                weights(*nxt)
                            if g == S_COMB_SPLIT:
                                split_comb(*nxt)
                        if g == S_STATS and not last_pair:
                            graph_stats(pair + 1, half)
                        if g == S_NORM and not last_pair:
                            normalize(pair + 1, half)
                            if own_ln:
                                graph_stats2(pair + 1, half)
                        if g == S_NORM2 and own_ln and not last_pair:
                            normalize2(pair + 1, half)
                if not last_pair:
                    chain.end_pair()
            pairs(dve, body)
            if split_h:
                low_part(B * NG - 1, NG - 1)
            for done in range(NG - LATE + 1, NG + 1):
                if done % HC == 0:
                    combine((B - 1) * E + done // HC - 1, done // HC - 1)
            update(PAIRS - 1, 1)
            dve.wait_ge(x_done, B)

        @block.tensor
        def _(pe):
            def transposes(pair, half):
                b = 2 * pair + half
                pe.wait_ge(xn_ready, b + 1)
                for r in range(R):
                    ins = nc.tensor.transpose(ps_xT[:, r * P:(r + 1) * P], xn[:, half, r, :], ident[:, :])
                if own_ln:
                    pe.wait_ge(xn2_ready, b + 1)
                    wait(pe, x_done, b - 2)
                    for r in range(R):
                        ins = nc.tensor.transpose(ps_out[:, r * P:(r + 1) * P], xn2[:, half, r, :], ident[:, :])
                ins.then_inc(xT_ready, 1)

            def logits(pair, half):
                b = 2 * pair + half
                pe.wait_ge(xT_copied, (b + 1) * (2 if own_ln else 1))
                wait(pe, combT_split, b)
                for r in range(R):
                    ins = nc.tensor.matmul(ps_small[:, r * E:(r + 1) * E], xT[:, r * P:(r + 1) * P], wr_sb[:, :],
                                           start=True, stop=True)
                ins.then_inc(logits_ready, 1)

            def transpose_comb(pair, half):
                pe.wait_ge(comb_ready, 2 * pair + half + 1)
                for r in range(R):
                    ins = nc.tensor.transpose(ps_small[0:E, r * P:(r + 1) * P], comb[:, r, :], ident[:, :])
                ins.then_inc(combT_ready, 1)

            def first_product(pair, half, g):
                n = (2 * pair + half) * NG + g
                if g == 0:
                    pe.wait_ge(x_split, 2 * pair + half + 1)
                wait(pe, gelu_done, n - 1)
                e, c = g // HC, g % HC
                cols = slice(c * P, (c + 1) * P)
                nc.tensor.matmul(ps_h[g % 2][:, :], w1h[:, e, cols], xh[:, half, :], start=True, stop=False)
                nc.tensor.matmul(ps_h[g % 2][:, :], w1h[:, e, cols], xl[:, half, :], start=False, stop=False)
                nc.tensor.matmul(ps_h[g % 2][:, :], w1l[:, e, cols], xh[:, half, :], start=False, stop=True)\
                  .then_inc(h_ready, 1)

            def second_product(n, g, half):
                e, c = g // HC, g % HC
                slot = g % HR
                y = ps_y[e % 2]
                if split_h:
                    pe.wait_ge(h_split, n + 1)
                    nc.tensor.matmul(y[:, :], w2h[:, e, c, :], hh[:, slot, :], start=c == 0, stop=False)
                    nc.tensor.matmul(y[:, :], w2h[:, e, c, :], hl[:, slot, :], start=False, stop=False)
                    nc.tensor.matmul(y[:, :], w2l[:, e, c, :], hh[:, slot, :], start=False, stop=c == HC - 1)\
                      .then_inc(y_chunk, 1)
                else:
                    pe.wait_ge(gelu_done, n + 1)
                    nc.tensor.matmul(y[:, :], w2h[:, e, c, :], h[:, slot, :], start=c == 0, stop=c == HC - 1)\
                      .then_inc(y_chunk, 1)

            def lagged(pair, half, g):
                b = 2 * pair + half
                lg = g - LAG
                n = b * NG + lg
                if lg < 0:
                    lg, lb, lh = lg + NG, b - 1, 1 - half
                else:
                    lb, lh = b, half
                e = lg // HC
                if lg % HC == 0:
                    if e == 0:
                        pe.wait_ge(combT_split, lb + 1)
                    en = lb * E + e
                    wait(pe, w_copied, en)
                    nc.tensor.matmul(ps_w[:, :], sel[:, e:e + 1].to_broadcast([64, P]), comb_T[:, lh, :], start=True, stop=True)\
                      .then_inc(w_ready, 1)
                    wait(pe, y_scaled, en - 1)
                second_product(n, lg, lh)

            def transpose_out(pair, half):
                b = 2 * pair + half
                pe.wait_ge(added, (b + 1) * E)
                wait(pe, x_done, b)
                for r in range(R):
                    ins = nc.tensor.transpose(ps_out[:, r * P:(r + 1) * P], acc[:, half, r * P:(r + 1) * P], ident[:, :])
                ins.then_inc(out_ready, 1)

            transposes(0, 0)
            logits(0, 0)
            transpose_comb(0, 0)

            def body(pair):
                for half in range(2):
                    first, last, nxt, prev = steps(pair, half)
                    for g in range(NG):
                        first_product(pair, half, g)
                        if not (first and g < LAG):
                            lagged(pair, half, g)
                        if g == S_OUT and not first:
                            transpose_out(*prev)
                        if not last:
                            if g == S_TRANSPOSE:
                                transposes(*nxt)
                            if g == S_LOGITS:
                                logits(*nxt)
                            if g == S_COMB_T:
                                transpose_comb(*nxt)
            pairs(pe, body)
            for g in range(LAG):
                lagged(PAIRS, 0, g)
            transpose_out(PAIRS - 1, 1)


def mamba_layer(nc, env, name, w_in, conv_w, conv_b, dt_bias, a_log, d_skip, norm_w, w_out_t, w_lin, b_lin):
    X, ident = env["X"], env["ident"]
    INNER, STATE, HEADS, HEAD, TAPS = 256, 64, 4, 64, 4
    XBC = INNER + 2 * STATE
    CC = XBC // P
    RMS_EPS = 1e-5
    PAD = 4
    RH = R * HEADS
    ctx = ExitStack()
    with ctx:
        def sb(n, shape, dt=F32):
            return ctx.enter_context(nc.sbuf_tensor(f"{name}_{n}", shape, dt))

        def pb(n):
            return ctx.enter_context(nc.psum_tensor(f"{name}_{n}", [P, 512], F32))

        sem = layer_semaphores(nc, ctx, name)

        wch, wcl = sb("wch", [P, TAPS, XBC], F32R), sb("wcl", [P, TAPS, XBC], F32R)
        wz, wdt_sb = sb("wz", [P, INNER]), sb("wdt", [P, HEADS])
        wo = sb("wo", [P, 2, D])
        half_cb = sb("half_cb", [P, CC])
        dtb, a_neg = sb("dtb", [P, R, HEADS]), sb("a_neg", [P, R, HEADS])
        d_row = sb("d_row", [P, HEADS, HEAD])
        b_row = sb("b_row", [P, R, D])
        rms_eps = sb("rms_eps", [P, 1])
        ones, tri, strict = sb("ones", [P, P]), sb("tri", [P, P]), sb("strict", [P, P])
        xh, xl = sb("xh", [P, PAD + N], F32R), sb("xl", [P, PAD + N], F32R)

        with ExitStack() as setup:
            def ssb(n, shape, dt=F32):
                return setup.enter_context(nc.sbuf_tensor(f"{name}_{n}", shape, dt))

            w_xbc, cw_row, w_tap = ssb("w_xbc", [P, XBC]), ssb("cw_row", [P, TAPS, XBC]), ssb("w_tap", [P, TAPS, XBC])
            wot, wlin, nw = ssb("wot", [P, INNER]), ssb("wlin", [P, D]), ssb("nw", [P, 2])
            d_in, cb_in = ssb("d_in", [P, HEADS]), ssb("cb_in", [P, CC])
            zeros = ssb("zeros", [P, PAD])
            ps_w = setup.enter_context(nc.psum_tensor(f"{name}_ps_w", [P, 512], F32))
            loaded, masks, prep, wo_mm, a_exp = [sem(n) for n in ("loaded", "masks", "prep", "wo_mm", "a_exp")]
            loads = [(w_xbc[:, :], w_in[:, INNER:INNER + XBC]), (wz[:, :], w_in[:, 0:INNER]),
                     (wdt_sb[:, :], w_in[:, INNER + XBC:]), (wot[:, :], w_out_t), (wlin[:, :], w_lin),
                     (nw[:, :], norm_w), (cb_in[:, :], conv_b), (d_in[:, :], d_skip.partition_broadcast(P))]
            loads += [(cw_row[:, k, :], conv_w[k].partition_broadcast(P)) for k in range(TAPS)]
            for r in range(R):
                loads += [(dtb[:, r, :], dt_bias.partition_broadcast(P)), (a_neg[:, r, :], a_log.partition_broadcast(P)),
                          (b_row[:, r, :], b_lin.partition_broadcast(P))]
            with nc.Block() as block:
                @block.sync
                def _(sp):
                    for dst, src in loads:
                        sp.dma_start(dst, src).then_inc(loaded, 16)

                @block.gpsimd
                def _(pool):
                    nc.gpsimd.memset(zeros[:, :], 0.0)
                    nc.gpsimd.memset(rms_eps[:, :], RMS_EPS * INNER)
                    nc.gpsimd.memset(ones[:, :], 1.0).then_inc(masks, 1)
                    pool.wait_ge(masks, 1)
                    nc.gpsimd.affine_select(out=tri[:, :], in_=ones[:, :], compare_op=ALU.is_ge, fill=0.0,
                                            base=0, pattern=[[1, P]], channel_multiplier=-1).then_inc(masks, 1)

                @block.scalar
                def _(act):
                    act.wait_ge(loaded, 16 * len(loads))
                    nc.scalar.activation(a_neg[:, :, :], a_neg[:, :, :], ACT.Exp).then_inc(a_exp, 1)
                    nc.scalar.mul(half_cb[:, :], cb_in[:, :], 0.5)

                @block.tensor
                def _(pe):
                    pe.wait_ge(loaded, 16 * len(loads))
                    for k in range(2):
                        ins = nc.tensor.matmul(ps_w[:, k * D:(k + 1) * D], wot[:, k * P:(k + 1) * P], wlin[:, :],
                                               start=True, stop=True)
                    ins.then_inc(wo_mm, 1)

                @block.vector
                def _(dve):
                    dve.wait_ge(masks, 2)
                    nc.vector.tensor_tensor(strict[:, :], tri[:, :], ident[:, :], ALU.subtract)
                    nc.vector.tensor_copy(xh[:, 0:PAD], zeros[:, :])
                    nc.vector.tensor_copy(xl[:, 0:PAD], zeros[:, :])
                    dve.wait_ge(loaded, 16 * len(loads))
                    for k in range(TAPS):
                        ins = nc.vector.tensor_tensor(w_tap[:, k, :], w_xbc[:, :], cw_row[:, k, :], ALU.mult)
                    ins.then_inc(prep, 1)
                    dve.wait_ge(prep, 1)
                    nc.vector.tensor_copy(wch[:, :, :], w_tap[:, :, :]).then_inc(prep, 1)
                    dve.wait_ge(prep, 2)
                    nc.vector.tensor_tensor(wcl[:, :, :], w_tap[:, :, :], wch[:, :, :].bitcast(F32), ALU.subtract)
                    nc.vector.tensor_copy(d_row[:, :, :], d_in[:, :].unsqueeze(2).to_broadcast([P, HEADS, HEAD]))
                    dve.wait_ge(wo_mm, 1)
                    for k in range(2):
                        nc.vector.tensor_scalar(wo[:, k, :], ps_w[:, k * D:(k + 1) * D], nw[:, k:k + 1], float(INNER) ** 0.5,
                                                ALU.mult, ALU.mult)
                    dve.wait_ge(a_exp, 1)
                    nc.vector.tensor_scalar(a_neg[:, :, :], a_neg[:, :, :], -1.0, None, ALU.mult)

        stats, aggr, rstd = sb("stats", [P, 2, R, 6]), sb("aggr", [P, 2, R, 2]), sb("rstd", [P, 2, R])
        xn = sb("xn", [P, 2, R, P])
        xT = sb("xT", [P, N])
        th, hv = sb("th", [P, 2, N]), sb("hv", [P, 2, N])
        xc = sb("xc", [P, 2, 2, N])
        BT, CT = sb("BT", [STATE, 2, N]), sb("CT", [STATE, 2, N])
        zg = sb("zg", [P, 2, R, INNER])
        dt_raw, dt_abs, dt_exp, dt_ln = [sb(n, [P, RH]) for n in ("dt_raw", "dt_abs", "dt_exp", "dt_ln")]
        dt, dA = sb("dt", [P, 2, RH]), sb("dA", [P, 2, RH])
        acum, exp_acum = sb("acum", [P, 2, RH]), sb("exp_acum", [P, 2, RH])
        rest, exp_rest = sb("rest", [P, RH]), sb("exp_rest", [P, RH])
        exp_total, dt_rest = sb("exp_total", [P, 2, RH]), sb("dt_rest", [P, 2, RH])
        diff, ediff = sb("diff", [P, HEADS, P]), sb("ediff", [P, HEADS, P])
        cb_m = sb("cb_m", [P, P])
        mix = sb("mix", [P, 2, HEADS, P])
        xB = sb("xB", [P, 2, INNER + STATE])
        xdt, xrest, xD = sb("xdt", [P, 2, INNER]), sb("xrest", [P, 2, INNER]), sb("xD", [P, 2, INNER])
        state, decayed = sb("state", [STATE, INNER]), sb("decayed", [STATE, INNER])
        y_part, y, gated = sb("y_part", [P, INNER]), sb("y", [P, INNER]), sb("gated", [P, 2, INNER])
        squares = sb("squares", [P, INNER])
        sumsq, rms = sb("sumsq", [P, 2]), sb("rms", [P, 2])
        gT = sb("gT", [P, 2, INNER])
        minus_half1 = env["minus_half"][:, 0:1]

        ps_f = [pb("ps_f0"), pb("ps_f1")]
        ps_bc, ps_c1, ps_c2, ps_s, ps_small, ps_c3 = [pb(n) for n in ("ps_bc", "ps_c1", "ps_c2", "ps_s", "ps_small", "ps_c3")]

        (stats_ready, rstd_ready, xn_ready, f_ready, f_read, x_split, conv_act, silu_done, dtm_ready, dt_pre, dt_ln_done, dA_ready,
         cum_ready, cum_act, cum_dve, rest_exp, front_done, c1_ready, c1_copied, diff_ready, ediff_ready, mix_ready,
         c2_ready, state_done, decay_done, gated_ready, sq_done, rms_ready, gT_ready, gT_copied, o_ready, x_done, xD_ready,
         z_act, zg_ready, dve_chain, pool_chain) = [sem(n) for n in (
             "stats_ready rstd_ready xn_ready f_ready f_read x_split conv_act silu_done dtm_ready dt_pre dt_ln_done dA_ready "
             "cum_ready cum_act cum_dve rest_exp front_done c1_ready c1_copied diff_ready ediff_ready mix_ready "
             "c2_ready state_done decay_done gated_ready sq_done rms_ready gT_ready gT_copied o_ready x_done xD_ready "
             "z_act zg_ready dve_chain pool_chain").split()]
        FU = 1 + CC + 2

        block = ctx.enter_context(nc.Block())

        def schedule(body_of):
            def body(pair):
                for half in range(2):
                    first = isinstance(pair, int) and pair == 0 and half == 0
                    last = isinstance(pair, int) and pair == PAIRS - 1 and half == 1
                    nxt = (pair, 1) if half == 0 else (pair + 1, 0)
                    for r in range(R):
                        body_of(pair, half, r, first, last, nxt)
            return body

        @block.gpsimd
        def _(pool):
            chain = Chain(pool, pool_chain, 0)

            def rstd_of(pair, half):
                b = 2 * pair + half
                pool.wait_ge(stats_ready, b + 1)
                chain.link(nc.gpsimd.tensor_tensor(rstd[:, half, :], aggr[:, half, :, 1], env["eps"][:, :], ALU.add))
                nc.gpsimd.tensor_tensor(rstd[:, half, :], rstd[:, half, :], env["minus_half"][:, :], ALU.pow)\
                  .then_inc(rstd_ready, 1)

            def add_bias(pair, half):
                b = 2 * pair + half
                pool.wait_ge(xn_ready, b + 1)
                alone(pool, env["pool_passed"])
                chain.link(nc.gpsimd.tensor_tensor(X[:, bass.ts(b, N)], X[:, bass.ts(b, N)],
                                                   b_row[:, :, :].rearrange("p r d -> p (r d)"), ALU.add))

            def skip(n, s):
                pool.wait_ge(c1_copied, n + 1)
                wait(pool, gated_ready, n - 1)
                nc.gpsimd.tensor_tensor(xD[:, s, :], xB[:, s, 0:INNER], d_row[:, :, :].rearrange("p h c -> p (h c)"), ALU.mult)\
                    .then_inc(xD_ready, 1)

            def rms_of(n, s):
                pool.wait_ge(sq_done, n + 1)
                chain.link(nc.gpsimd.tensor_tensor(rms[:, s:s + 1], sumsq[:, s:s + 1], rms_eps[:, :], ALU.add))
                nc.gpsimd.tensor_tensor(rms[:, s:s + 1], rms[:, s:s + 1], minus_half1, ALU.pow).then_inc(rms_ready, 1)

            rstd_of(0, 0)
            rstd_of(0, 1)
            add_bias(0, 0)
            add_bias(0, 1)
            skip(0, 0)
            chain.end_prologue()
            chain.per_pair = 2 * 2 + 2 * R

            def step(pair, half, r, first, last, nxt):
                n = (2 * pair + half) * R + r
                rms_of(n, r % 2)
                if not (last and r == R - 1):
                    skip(n + 1, (r + 1) % 2)
                if not (isinstance(pair, int) and pair == PAIRS - 1):
                    if r == 1:
                        rstd_of(pair + 1, half)
                    if r == 3:
                        add_bias(pair + 1, half)
            inner = schedule(step)

            def body(pair):
                chain.pair(pair)
                inner(pair)
                if not (isinstance(pair, int) and pair == PAIRS - 1):
                    chain.end_pair()
            pairs(pool, body)


        @block.scalar
        def _(act):
            def copy_xT(b):
                act.wait_ge(f_ready, b * FU + 1)
                wait(act, x_split, b)
                wait(act, f_ready, (b - 1) * FU + FU)
                nc.scalar.copy(xT[:, :], ps_f[0][:, :]).then_inc(f_read, 1)

            def conv_act_of(b, c):
                u = 1 + c
                act.wait_ge(f_ready, b * FU + u + 1)
                wait(act, silu_done, b * CC + c - 1 if c >= 2 else b * CC)
                if c < 2:
                    wait(act, zg_ready, b * 2)
                nc.scalar.activation(th[:, c % 2, :], ps_f[u % 2][:, :], ACT.Tanh, bias=half_cb[:, c:c + 1], scale=0.5)
                nc.scalar.activation(hv[:, c % 2, :], ps_f[u % 2][:, :], ACT.Identity, bias=half_cb[:, c:c + 1], scale=0.5)\
                    .then_inc(f_read, 1)

            def z_act_of(b, k):
                u = 1 + CC + k
                act.wait_ge(f_ready, b * FU + u + 1)
                wait(act, silu_done, (b + 1) * CC)
                s = (k + 1) % 2
                nc.scalar.activation(th[:, s, :], ps_f[u % 2][:, :], ACT.Tanh, scale=0.5)
                nc.scalar.activation(hv[:, s, :], ps_f[u % 2][:, :], ACT.Identity, scale=0.5).then_inc(f_read, 1)

            def dt_act(b):
                act.wait_ge(dt_pre, b + 1)
                nc.scalar.activation(dt_abs[:, :], dt_raw[:, :], ACT.Abs).then_inc(dt_ln_done, 1)
                act.wait_ge(dt_ln_done, 3 * b + 1)
                nc.scalar.activation(dt_exp[:, :], dt_abs[:, :], ACT.Exp, scale=-1.0).then_inc(dt_ln_done, 1)
                act.wait_ge(dt_ln_done, 3 * b + 2)
                nc.scalar.activation(dt_ln[:, :], dt_exp[:, :], ACT.Ln, bias=1.0).then_inc(dt_ln_done, 1)

            def cum_act_of(b, half):
                act.wait_ge(cum_dve, b + 1)
                nc.scalar.activation(exp_acum[:, half, :], acum[:, half, :], ACT.Exp)
                nc.scalar.activation(exp_total[:, half, :], ps_small[:, 2 * RH:3 * RH], ACT.Exp)
                nc.scalar.activation(exp_rest[:, :], rest[:, :], ACT.Exp).then_inc(rest_exp, 1)

            def exp_diff(n):
                act.wait_ge(diff_ready, n + 1)
                wait(act, mix_ready, n)
                nc.scalar.activation(ediff[:, :, :], diff[:, :, :], ACT.Exp).then_inc(ediff_ready, 1)

            def copy_c1(n, s):
                act.wait_ge(c1_ready, n + 1)
                wait(act, c2_ready, n - 1)
                wait(act, diff_ready, n - 1)
                nc.scalar.copy(xB[:, s, :], ps_c1[:, P:P + INNER + STATE]).then_inc(c1_copied, 1)

            def square(n, s):
                act.wait_ge(gated_ready, n + 1)
                nc.scalar.activation(squares[:, :], gated[:, s, :], ACT.Square, accum_out=sumsq[:, s:s + 1]).then_inc(sq_done, 1)

            def copy_gT(n, s):
                act.wait_ge(gT_ready, n + 1)
                nc.scalar.copy(gT[:, s, :], ps_c3[:, 0:INNER]).then_inc(gT_copied, 1)

            def front_step(b, half, r):
                if r == 0:
                    copy_xT(b)
                if r == 1:
                    conv_act_of(b, 0)
                    conv_act_of(b, 1)
                    conv_act_of(b, 2)
                if r == 2:
                    dt_act(b)
                    cum_act_of(b, half)
                if r == 3:
                    z_act_of(b, 0)
                    z_act_of(b, 1)

            for r in range(3):
                front_step(0, 0, r)
            copy_c1(0, 0)
            exp_diff(0)
            front_step(0, 0, 3)

            def step(pair, half, r, first, last, nxt):
                n = (2 * pair + half) * R + r
                if not (first and r == 0):
                    copy_gT(n - 1, (r + 1) % 2)
                if not last and r < 3:
                    front_step(2 * nxt[0] + nxt[1], nxt[1], r)
                square(n, r % 2)
                if not (last and r == R - 1):
                    copy_c1(n + 1, (r + 1) % 2)
                    exp_diff(n + 1)
                if not last and r == 3:
                    front_step(2 * nxt[0] + nxt[1], nxt[1], 3)
            pairs(act, schedule(step))
            copy_gT(B * R - 1, 1)

        @block.vector
        def _(dve):
            chain = Chain(dve, dve_chain, 0)

            def graph_stats(pair, half):
                b = 2 * pair + half
                wait(dve, xn_ready, b - 1)
                for r in range(R):
                    ins = nc.vector.bn_stats(stats[:, half, r, :], X[:, bass.ds(b * N + r * D, D)])
                chain.link(ins)
                alone(dve, env["dve_passed"])
                for r in range(R):
                    ins = nc.vector.bn_aggr(aggr[:, half, r, :], stats[:, half, r, :])
                ins.then_inc(stats_ready, 1)

            def normalize(pair, half):
                b = 2 * pair + half
                dve.wait_ge(rstd_ready, b + 1)
                wait(dve, f_ready, FU * (b - 2) + 1)
                for r in range(R):
                    ins = nc.vector.tensor_scalar(xn[:, half, r, :], X[:, bass.ds(b * N + r * D, D)],
                                                  aggr[:, half, r, 0:1], rstd[:, half, r:r + 1], ALU.subtract, ALU.mult)
                ins.then_inc(xn_ready, 1)

            def split_x(b):
                dve.wait_ge(f_read, b * FU + 1)
                wait(dve, f_ready, (b - 1) * FU + 1 + CC)
                chain.link(nc.vector.tensor_copy(xh[:, PAD:], xT[:, :]))
                nc.vector.tensor_tensor(xl[:, PAD:], xT[:, :], xh[:, PAD:].bitcast(F32), ALU.subtract).then_inc(x_split, 1)

            def silu(b, half, c):
                dve.wait_ge(f_read, b * FU + 1 + c + 1)
                wait(dve, c1_ready, (b - 1) * R)
                if c < 2:
                    nc.vector.scalar_tensor_tensor(xc[:, half, c, :], th[:, c % 2, :], 1.0, hv[:, c % 2, :], ALU.add, ALU.mult)\
                        .then_inc(silu_done, 1)
                else:
                    wait(dve, c2_ready, (b - 1) * R)
                    nc.vector.scalar_tensor_tensor(BT[:, half, :], th[0:STATE, 0, :], 1.0, hv[0:STATE, 0, :], ALU.add, ALU.mult)
                    nc.vector.scalar_tensor_tensor(CT[:, half, :], th[STATE:, 0, :], 1.0, hv[STATE:, 0, :], ALU.add, ALU.mult)\
                        .then_inc(silu_done, 1)

            def z_silu(b, half, k):
                dve.wait_ge(f_read, b * FU + 1 + CC + k + 1)
                s = (k + 1) % 2
                nc.vector.scalar_tensor_tensor(zg[:, half, 2 * k:2 * k + 2, :].rearrange("p r c -> p (r c)"), th[:, s, :], 1.0,
                                               hv[:, s, :], ALU.add, ALU.mult).then_inc(zg_ready, 1)

            def dt_first(b):
                dve.wait_ge(dtm_ready, b + 1)
                nc.vector.tensor_tensor(dt_raw[:, :], ps_small[:, 0:RH], dtb[:, :, :].rearrange("p r h -> p (r h)"), ALU.add)\
                    .then_inc(dt_pre, 1)

            def dt_second(b, half):
                dve.wait_ge(dt_ln_done, 3 * b + 3)
                dve.wait_ge(dt_pre, b + 1)
                wait(dve, c1_ready, (b - 1) * R)
                chain.link(nc.vector.scalar_tensor_tensor(dt[:, half, :], dt_raw[:, :], 0.0, dt_ln[:, :], ALU.max, ALU.add))
                nc.vector.tensor_tensor(dA[:, half, :], dt[:, half, :], a_neg[:, :, :].rearrange("p r h -> p (r h)"), ALU.mult)\
                    .then_inc(dA_ready, 1)

            def cum_first(b, half):
                dve.wait_ge(cum_ready, b + 1)
                chain.link(nc.vector.tensor_copy(acum[:, half, :], ps_small[:, RH:2 * RH]))
                wait(dve, rest_exp, b)
                nc.vector.tensor_tensor(rest[:, :], ps_small[:, 2 * RH:3 * RH], acum[:, half, :], ALU.subtract)\
                    .then_inc(cum_dve, 1)

            def cum_second(b, half):
                dve.wait_ge(rest_exp, b + 1)
                nc.vector.tensor_tensor(dt_rest[:, half, :], exp_rest[:, :], dt[:, half, :], ALU.mult).then_inc(front_done, 1)

            def by_head(v, half, r):
                return v[:, half, r * HEADS:(r + 1) * HEADS].unsqueeze(2).to_broadcast([P, HEADS, HEAD])

            def chunk_first(n, b, half, r):
                s = r % 2
                dve.wait_ge(c1_ready, n + 1)
                wait(dve, ediff_ready, n)
                dve.wait_ge(front_done, b + 1)
                for h in range(HEADS):
                    ins = nc.vector.scalar_tensor_tensor(diff[:, h, :], ps_bc[:, h * P:(h + 1) * P],
                                                         acum[:, half, r * HEADS + h:r * HEADS + h + 1], strict[:, :],
                                                         ALU.subtract, ALU.mult)
                ins.then_inc(diff_ready, 1)
                dve.wait_ge(c1_copied, n + 1)
                wait(dve, mix_ready, n)
                chain.link(nc.vector.tensor_tensor(cb_m[:, :], ps_c1[:, 0:P], tri[:, :], ALU.mult))
                wait(dve, c2_ready, n - 1)
                x_v = xB[:, s, 0:INNER].rearrange("p (h c) -> p h c", c=HEAD)
                nc.vector.tensor_tensor(xdt[:, s, :].rearrange("p (h c) -> p h c", c=HEAD), x_v, by_head(dt, half, r), ALU.mult)
                nc.vector.tensor_tensor(xrest[:, s, :].rearrange("p (h c) -> p h c", c=HEAD), x_v, by_head(dt_rest, half, r),
                                        ALU.mult)
                dve.wait_ge(ediff_ready, n + 1)
                nc.vector.scalar_tensor_tensor(mix[:, s, :, :], ediff[:, :, :], 1.0, cb_m[:, :].unsqueeze(1).to_broadcast([P, HEADS, P]),
                                               ALU.min, ALU.mult).then_inc(mix_ready, 1)

            def chunk_second(n, half, r):
                s = r % 2
                dve.wait_ge(c2_ready, n + 1)
                if r == 0:
                    nc.vector.tensor_copy(state[:, :], ps_s[0:STATE, 0:INNER]).then_inc(state_done, 1)
                else:
                    chain.link(nc.vector.tensor_tensor(
                        decayed[:, :].rearrange("p (h c) -> p h c", c=HEAD), state[:, :].rearrange("p (h c) -> p h c", c=HEAD),
                        exp_total[0:STATE, half, r * HEADS:(r + 1) * HEADS].unsqueeze(2).to_broadcast([STATE, HEADS, HEAD]),
                        ALU.mult))
                    nc.vector.tensor_tensor(state[:, :], decayed[:, :], ps_s[0:STATE, 0:INNER], ALU.add).then_inc(state_done, 1)
                dve.wait_ge(xD_ready, n + 1)
                if r == 0:
                    chain.link(nc.vector.tensor_tensor(y[:, :], ps_c2[:, 0:INNER], xD[:, s, :], ALU.add))
                else:
                    for h in range(HEADS):
                        cols = slice(h * HEAD, (h + 1) * HEAD)
                        ins = nc.vector.scalar_tensor_tensor(y_part[:, cols], ps_c2[:, INNER + h * HEAD:INNER + (h + 1) * HEAD],
                                                             exp_acum[:, half, r * HEADS + h:r * HEADS + h + 1], xD[:, s, cols],
                                                             ALU.mult, ALU.add)
                    chain.link(ins)
                    chain.link(nc.vector.tensor_tensor(y[:, :], y_part[:, :], ps_c2[:, 0:INNER], ALU.add))
                wait(dve, gT_ready, n - 1)
                wait(dve, sq_done, n - 1)
                nc.vector.tensor_tensor(gated[:, s, :], y[:, :], zg[:, half, r, :], ALU.mult).then_inc(gated_ready, 1)

            def update(n, col, s):
                dve.wait_ge(o_ready, n + 1)
                dve.wait_ge(rms_ready, n + 1)
                nc.vector.scalar_tensor_tensor(X[:, bass.ds(col, D)], ps_c3[:, INNER:INNER + D], rms[:, s:s + 1],
                                               X[:, bass.ds(col, D)], ALU.mult, ALU.add).then_inc(x_done, 1)

            def front_step(b, half, r):
                if r == 0:
                    split_x(b)
                if r == 1:
                    silu(b, half, 0)
                    silu(b, half, 1)
                    silu(b, half, 2)
                    dt_first(b)
                if r == 2:
                    dt_second(b, half)
                    cum_first(b, half)
                    cum_second(b, half)
                if r == 3:
                    z_silu(b, half, 0)
                    z_silu(b, half, 1)

            graph_stats(0, 0)
            graph_stats(0, 1)
            normalize(0, 0)
            normalize(0, 1)
            for r in range(3):
                front_step(0, 0, r)
            chunk_first(0, 0, 0, 0)
            front_step(0, 0, 3)
            chain.end_prologue()
            chain.per_pair = 2 * (1 + 1 + 1 + 1 + R + 1 + 3 * (R - 1))

            def step(pair, half, r, first, last, nxt):
                b = 2 * pair + half
                n = b * R + r
                chunk_second(n, half, r)
                if not last and r < 3:
                    front_step(2 * nxt[0] + nxt[1], nxt[1], r)
                if not (last and r == R - 1):
                    if r < R - 1:
                        chunk_first(n + 1, b, half, r + 1)
                    else:
                        chunk_first(n + 1, b + 1, 1 - half, 0)
                if not last and r == 3:
                    front_step(2 * nxt[0] + nxt[1], nxt[1], 3)
                if not (first and r == 0):
                    update(n - 1, (n - 1) * D, (r + 1) % 2)
                if not (isinstance(pair, int) and pair == PAIRS - 1):
                    if r == 1:
                        graph_stats(pair + 1, half)
                    if r == 3:
                        normalize(pair + 1, half)
            inner = schedule(step)

            def body(pair):
                chain.pair(pair)
                inner(pair)
                if not (isinstance(pair, int) and pair == PAIRS - 1):
                    chain.end_pair()
            pairs(dve, body)
            update(B * R - 1, (B * R - 1) * D, 1)
            dve.wait_ge(x_done, B * R)

        @block.tensor
        def _(pe):
            def transposes(b, half):
                pe.wait_ge(xn_ready, b + 1)
                wait(pe, f_read, b * FU - 1)
                for r in range(R):
                    ins = nc.tensor.transpose(ps_f[0][:, r * P:(r + 1) * P], xn[:, half, r, :], ident[:, :])
                ins.then_inc(f_ready, 1)

            def conv(b, c):
                u = 1 + c
                if c == 0:
                    pe.wait_ge(x_split, b + 1)
                wait(pe, f_read, b * FU + u - 1)
                cols = slice(c * P, (c + 1) * P)
                for k in range(TAPS):
                    shift = slice(PAD - (TAPS - 1) + k, PAD - (TAPS - 1) + k + N)
                    nc.tensor.matmul(ps_f[u % 2][:, :], wch[:, k, cols], xh[:, shift], start=k == 0, stop=False)
                    nc.tensor.matmul(ps_f[u % 2][:, :], wch[:, k, cols], xl[:, shift], start=False, stop=False)
                    ins = nc.tensor.matmul(ps_f[u % 2][:, :], wcl[:, k, cols], xh[:, shift], start=False, stop=k == TAPS - 1)
                ins.then_inc(f_ready, 1)

            def z_of(b, k):
                u = 1 + CC + k
                wait(pe, f_read, b * FU + u - 1)
                for j in range(2):
                    r = 2 * k + j
                    ins = nc.tensor.matmul(ps_f[u % 2][:, j * INNER:(j + 1) * INNER], xT[:, r * P:(r + 1) * P], wz[:, :],
                                           start=True, stop=True)
                ins.then_inc(f_ready, 1)

            def dt_of(b):
                wait(pe, rest_exp, b)
                for r in range(R):
                    ins = nc.tensor.matmul(ps_small[:, r * HEADS:(r + 1) * HEADS], xT[:, r * P:(r + 1) * P], wdt_sb[:, :],
                                           start=True, stop=True)
                ins.then_inc(dtm_ready, 1)

            def sums(b, half):
                pe.wait_ge(dA_ready, b + 1)
                nc.tensor.matmul(ps_small[:, RH:2 * RH], tri[:, :], dA[:, half, :], start=True, stop=True)
                nc.tensor.matmul(ps_small[:, 2 * RH:3 * RH], ones[:, :], dA[:, half, :], start=True, stop=True)\
                    .then_inc(cum_ready, 1)

            def chunk_prep(n, b, half, r):
                wait(pe, diff_ready, n)
                wait(pe, c1_copied, n)
                wait(pe, mix_ready, n)
                if r == 0:
                    pe.wait_ge(silu_done, (b + 1) * CC)
                for h in range(HEADS):
                    col = r * HEADS + h
                    nc.tensor.matmul(ps_bc[:, h * P:(h + 1) * P], dA[:, half, col:col + 1].to_broadcast([P, P]), tri[:, :],
                                     start=True, stop=True)
                tile = slice(r * P, (r + 1) * P)
                nc.tensor.matmul(ps_c1[:, 0:P], BT[:, half, tile], CT[:, half, tile], start=True, stop=True)
                for k in range(2):
                    nc.tensor.transpose(ps_c1[:, P + k * P:P + (k + 1) * P], xc[:, half, k, tile], ident[:, :])
                nc.tensor.transpose(ps_c1[:, P + INNER:P + INNER + STATE], BT[:, half, tile], ident[0:STATE, 0:STATE])\
                    .then_inc(c1_ready, 1)

            def chunk_products(n, half, r):
                s = r % 2
                pe.wait_ge(mix_ready, n + 1)
                wait(pe, gated_ready, n)
                wait(pe, state_done, n)
                for h in range(HEADS):
                    nc.tensor.matmul(ps_c2[:, h * HEAD:(h + 1) * HEAD], mix[:, s, h, :], xdt[:, s, h * HEAD:(h + 1) * HEAD],
                                     start=True, stop=True)
                if r > 0:
                    nc.tensor.matmul(ps_c2[:, INNER:2 * INNER], CT[:, half, r * P:(r + 1) * P], state[:, :],
                                     start=True, stop=True)
                nc.tensor.matmul(ps_s[0:STATE, 0:INNER], xB[:, s, INNER:INNER + STATE], xrest[:, s, :],
                                 start=True, stop=True).then_inc(c2_ready, 1)

            def transpose_gated(n, s):
                pe.wait_ge(gated_ready, n + 1)
                wait(pe, x_done, n)
                for k in range(2):
                    ins = nc.tensor.transpose(ps_c3[:, k * P:(k + 1) * P], gated[:, s, k * P:(k + 1) * P], ident[:, :])
                ins.then_inc(gT_ready, 1)

            def project(n, s):
                pe.wait_ge(gT_copied, n + 1)
                for k in range(2):
                    ins = nc.tensor.matmul(ps_c3[:, INNER:INNER + D], gT[:, s, k * P:(k + 1) * P], wo[:, k, :],
                                           start=k == 0, stop=k == 1)
                ins.then_inc(o_ready, 1)

            def front_step(b, half, r):
                if r == 0:
                    transposes(b, half)
                if r == 1:
                    conv(b, 0)
                    conv(b, 1)
                    conv(b, 2)
                    dt_of(b)
                if r == 2:
                    sums(b, half)
                if r == 3:
                    z_of(b, 0)
                    z_of(b, 1)

            for r in range(3):
                front_step(0, 0, r)
            chunk_prep(0, 0, 0, 0)
            front_step(0, 0, 3)

            def step(pair, half, r, first, last, nxt):
                b = 2 * pair + half
                n = b * R + r
                if not (first and r == 0):
                    transpose_gated(n - 1, (r + 1) % 2)
                chunk_products(n, half, r)
                if not last and r < 3:
                    front_step(2 * nxt[0] + nxt[1], nxt[1], r)
                if not (last and r == R - 1):
                    if r < R - 1:
                        chunk_prep(n + 1, b, half, r + 1)
                    else:
                        chunk_prep(n + 1, b + 1, 1 - half, 0)
                if not last and r == 3:
                    front_step(2 * nxt[0] + nxt[1], nxt[1], 3)
                if not (first and r == 0):
                    project(n - 1, (r + 1) % 2)
            pairs(pe, schedule(step))
            transpose_gated(B * R - 1, 1)
            project(B * R - 1, 1)


def build(nc, a, out, layers=range(8), only_load=None):
    ctx = ExitStack()
    with ctx:
        X = ctx.enter_context(nc.sbuf_tensor("X", [P, B * N], F32))
        ident = ctx.enter_context(nc.sbuf_tensor("ident", [P, P], F32))
        minus_half = ctx.enter_context(nc.sbuf_tensor("minus_half", [P, R], F32))
        ident_zero, ident_done = (ctx.enter_context(nc.semaphore(n)) for n in ("ident_zero", "ident_done"))
        dve_passed, pool_passed = (ctx.enter_context(nc.semaphore(n)) for n in ("dve_passed", "pool_passed"))
        out_stored = ctx.enter_context(nc.semaphore("out_stored"))
        mask_dram = nc.dram_tensor("mask_dram", [B, P, R * N], BF16, kind="Internal").ap()
        eps = ctx.enter_context(nc.sbuf_tensor("eps", [P, R], F32))
        env = {"X": X, "ident": ident, "minus_half": minus_half, "eps": eps, "mask_dram": mask_dram,
               "dve_passed": dve_passed, "pool_passed": pool_passed}

        with nc.Block() as block:
            @block.gpsimd
            def _(pool):
                nc.gpsimd.memset(minus_half[:, :], -0.5)
                nc.gpsimd.memset(eps[:, :], LN_EPS)
                nc.gpsimd.memset(ident[:, :], 0.0).then_inc(ident_zero, 1)
                pool.wait_ge(ident_zero, 1)
                nc.gpsimd.affine_select(out=ident[:, :], in_=ident[:, :], compare_op=ALU.not_equal, fill=1.0,
                                        base=0, pattern=[[-1, P]], channel_multiplier=1).then_inc(ident_done, 1)
                pool.wait_ge(ident_done, 1)

        if 0 not in layers:
            only_load(nc, env, a)
        else:
            gnn_layer(nc, env, "g0", a["L0_gnn_W"], a["L0_gnn_Wt"], a["L0_gnn_A"], 1, elu=True,
                      node_mask=True, load=(a["x"], a["adj"], a["nodemask"]))
        if 1 in layers:
            f = {k: a[f"L0_ffn_{k}"] for k in ("W_in", "conv_w", "conv_b", "dt_bias", "A_log", "D", "norm_w", "W_out_t",
                                               "W_lin", "b_lin")}
            mamba_layer(nc, env, "f0", f["W_in"], f["conv_w"], f["conv_b"], f["dt_bias"], f["A_log"], f["D"],
                        f["norm_w"], f["W_out_t"], f["W_lin"], f["b_lin"])
        if 2 in layers:
            gnn_layer(nc, env, "g1", a["L1_gnn_W"], a["L1_gnn_Wt"], a["L1_gnn_A"], 1)
        if 3 in layers:
            moe_layer(nc, env, "f1", a["L1_ffn_w1"], a["L1_ffn_b1"], a["L1_ffn_w2"], a["L1_ffn_b2"],
                      a["L1_ffn_router_w"], None, 128, keep_tokens=True, split_h=False)
        if 4 in layers:
            gnn_layer(nc, env, "g2", a["L2_gnn_W"], a["L2_gnn_Wt"], a["L2_gnn_A"], 1, elu=True)
        if 5 in layers:
            moe_layer(nc, env, "f2", a["L2_ffn_W1"], a["L2_ffn_b1"], a["L2_ffn_W2"], a["L2_ffn_b2"],
                      a["L2_ffn_Wg"], a["L2_ffn_bg"], 512)
        if 6 in layers:
            gnn_layer(nc, env, "g3", a["L3_gnn_W"], a["L3_gnn_Wt"], a["L3_gnn_A"], 4, bias=a["L3_gnn_b"])
        if 7 in layers:
            moe_layer(nc, env, "f3", a["L3_ffn_W1"], a["L3_ffn_b1"], a["L3_ffn_W2"], a["L3_ffn_b2"],
                      a["L3_ffn_Wr"], a["L3_ffn_br"], 512, own_ln=(a["L3_ffn_ln_g"], a["L3_ffn_ln_b"]))

        with nc.Block() as block:
            @block.sync
            def _(sp):
                out_v = out.rearrange("b (r p) d -> p (b r) d", p=P)
                sp.dma_start(out_v, X[:, :].rearrange("p (t d) -> p t d", d=D)).then_inc(out_stored, 16)
                sp.wait_ge(out_stored, 16)


def _layout(inputs):
    arrays = {k: np.ascontiguousarray(v) for k, v in inputs.items()}
    arrays["nodemask"] = np.ascontiguousarray(inputs["nodemask"].reshape(B * R, P).T)
    for l in range(4):
        w, a = arrays.pop(f"L{l}_gnn_W"), arrays.pop(f"L{l}_gnn_a")
        if l >= 2:
            w = w.T
        arrays[f"L{l}_gnn_W"], arrays[f"L{l}_gnn_Wt"] = np.ascontiguousarray(w), np.ascontiguousarray(w.T)
        heads = a.shape[0] if l == 3 else 1
        a = a.reshape(heads, 2, D // heads)
        cols = np.zeros((D, P), a.dtype)
        for h in range(heads):
            for q in range(4):
                cols[h * (D // heads):(h + 1) * (D // heads), 32 * q + h] = a[h, q // 2]
        arrays[f"L{l}_gnn_A"] = cols
    for name in ("L0_ffn_conv_b", "L0_ffn_norm_w"):
        arrays[name] = np.ascontiguousarray(arrays[name].reshape(-1, P).T)
    arrays["L0_ffn_conv_w"] = np.ascontiguousarray(arrays["L0_ffn_conv_w"].T)
    arrays["L0_ffn_W_out_t"] = np.ascontiguousarray(arrays.pop("L0_ffn_W_out").T)
    arrays["L1_ffn_router_w"] = np.ascontiguousarray(arrays["L1_ffn_router_w"].T)
    for l in (1, 2, 3):
        name = f"L{l}_ffn_b1"
        arrays[name] = np.ascontiguousarray(arrays[name].reshape(-1, P).T)
        arrays[f"L{l}_ffn_b2"] = np.ascontiguousarray(arrays[f"L{l}_ffn_b2"].T)
    for name in ("L3_ffn_ln_g", "L3_ffn_ln_b"):
        arrays[name] = np.ascontiguousarray(arrays[name].T)
    return arrays


def kernel(**inputs):
    import concourse.bacc as bacc
    from concourse.bass_utils import run_bass_kernel_spmd

    arrays = {f"in_{k}": v for k, v in _layout(inputs).items()}
    nc = bacc.Bacc("TRN2", target_bir_lowering=False, num_devices=1)
    aps = {k[3:]: nc.dram_tensor(k, v.shape, mybir.dt.from_np(v.dtype), kind="ExternalInput").ap()
           for k, v in arrays.items()}
    out = nc.dram_tensor("out", [B, N, D], F32, kind="ExternalOutput").ap()
    build(nc, aps, out)
    r = run_bass_kernel_spmd(nc, [arrays], core_ids=[0])
    return r.results[0]["out"]
```

```python
import numpy as np
import concourse.bass as bass
from concourse import mybir
from contextlib import ExitStack, contextmanager

F32 = mybir.dt.float32
F32R = mybir.dt.float32r
BF16 = mybir.dt.bfloat16
I32 = mybir.dt.int32
U32 = mybir.dt.uint32
ALU = mybir.AluOpType
ACT = mybir.ActivationFunctionType

B, N, D = 16, 512, 128
P = 128
R = N // P
PAIRS = B // 2
E = 8
LN_EPS = 1e-5
SLOPE = 0.2
MASKED = -float(2 ** 53)


def pairs(eng, body):
    body(0)
    with eng.Fori(1, PAIRS - 1) as pair:
        body(pair)
    body(PAIRS - 1)


def wait(eng, sem, value):
    if isinstance(value, int) and value <= 0:
        return
    eng.wait_ge(sem, value)


def layer_semaphores(nc, ctx, name):
    made = []

    def clear():
        nc.clear_and_free_semaphores(made)
        nc.all_engine_barrier()

    def sem(n):
        made.append(nc.alloc_semaphore(name=f"{name}_{n}"))
        return made[-1]
    ctx.callback(clear)
    return sem


def alone(eng, passed):
    eng.sem_inc(passed, 1)


class Chain:

    def __init__(self, eng, sem, per_pair):
        self.eng, self.sem, self.per_pair = eng, sem, per_pair
        self.base, self.count, self.before = 0, 0, 0

    def pair(self, pair):
        self.base, self.count = pair * self.per_pair + self.before, 0

    def end_pair(self):
        assert self.count == self.per_pair, f"chain {self.count}"

    def link(self, ins):
        self.count += 1
        ins.then_inc(self.sem, 1)
        self.eng.wait_ge(self.sem, self.base + self.count)

    def end_prologue(self):
        self.before, self.count = self.count, 0


def gnn_layer(nc, env, name, w, wt, a_pad, heads, elu=False, node_mask=None, bias=None, load=None,
              prefetch=((), None)):
    X, ident, mask_dram = env["X"], env["ident"], env["mask_dram"]
    C = D // heads
    T = heads * R
    Z_AT, SCORE_AT, LEAKY_AT, TRANS_AT, COPY_AT = 7, 6, 5, -1, -2
    ATTEND_AT = COPY_AT - R
    if heads == 1:
        G = 4
        STATS_AT, NORM_AT, XT_AT, ROWS_AT, SPLIT_AT, SIDES_AT = 14, 12, 11, 10, 9, 8
    else:
        G = 2
        STATS_AT, NORM_AT, XT_AT, ROWS_AT, SPLIT_AT, SIDES_AT = 20, 18, 16, 15, 13, 12
    MASK_AT, WH_AT, COPY_WH_AT = 8, -2, -3
    OUT_AT, BACK_AT, FINISH_AT, ELU_AT, UPDATE_AT = [-(T + R + 2 + i) for i in range(5)]
    TAIL = -UPDATE_AT
    TURNS = B // G
    LAG = -(-(WH_AT - BACK_AT) // T)
    ctx = ExitStack()
    with ctx:
        def sb(n, shape, dt=F32):
            return ctx.enter_context(nc.sbuf_tensor(f"{name}_{n}", shape, dt))

        def pb(n):
            return ctx.enter_context(nc.psum_tensor(f"{name}_{n}", [P, 512], F32))

        sem = layer_semaphores(nc, ctx, name)

        w_sb, wt_sb, a_sb = sb("w", [P, D]), sb("wt", [P, D]), sb("a", [P, P])
        wa = sb("wa", [P, P])
        st_const = sb("st_const", [P, 1])
        row_lo, row_hi = sb("row_lo", [P, 1]), sb("row_hi", [P, 1])
        head_lo, head_hi = sb("head_lo", [P, heads]), sb("head_hi", [P, heads])
        stats, aggr, rstd = sb("stats", [P, 2, R, 6]), sb("aggr", [P, 2, R, 2]), sb("rstd", [P, 2, R])
        shift = sb("shift", [P, 2, R])
        xn = sb("xn", [P, 2, R, P])
        xT = sb("xT", [P, G, N])
        wh = sb("wh", [P, 2, R, D])
        rows = sb("rows", [P, N], F32R)
        lhs, rhs = sb("lhs", [P, 2, heads, N], F32R), sb("rhs", [P, 2, N], F32R)
        score = sb("score", [P, 2, R, N])
        z_max, z_low, neg_top = sb("z_max", [P, 2, R]), sb("z_low", [P, R]), sb("neg_top", [P, 2, R])
        prob, probT = sb("prob", [P, R, N]), sb("probT", [P, 2, R, R, P])
        outT = sb("outT", [P, N])
        rowsum, rinv = sb("rowsum", [P, G, R, heads]), sb("rinv", [P, R, heads])
        att = sb("att", [P, 2, N])
        neg, eneg = sb("neg", [P, N]), sb("eneg", [P, N])
        mask = sb("mask", [P, 2, R * N], BF16)
        if bias is not None:
            bias_col, bias_row = sb("bias_col", [P, 1]), sb("bias_row", [P, R, D])
        if load:
            adj_in, nm_sb = sb("adj_in", [P, 2, R, N], I32), sb("nm", [P, B * R])

        ps_xT, ps_wh = pb("ps_xT"), pb("ps_wh")
        ps_outT = [pb(f"ps_outT{i}") for i in range(2)]
        ps_z = [pb(f"ps_z{i}") for i in range(2)]
        ps_pT = [pb(f"ps_pT{i}") for i in range(2)]

        w_loaded, wa_done, wa_copied, consts = [sem(n) for n in ("w_loaded", "wa_done", "wa_copied", "consts")]
        stats_ready, rstd_ready, xn_ready = sem("stats_ready"), sem("rstd_ready"), sem("xn_ready")
        xT_ready, xT_copied, wh_ready, wh_copied = [sem(n) for n in ("xT_ready", "xT_copied", "wh_ready", "wh_copied")]
        rows_ready, rows_split, sides_ready = sem("rows_ready"), sem("rows_split"), sem("sides_ready")
        z_ready, scored, leaky_done, top_ready = sem("z_ready"), sem("scored"), sem("leaky_done"), sem("top_ready")
        prob_ready, pT_ready, pT_copied, out_done = [sem(n) for n in ("prob_ready", "pT_ready", "pT_copied", "out_done")]
        outT_copied, back_ready = sem("outT_copied"), sem("back_ready")
        out_used, neg_ready, eneg_ready, att_ready, x_done = [
            sem(n) for n in ("out_used", "neg_ready", "eneg_ready", "att_ready", "x_done")]
        dve_chain, pool_chain = sem("dve_chain"), sem("pool_chain")
        if load:
            x_loaded, adj_loaded = [sem("x_loaded0"), sem("x_loaded1")], [sem("adj_loaded0"), sem("adj_loaded1")]
            mask_done, mask_stored = sem("mask_done"), [sem("mask_stored0"), sem("mask_stored1")]
        else:
            mask_loaded = [sem("mask_loaded0"), sem("mask_loaded1")]

        def tile_at(turn, g, k, ahead):
            turns, rest = divmod(g * T + k + ahead, G * T)
            if isinstance(turn, int) and not 0 <= turn + turns < TURNS:
                return None
            return turn + turns, rest // T, rest % T // R, rest % R

        def graph_at(turn, g, k, ahead):
            t = tile_at(turn, g, k, ahead)
            return t[:2] if t and t[2:] == (0, 0) else None

        def tile_number(turn, g, h, r):
            return (G * turn + g) * T + h * R + r

        def walk(eng, step):
            before = -(-STATS_AT // T)
            for k in range(-before * T, 0):
                step(0, 0, k)
            for k in range(G * T):
                step(0, k // T, k % T)
            with eng.Fori(1, TURNS - 1) as turn:
                for k in range(G * T):
                    step(turn, k // T, k % T)
            for k in range(G * T):
                step(TURNS - 1, k // T, k % T)
            for k in range(TAIL - T + 1):
                step(TURNS, 0, k)

        block = ctx.enter_context(nc.Block())

        @block.sync
        def _(sp):
            if load:
                x_in, adj, nm = load
                x_v = x_in.rearrange("b (r p) d -> p (b r) d", p=P)
                adj_v = adj.rearrange("b (r p) j -> p (b r) j", p=P)
                sp.dma_start(X[:, 0:2 * N].rearrange("p (t d) -> p t d", d=D), x_v[:, 0:2 * R, :]).then_inc(x_loaded[0], 16)
            sp.dma_start(w_sb[:, :], w).then_inc(w_loaded, 16)
            sp.dma_start(wt_sb[:, :], wt).then_inc(w_loaded, 16)
            sp.dma_start(a_sb[:, :], a_pad).then_inc(w_loaded, 16)
            if bias is not None:
                sp.dma_start(bias_col[:, :], bias.rearrange("(p o) -> p o", o=1)).then_inc(w_loaded, 16)
                for r in range(R):
                    sp.dma_start(bias_row[:, r, :], bias.partition_broadcast(P)).then_inc(w_loaded, 16)
            if load:
                sp.dma_start(nm_sb[:, :], nm).then_inc(w_loaded, 16)

                def load_adj(pair, half):
                    wait(sp, mask_done, 2 * pair + half - 1)
                    sp.dma_start(adj_in[:, half, :, :], adj_v[:, bass.ds((2 * pair + half) * R, R), :])\
                      .then_inc(adj_loaded[half], 16)

                def store_mask(pair, half):
                    b = 2 * pair + half
                    sp.wait_ge(mask_done, b + 1)
                    sp.dma_start(mask_dram[bass.ds(b, 1)].rearrange("b p n -> p (b n)"), mask[:, half, :])\
                      .then_inc(mask_stored[half], 16)

                load_adj(0, 0)
                load_adj(0, 1)
                sp.dma_start(X[:, 2 * N:B * N].rearrange("p (t d) -> p t d", d=D), x_v[:, 2 * R:, :]).then_inc(x_loaded[1], 16)
                with sp.Fori(1, PAIRS) as pair:
                    for half in range(2):
                        store_mask(pair - 1, half)
                        load_adj(pair, half)
                for half in range(2):
                    store_mask(PAIRS - 1, half)
                for half in range(2):
                    sp.wait_ge(mask_stored[half], 16 * PAIRS)
            else:
                def load_mask(pair, half):
                    wait(sp, scored, (2 * pair + half - 1) * T)
                    sp.dma_start(mask[:, half, :], mask_dram[bass.ds(2 * pair + half, 1)].rearrange("b p n -> p (b n)"))\
                      .then_inc(mask_loaded[half], 16)

                load_mask(0, 0)
                load_mask(0, 1)
                for dst, src in prefetch[0]:
                    sp.dma_start(dst, src).then_inc(prefetch[1], 16)
                with sp.Fori(1, PAIRS) as pair:
                    load_mask(pair, 0)
                    load_mask(pair, 1)

        n_loads = 16 * (3 + (1 + R if bias is not None else 0) + (1 if load else 0))

        @block.gpsimd
        def _(pool):
            def rstd_of(turn, g):
                b = G * turn + g
                pool.wait_ge(stats_ready, b + 1)
                nc.gpsimd.tensor_tensor(rstd[:, g % 2, :], aggr[:, g % 2, :, 1], env["eps"][:, :], ALU.add)\
                  .then_inc(pool_chain, 1)
                pool.wait_ge(pool_chain, 3 * b + 1)
                nc.gpsimd.tensor_tensor(rstd[:, g % 2, :], rstd[:, g % 2, :], env["minus_half"][:, :], ALU.pow)\
                  .then_inc(pool_chain, 1)
                pool.wait_ge(pool_chain, 3 * b + 2)
                nc.gpsimd.tensor_tensor(shift[:, g % 2, :], aggr[:, g % 2, :, 0], rstd[:, g % 2, :], ALU.mult)\
                  .then_inc(pool_chain, 1)
                pool.wait_ge(pool_chain, 3 * b + 3)
                alone(pool, env["pool_passed"])
                nc.gpsimd.tensor_scalar(shift[:, g % 2, :], shift[:, g % 2, :], -1.0, None, ALU.mult).then_inc(rstd_ready, 1)

            def sides(turn, g):
                b = G * turn + g
                pool.wait_ge(rows_split, 3 * b + 3)
                alone(pool, env["pool_passed"])
                wait(pool, z_ready, (b - 1) * T)
                alone(pool, env["pool_passed"])
                for h in range(heads):
                    nc.gpsimd.tensor_scalar(lhs[:, g % 2, h, :], rows[:, :].bitcast(F32), head_lo[:, h:h + 1], head_hi[:, h:h + 1],
                                            ALU.mult, ALU.add)
                nc.gpsimd.tensor_scalar(rhs[:, g % 2, :], rows[:, :].bitcast(F32), row_hi[:, :], row_lo[:, :], ALU.mult, ALU.add)\
                    .then_inc(sides_ready, 1)

            def residual(turn, g):
                b = G * turn + g
                pool.wait_ge(out_used, b + 1)
                alone(pool, env["pool_passed"])
                if bias is not None:
                    nc.gpsimd.tensor_tensor(att[:, g % 2, :], att[:, g % 2, :], bias_row[:, :, :].rearrange("p r d -> p (r d)"),
                                            ALU.add).then_inc(att_ready, 1)
                    pool.wait_ge(att_ready, b + 1)
                    alone(pool, env["pool_passed"])
                nc.gpsimd.tensor_tensor(X[:, bass.ts(b, N)], X[:, bass.ts(b, N)], att[:, g % 2, :], ALU.add)\
                    .then_inc(x_done, 1)

            nc.gpsimd.memset(row_lo[0:64, :], 1.0)
            nc.gpsimd.memset(row_lo[64:P, :], 0.0)
            nc.gpsimd.memset(row_hi[0:64, :], 0.0)
            nc.gpsimd.memset(row_hi[64:P, :], 1.0)
            nc.gpsimd.memset(head_hi[0:64, :], 0.0)
            nc.gpsimd.memset(head_lo[64:P, :], 0.0).then_inc(consts, 1)
            pool.wait_ge(consts, 1)
            nc.gpsimd.tensor_tensor(head_lo[0:64, :], ident[0:64, 0:heads], ident[0:64, 32:32 + heads], ALU.add)
            nc.gpsimd.tensor_tensor(head_hi[64:P, :], ident[64:P, 64:64 + heads], ident[64:P, 96:96 + heads], ALU.add)\
                .then_inc(consts, 1)
            pool.wait_ge(consts, 2)

            def step(turn, g, k):
                if b := graph_at(turn, g, k, STATS_AT):
                    rstd_of(*b)
                if b := graph_at(turn, g, k, SIDES_AT):
                    sides(*b)
                if not elu and (b := graph_at(turn, g, k, UPDATE_AT)):
                    residual(*b)
            walk(pool, step)

        @block.scalar
        def _(act):
            def normalize(turn, g):
                b = G * turn + g
                act.wait_ge(rstd_ready, b + 1)
                wait(act, xT_ready, b - 1)
                for r in range(R):
                    ins = nc.scalar.activation(xn[:, g % 2, r, :], X[:, bass.ds(b * N + r * D, D)], ACT.Identity,
                                               bias=shift[:, g % 2, r:r + 1], scale=rstd[:, g % 2, r:r + 1])
                ins.then_inc(xn_ready, 1)

            def high_rows(turn, g):
                b = G * turn + g
                act.wait_ge(rows_ready, b + 1)
                wait(act, sides_ready, b)
                nc.scalar.activation(rows[:, :], ps_xT[:, :], ACT.Identity, bias=st_const[:, :]).then_inc(rows_split, 1)

            def copy_xT(turn, g):
                act.wait_ge(xT_ready, G * turn + g + 1)
                nc.scalar.copy(xT[:, g, :], ps_xT[:, :]).then_inc(xT_copied, 1)

            def copy_wh(turn, g):
                b = G * turn + g
                act.wait_ge(wh_ready, b + 1)
                wait(act, out_done, (b - 1) * T)
                nc.scalar.copy(wh[:, g % 2, :, :].rearrange("p r d -> p (r d)"), ps_wh[:, :]).then_inc(wh_copied, 1)

            def copy_outT(turn, g):
                b = G * turn + g
                act.wait_ge(out_done, (b + 1) * T)
                wait(act, back_ready, b)
                nc.scalar.copy(outT[:, :], ps_outT[g % 2][:, :]).then_inc(outT_copied, 1)

            def exp(turn, g, h, r):
                n = tile_number(turn, g, h, r)
                if r == 0:
                    act.wait_ge(top_ready, (G * turn + g) * heads + h + 1)
                wait(act, pT_ready, n - R + 1)
                if h == 0 and r == 0:
                    wait(act, out_used, G * turn + g - G + 1)
                nc.scalar.activation(prob[:, r, :], score[:, (g * heads + h) % 2, r, :], ACT.Exp,
                                     bias=neg_top[:, (g * heads + h) % 2, r:r + 1],
                                     accum_out=rowsum[:, g, r, h:h + 1]).then_inc(prob_ready, 1)

            def copy_pT(turn, g, h, r):
                n = tile_number(turn, g, h, r)
                act.wait_ge(pT_ready, n + 1)
                if r == 0:
                    wait(act, out_done, n - R)
                nc.scalar.copy(probT[:, (g * heads + h) % 2, :, r, :], ps_pT[r % 2][:, :].rearrange("p (c i) -> p c i", c=R))\
                    .then_inc(pT_copied, 1)

            def elu_exp(turn, g):
                b = G * turn + g
                act.wait_ge(out_used, b + 1)
                nc.scalar.activation(neg[:, :], att[:, g % 2, :], ACT.Relu, scale=-1.0).then_inc(neg_ready, 1)
                act.wait_ge(neg_ready, b + 1)
                wait(act, x_done, b)
                nc.scalar.activation(eneg[:, :], neg[:, :], ACT.Exp, scale=-1.0).then_inc(eneg_ready, 1)

            act.wait_ge(wa_done, 1)
            nc.scalar.copy(wa[:, :], ps_wh[:, 0:P]).then_inc(wa_copied, 1)
            nc.scalar.copy(st_const[:, :], ps_wh[:, P:P + 1]).then_inc(wa_copied, 1)

            def step(turn, g, k):
                if b := graph_at(turn, g, k, XT_AT):
                    copy_xT(*b)
                if t := tile_at(turn, g, k, 0):
                    exp(*t)
                if b := graph_at(turn, g, k, NORM_AT):
                    normalize(*b)
                if b := graph_at(turn, g, k, ROWS_AT):
                    high_rows(*b)
                if b := graph_at(turn, g, k, COPY_WH_AT):
                    copy_wh(*b)
                if b := graph_at(turn, g, k, OUT_AT):
                    copy_outT(*b)
                if t := tile_at(turn, g, k, COPY_AT):
                    copy_pT(*t)
                if elu and (b := graph_at(turn, g, k, ELU_AT)):
                    elu_exp(*b)
            walk(act, step)

        @block.vector
        def _(dve):
            def graph_stats(turn, g):
                b = G * turn + g
                wait(dve, xn_ready, b - 1)
                if load:
                    dve.wait_ge(x_loaded[0], 16)
                    if not (isinstance(turn, int) and turn == 0 and g < 2):
                        dve.wait_ge(x_loaded[1], 16)
                for r in range(R):
                    ins = nc.vector.bn_stats(stats[:, g % 2, r, :], X[:, bass.ds(b * N + r * D, D)])
                ins.then_inc(dve_chain, 1)
                dve.wait_ge(dve_chain, b + 1)
                alone(dve, env["dve_passed"])
                for r in range(R):
                    ins = nc.vector.bn_aggr(aggr[:, g % 2, r, :], stats[:, g % 2, r, :])
                ins.then_inc(stats_ready, 1)

            def make_mask(turn, g):
                before = G // 2 * turn + g // 2
                dve.wait_ge(adj_loaded[g % 2], 16 * (before + 1))
                wait(dve, mask_stored[g % 2], 16 * before)
                nc.vector.tensor_scalar(mask[:, g % 2, :], adj_in[:, g % 2, :, :].rearrange("p r j -> p (r j)"),
                                        0.0, MASKED, ALU.is_le, ALU.mult).then_inc(mask_done, 1)

            def low_rows(turn, g):
                b = G * turn + g
                dve.wait_ge(rows_split, 3 * b + 1)
                for q in (32, 96):
                    nc.vector.scalar_tensor_tensor(rows[q:q + 32, :], ps_xT[q:q + 32, :], st_const[q:q + 32, :],
                                                   rows[q:q + 32, :].bitcast(F32), ALU.add, ALU.subtract)\
                        .then_inc(rows_split, 1)

            def scores(turn, g, h, r):
                n = tile_number(turn, g, h, r)
                dve.wait_ge(z_ready, n + 1)
                if h == 0 and r == 0:
                    if load:
                        dve.wait_ge(mask_done, G * turn + g + 1)
                    else:
                        dve.wait_ge(mask_loaded[g % 2], 16 * (G // 2 * turn + g // 2 + 1))
                wait(dve, prob_ready, n - 2 * R + 1)
                alone(dve, env["dve_passed"])
                u2 = (g * heads + h) % 2
                nc.vector.tensor_tensor_reduce(out=score[:, u2, r, :], in0=ps_z[r % 2][:, :],
                                               in1=mask[:, g % 2, r * N:(r + 1) * N],
                                               scale=1.0, scalar=-3.0e38, op0=ALU.add, op1=ALU.max,
                                               accum_out=z_max[:, u2, r:r + 1]).then_inc(scored, 1)

            def leaky(turn, g, h, r):
                n = tile_number(turn, g, h, r)
                u2 = (g * heads + h) % 2
                dve.wait_ge(scored, n + 1)
                nc.vector.scalar_tensor_tensor(score[:, u2, r, :], score[:, u2, r, :], SLOPE, score[:, u2, r, :],
                                               ALU.mult, ALU.max).then_inc(leaky_done, 1)

            def top(turn, g, h):
                u = (G * turn + g) * heads + h
                u2 = (g * heads + h) % 2
                nc.vector.tensor_scalar(z_low[:, :], z_max[:, u2, :], -SLOPE, None, ALU.mult).then_inc(leaky_done, 1)
                dve.wait_ge(leaky_done, (u + 1) * (R + 1))
                nc.vector.scalar_tensor_tensor(neg_top[:, u2, :], z_max[:, u2, :], -1.0, z_low[:, :], ALU.mult, ALU.min)\
                    .then_inc(top_ready, 1)

            def finish(turn, g):
                b = G * turn + g
                wait(dve, out_used, b)
                dve.wait_ge(prob_ready, (b + 1) * T)
                nc.vector.reciprocal(rinv[:, :, :], rowsum[:, g, :, :]).then_inc(finish_chain, 1)
                dve.wait_ge(finish_chain, links * b + 1)
                if node_mask is not None:
                    nc.vector.tensor_tensor(rinv[:, :, 0], rinv[:, :, 0], nm_sb[:, bass.ds(b * R, R)], ALU.mult)\
                        .then_inc(finish_chain, 1)
                    dve.wait_ge(finish_chain, links * b + 2)
                dve.wait_ge(back_ready, b + 1)
                if not elu:
                    wait(dve, x_done, b - 1)
                nc.vector.tensor_tensor(att[:, g % 2, :].rearrange("p (r h c) -> p r h c", r=R, h=heads),
                                        ps_wh[:, :].rearrange("p (r h c) -> p r h c", r=R, h=heads),
                                        rinv[:, :, :].unsqueeze(3).to_broadcast([P, R, heads, C]), ALU.mult)\
                    .then_inc(out_used, 1)

            def elu_update(turn, g):
                b = G * turn + g
                dve.wait_ge(eneg_ready, b + 1)
                dve.wait_ge(out_used, b + 1)
                nc.vector.scalar_tensor_tensor(att[:, g % 2, :], att[:, g % 2, :], 0.0, eneg[:, :], ALU.max, ALU.add)\
                    .then_inc(att_ready, 1)
                dve.wait_ge(att_ready, b + 1)
                nc.vector.scalar_tensor_tensor(X[:, bass.ts(b, N)], att[:, g % 2, :], -1.0, X[:, bass.ts(b, N)],
                                               ALU.add, ALU.add).then_inc(x_done, 1)

            finish_chain = sem("finish_chain")
            links = 2 if node_mask is not None else 1
            dve.wait_ge(w_loaded, n_loads)
            dve.wait_ge(wa_copied, 2)

            def step(turn, g, k):
                if b := graph_at(turn, g, k, STATS_AT):
                    graph_stats(*b)
                if t := tile_at(turn, g, k, SCORE_AT):
                    scores(*t)
                if load and (b := graph_at(turn, g, k, MASK_AT)):
                    make_mask(*b)
                if t := tile_at(turn, g, k, LEAKY_AT):
                    leaky(*t)
                    if t[3] == R - 1:
                        top(*t[:3])
                if b := graph_at(turn, g, k, SPLIT_AT):
                    low_rows(*b)
                if b := graph_at(turn, g, k, FINISH_AT):
                    finish(*b)
                if elu and (b := graph_at(turn, g, k, UPDATE_AT)):
                    elu_update(*b)
            walk(dve, step)
            dve.wait_ge(x_done, B)

        @block.tensor
        def _(pe):
            def transpose_x(turn, g):
                b = G * turn + g
                pe.wait_ge(xn_ready, b + 1)
                wait(pe, rows_split, 3 * b)
                for r in range(R):
                    ins = nc.tensor.transpose(ps_xT[:, r * P:(r + 1) * P], xn[:, g % 2, r, :], ident[:, :])
                ins.then_inc(xT_ready, 1)

            def rows_of(turn, g):
                b = G * turn + g
                pe.wait_ge(xT_copied, b + 1)
                nc.tensor.matmul(ps_xT[:, :], wa[:, :], xT[:, g, :], start=True, stop=True).then_inc(rows_ready, 1)

            def wh_of(turn, g):
                b = G * turn + g
                wait(pe, out_used, b - LAG + 1)
                for r in range(R):
                    ins = nc.tensor.matmul(ps_wh[:, r * P:(r + 1) * P], xT[:, g, r * P:(r + 1) * P], w_sb[:, :],
                                           start=True, stop=True)
                ins.then_inc(wh_ready, 1)

            def z_of(turn, g, h, r):
                n = tile_number(turn, g, h, r)
                if h == 0 and r == 0:
                    pe.wait_ge(sides_ready, G * turn + g + 1)
                wait(pe, scored, n - 1)
                nc.tensor.matmul(ps_z[r % 2][:, :], lhs[:, g % 2, h, r * P:(r + 1) * P], rhs[:, g % 2, :],
                                 start=True, stop=True).then_inc(z_ready, 1)

            def transpose_probs(turn, g, h, r):
                n = tile_number(turn, g, h, r)
                pe.wait_ge(prob_ready, n + 1)
                wait(pe, pT_copied, n - 1)
                for c in range(R):
                    ins = nc.tensor.transpose(ps_pT[r % 2][:, c * P:(c + 1) * P], prob[:, r, c * P:(c + 1) * P], ident[:, :])
                ins.then_inc(pT_ready, 1)

            def attend(turn, g, h, c):
                n = tile_number(turn, g, h, c)
                if h == 0 and c == 0:
                    wait(pe, outT_copied, G * turn + g - 1)
                    pe.wait_ge(wh_copied, G * turn + g + 1)
                if c == 0:
                    pe.wait_ge(pT_copied, n + R)
                nc.tensor.matmul(ps_outT[g % 2][h * C:(h + 1) * C, :], wh[:, g % 2, c, h * C:(h + 1) * C],
                                 probT[:, (g * heads + h) % 2, c, :, :].rearrange("p r i -> p (r i)"),
                                 start=c == 0, stop=c == R - 1).then_inc(out_done, 1)

            def turn_back(turn, g):
                b = G * turn + g
                pe.wait_ge(outT_copied, b + 1)
                wait(pe, out_used, b)
                copied = b + LAG
                pe.wait_ge(wh_copied, min(B, copied) if isinstance(copied, int) else copied)
                for r in range(R):
                    ins = nc.tensor.transpose(ps_wh[:, r * P:(r + 1) * P], outT[:, r * P:(r + 1) * P], ident[:, :])
                ins.then_inc(back_ready, 1)

            pe.wait_ge(w_loaded, n_loads)
            nc.tensor.matmul(ps_wh[:, 0:P], wt_sb[:, :], a_sb[:, :], start=True, stop=True)
            nc.tensor.matmul(ps_wh[:, P:P + 1], a_sb[:, :], bias_col[:, :] if bias is not None else a_sb[:, P - 1:P],
                             start=True, stop=True).then_inc(wa_done, 1)
            pe.wait_ge(wa_copied, 2)
            pe.wait_ge(consts, 2)

            def step(turn, g, k):
                if t := tile_at(turn, g, k, Z_AT):
                    z_of(*t)
                if b := graph_at(turn, g, k, ROWS_AT):
                    rows_of(*b)
                if t := tile_at(turn, g, k, ATTEND_AT):
                    attend(*t)
                if b := graph_at(turn, g, k, WH_AT):
                    wh_of(*b)
                if b := graph_at(turn, g, k, XT_AT):
                    transpose_x(*b)
                if b := graph_at(turn, g, k, BACK_AT):
                    turn_back(*b)
                if t := tile_at(turn, g, k, TRANS_AT):
                    transpose_probs(*t)
            walk(pe, step)


def moe_layer(nc, env, name, raw, raw_loaded, b1, b2, router, router_bias, hidden, keep_tokens=False, own_ln=None, split_h=True):
    X, ident = env["X"], env["ident"]
    HC = hidden // P
    NG = E * HC
    LAG = 4 if split_h else 2
    LATE = LAG + 1
    unit = NG // 8
    S_TRANSPOSE, S_LOGITS, S_TOP, S_TANH, S_COMBINE_W, S_COMB_T, S_COMB_SPLIT = [unit * k for k in range(7)]
    S_OUT = LATE + 2
    S_UPDATE = S_OUT + 1
    S_STATS, S_NORM, S_NORM2 = unit + 1, 5 * unit, 7 * unit
    HB, HR = (4, 8) if split_h else (4, 4)
    ctx = ExitStack()
    with ctx:
        def sb(n, shape, dt=F32):
            return ctx.enter_context(nc.sbuf_tensor(f"{name}_{n}", shape, dt))

        def pb(n):
            return ctx.enter_context(nc.psum_tensor(f"{name}_{n}", [P, 512], F32))

        sem = layer_semaphores(nc, ctx, name)

        w1h, w1l = sb("w1h", [P, E, hidden], F32R), sb("w1l", [P, E, hidden], F32R)
        w2_raw = raw[:, :, 1, :].rearrange("p e (c d) -> p e c d", d=D)
        w2h = sb("w2h", [P, E, HC, D], F32R) if split_h else w2_raw
        w2l = sb("w2l", [P, E, HC, D], F32R) if split_h else None
        b1_sb, b2_sb, wr_sb = sb("b1", [P, NG]), sb("b2", [P, E]), sb("wr", [P, E])
        iota = sb("iota", [P, R, E])
        sel = sb("sel", [64, E], F32R)
        comb_T = sb("comb_T", [64, 2, N], F32R)
        if router_bias is not None:
            rb_sb = sb("rb", [P, R, E])

        with ExitStack() as setup:
            def ssb(n, shape, dt=F32):
                return setup.enter_context(nc.sbuf_tensor(f"{name}_{n}", shape, dt))

            zero64 = ssb("zero64", [64, 2 * N])
            if own_ln:
                g_sb, lnb_sb = ssb("g", [P, E]), ssb("lnb", [P, E])
                ps_b = setup.enter_context(nc.psum_tensor(f"{name}_ps_b", [P, 512], F32))
            small_loaded, zeroed = sem("small_loaded"), sem("zeroed")
            bias_mm, scaled, high = sem("bias_mm"), sem("scaled"), sem("w_high")
            with nc.Block() as block:
                small = [(b1_sb[:, :], b1), (b2_sb[:, :], b2), (wr_sb[:, :], router)]
                if router_bias is not None:
                    small += [(rb_sb[:, r, :], router_bias.partition_broadcast(P)) for r in range(R)]
                if own_ln:
                    small += [(g_sb[:, :], own_ln[0]), (lnb_sb[:, :], own_ln[1])]

                @block.sync
                def _(sp):
                    for dst, src in small:
                        sp.dma_start(dst, src).then_inc(small_loaded, 16)

                @block.gpsimd
                def _(pool):
                    nc.gpsimd.iota(iota[:, :, :], pattern=[[0, R], [1, E]], base=0, channel_multiplier=0,
                                   allow_small_or_imprecise_dtypes=True)
                    nc.gpsimd.memset(zero64[:, :], 0.0).then_inc(zeroed, 1)

                @block.vector
                def _(dve):
                    dve.wait_ge(small_loaded, 16 * len(small))
                    dve.wait_ge(zeroed, 1)
                    nc.vector.tensor_copy(comb_T[:, :, :].rearrange("k h n -> k (h n)"), zero64[:, :])
                    nc.vector.tensor_tensor(sel[:, :], ident[0:64, 0:E], ident[0:64, 32:32 + E], ALU.add)
                    dve.wait_ge(raw_loaded, 16 * 2 * E)
                    if own_ln:
                        dve.wait_ge(bias_mm, 1)
                        for e in range(E):
                            nc.vector.tensor_scalar(raw[:, e, 0, :], raw[:, e, 0, :], g_sb[:, e:e + 1], None, ALU.mult)\
                              .then_inc(scaled, 1)
                    for e in range(E):
                        if own_ln:
                            dve.wait_ge(scaled, e + 1)
                        nc.vector.tensor_copy(w1h[:, e, :], raw[:, e, 0, :]).then_inc(high, 1)
                        if split_h:
                            nc.vector.tensor_copy(w2h[:, e, :, :], w2_raw[:, e, :, :]).then_inc(high, 1)
                    for e in range(E):
                        dve.wait_ge(high, (e + 1) * (2 if split_h else 1))
                        nc.vector.tensor_tensor(w1l[:, e, :], raw[:, e, 0, :], w1h[:, e, :].bitcast(F32), ALU.subtract)
                        if split_h:
                            nc.vector.tensor_tensor(w2l[:, e, :, :], w2_raw[:, e, :, :], w2h[:, e, :, :].bitcast(F32), ALU.subtract)
                    if own_ln:
                        nc.vector.tensor_tensor(b1_sb[:, :], b1_sb[:, :], ps_b[:, 0:NG], ALU.add)

                if own_ln:
                    @block.tensor
                    def _(pe):
                        pe.wait_ge(small_loaded, 16 * len(small))
                        pe.wait_ge(raw_loaded, 16 * 2 * E)
                        for e in range(E):
                            for c in range(HC):
                                ins = nc.tensor.matmul(ps_b[:, e * HC + c:e * HC + c + 1],
                                                       raw[:, e, 0, c * P:(c + 1) * P], lnb_sb[:, e:e + 1],
                                                       start=True, stop=True)
                        ins.then_inc(bias_mm, 1)

        stats, aggr, rstd = sb("stats", [P, 2, R, 6]), sb("aggr", [P, 2, R, 2]), sb("rstd", [P, 2, R])
        xn = sb("xn", [P, 2, R, P])
        xT = sb("xT", [P, N])
        if own_ln:
            stats2, aggr2, rstd2 = sb("stats2", [P, R, 6]), sb("aggr2", [P, R, 2]), sb("rstd2", [P, R])
            xn2 = sb("xn2", [P, 2, R, P])
            xT2 = sb("xT2", [P, N])
        xe = xT2 if own_ln else xT
        xh, xl = sb("xh", [P, 2, N], F32R), sb("xl", [P, 2, N], F32R)
        logit, best, best_at = sb("logit", [P, R, E]), sb("best", [P, R, E]), sb("best_at", [P, R, E], U32)
        at_f = sb("at_f", [P, R, 2])
        gap, tanh_gap = sb("gap", [P, R]), sb("tanh_gap", [P, R])
        weight = sb("weight", [P, 2, R])
        hot = sb("hot", [P, 2, R, E])
        comb = sb("comb", [P, R, E])
        h = sb("h", [P, HB, N])
        hh = sb("hh", [P, HR, N], F32R) if split_h else None
        hl = sb("hl", [P, HR, N], F32R) if split_h else None
        w_rows = sb("w_rows", [P, 2, N])
        scaled_y = sb("scaled_y", [P, 2, N])
        acc = sb("acc", [P, 2, N])

        ps_h = [pb(f"ps_h{i}") for i in range(2)]
        ps_y = [pb(f"ps_y{i}") for i in range(2)]
        ps_w, ps_xT, ps_small, ps_out = pb("ps_w"), pb("ps_xT"), pb("ps_small"), pb("ps_out")

        high_done = sem("high_done")
        stats_ready, rstd_ready, xn_ready = sem("stats_ready"), sem("rstd_ready"), sem("xn_ready")
        stats2_ready, rstd2_ready, xn2_ready = sem("stats2_ready"), sem("rstd2_ready"), sem("xn2_ready")
        xT_ready, xT_copied = sem("xT_ready"), sem("xT_copied")
        x_split, logits_ready, gap_ready, tanh_ready = sem("x_split"), sem("logits_ready"), sem("gap_ready"), sem("tanh_ready")
        comb_ready, combT_ready, combT_split = sem("comb_ready"), sem("combT_ready"), sem("combT_split")
        h_ready, gelu_done, h_split, y_chunk = sem("h_ready"), sem("gelu_done"), sem("h_split"), sem("y_chunk")
        w_ready, w_copied, y_scaled, added = sem("w_ready"), sem("w_copied"), sem("y_scaled"), sem("added")
        out_ready, x_done = sem("out_ready"), sem("x_done")
        dve_chain, pool_chain = sem("dve_chain"), sem("pool_chain")

        def steps(pair, half):
            first = isinstance(pair, int) and pair == 0 and half == 0
            last = isinstance(pair, int) and pair == PAIRS - 1 and half == 1
            nxt = (pair, 1) if half == 0 else (pair + 1, 0)
            prev = (pair, 0) if half == 1 else (pair - 1, 1)
            return first, last, nxt, prev

        block = ctx.enter_context(nc.Block())

        @block.gpsimd
        def _(pool):
            chain = Chain(pool, pool_chain, 0)

            def rstd_of(pair, half):
                b = 2 * pair + half
                pool.wait_ge(stats_ready, b + 1)
                chain.link(nc.gpsimd.tensor_tensor(rstd[:, half, :], aggr[:, half, :, 1], env["eps"][:, :], ALU.add))
                nc.gpsimd.tensor_tensor(rstd[:, half, :], rstd[:, half, :], env["minus_half"][:, :], ALU.pow)\
                  .then_inc(rstd_ready, 1)

            def add_tokens(pair, half):
                if keep_tokens:
                    b = 2 * pair + half
                    pool.wait_ge(xn_ready, b + 1)
                    alone(pool, env["pool_passed"])
                    chain.link(nc.gpsimd.tensor_tensor(X[:, bass.ts(b, N)], X[:, bass.ts(b, N)],
                                                       xn[:, half, :, :].rearrange("p r d -> p (r d)"), ALU.add))

            def rstd2_of(pair, half):
                pool.wait_ge(stats2_ready, 2 * pair + half + 1)
                chain.link(nc.gpsimd.tensor_tensor(rstd2[:, :], aggr2[:, :, 1], env["eps"][:, :], ALU.add))
                nc.gpsimd.tensor_tensor(rstd2[:, :], rstd2[:, :], env["minus_half"][:, :], ALU.pow).then_inc(rstd2_ready, 1)

            def add_expert(pair, half, e):
                n = (2 * pair + half) * E + e
                if e == 0:
                    return
                pool.wait_ge(y_scaled, n + 1)
                if e == 1:
                    wait(pool, out_ready, 2 * pair + half - 1)
                    nc.gpsimd.tensor_tensor(acc[:, half, :], scaled_y[:, 0, :], scaled_y[:, 1, :], ALU.add)\
                      .then_inc(added, 2)
                else:
                    pool.wait_ge(added, n)
                    nc.gpsimd.tensor_tensor(acc[:, half, :], acc[:, half, :], scaled_y[:, e % 2, :], ALU.add)\
                      .then_inc(added, 1)

            for half in range(2):
                rstd_of(0, half)
            for half in range(2):
                add_tokens(0, half)
                if own_ln:
                    rstd2_of(0, half)
            chain.end_prologue()
            chain.per_pair = 2 + (2 if own_ln else 0) + (2 if keep_tokens else 0)

            def body(pair):
                last_pair = isinstance(pair, int) and pair == PAIRS - 1
                chain.pair(pair)
                for half in range(2):
                    first, last, nxt, prev = steps(pair, half)
                    for e in range(E):
                        add_expert(pair, half, e)
                        if e == 1 and not last_pair:
                            rstd_of(pair + 1, half)
                        if e == 4 and not last_pair:
                            add_tokens(pair + 1, half)
                            if own_ln:
                                rstd2_of(pair + 1, half)
                if not last_pair:
                    chain.end_pair()
            pairs(pool, body)

        @block.scalar
        def _(act):
            def front(pair, half):
                b = 2 * pair + half
                act.wait_ge(xT_ready, b + 1)
                wait(act, logits_ready, b)
                if not own_ln:
                    wait(act, x_split, b)
                nc.scalar.copy(xT[:, :], ps_xT[:, :]).then_inc(xT_copied, 1)
                if own_ln:
                    act.wait_ge(xT_ready, b + 1)
                    wait(act, x_split, b)
                    nc.scalar.copy(xT2[:, :], ps_out[:, :]).then_inc(xT_copied, 1)

            def gap_tanh(pair, half):
                act.wait_ge(gap_ready, 2 * pair + half + 1)
                nc.scalar.activation(tanh_gap[:, :], gap[:, :], ACT.Tanh, scale=0.5).then_inc(tanh_ready, 1)

            def gelu(pair, half, g):
                n = (2 * pair + half) * NG + g
                act.wait_ge(h_ready, n + 1)
                wait(act, h_split if split_h else y_chunk, n - HB + 1)
                nc.scalar.activation(h[:, g % HB, :], ps_h[g % 2][:, :], ACT.Gelu,
                                     bias=b1_sb[:, g:g + 1]).then_inc(gelu_done, 1)

            def copy_w(n, e):
                act.wait_ge(w_ready, n + 1)
                wait(act, y_scaled, n - 1)
                nc.scalar.copy(w_rows[:, e % 2, :], ps_w[:, :]).then_inc(w_copied, 1)

            front(0, 0)
            gap_tanh(0, 0)

            def body(pair):
                for half in range(2):
                    first, last, nxt, prev = steps(pair, half)
                    for g in range(NG):
                        gelu(pair, half, g)
                        if (g - LAG) % HC == 0 and not (first and g < LAG):
                            copy_w((2 * pair + half) * E + (g - LAG) // HC, (g - LAG) // HC)
                        if not last and g == S_TRANSPOSE:
                            front(*nxt)
                        if not last and g == S_TANH:
                            gap_tanh(*nxt)
            pairs(act, body)
            for g in range(LAG):
                if (g - LAG) % HC == 0:
                    copy_w(B * E + (g - LAG) // HC, (g - LAG) // HC)

        @block.vector
        def _(dve):
            chain = Chain(dve, dve_chain, 0)

            def graph_stats(pair, half):
                b = 2 * pair + half
                wait(dve, xn_ready, b - 1)
                for r in range(R):
                    ins = nc.vector.bn_stats(stats[:, half, r, :], X[:, bass.ds(b * N + r * D, D)])
                chain.link(ins)
                alone(dve, env["dve_passed"])
                for r in range(R):
                    ins = nc.vector.bn_aggr(aggr[:, half, r, :], stats[:, half, r, :])
                ins.then_inc(stats_ready, 1)

            def graph_stats2(pair, half):
                b = 2 * pair + half
                dve.wait_ge(xn_ready, b + 1)
                wait(dve, xn2_ready, b)
                for r in range(R):
                    ins = nc.vector.bn_stats(stats2[:, r, :], xn[:, half, r, :])
                chain.link(ins)
                alone(dve, env["dve_passed"])
                for r in range(R):
                    ins = nc.vector.bn_aggr(aggr2[:, r, :], stats2[:, r, :])
                ins.then_inc(stats2_ready, 1)

            def normalize(pair, half):
                b = 2 * pair + half
                dve.wait_ge(rstd_ready, b + 1)
                wait(dve, xT_ready, b - 1)
                for r in range(R):
                    ins = nc.vector.tensor_scalar(xn[:, half, r, :], X[:, bass.ds(b * N + r * D, D)],
                                                  aggr[:, half, r, 0:1], rstd[:, half, r:r + 1], ALU.subtract, ALU.mult)
                ins.then_inc(xn_ready, 1)

            def normalize2(pair, half):
                b = 2 * pair + half
                dve.wait_ge(rstd2_ready, b + 1)
                for r in range(R):
                    ins = nc.vector.tensor_scalar(xn2[:, half, r, :], xn[:, half, r, :],
                                                  aggr2[:, r, 0:1], rstd2[:, r:r + 1], ALU.subtract, ALU.mult)
                ins.then_inc(xn2_ready, 1)

            def split_x(pair, half):
                b = 2 * pair + half
                dve.wait_ge(xT_copied, (b + 1) * (2 if own_ln else 1))
                wait(dve, h_ready, (b - 1) * NG)
                chain.link(nc.vector.tensor_copy(xh[:, half, :], xe[:, :]))
                nc.vector.tensor_tensor(xl[:, half, :], xe[:, :], xh[:, half, :].bitcast(F32), ALU.subtract)\
                  .then_inc(x_split, 1)

            def top_two(pair, half):
                b = 2 * pair + half
                dve.wait_ge(logits_ready, b + 1)
                lv = logit[:, :, :].rearrange("p r e -> p (r e)")
                if router_bias is not None:
                    ins = nc.vector.tensor_tensor(lv, ps_small[:, 0:R * E], rb_sb[:, :, :].rearrange("p r e -> p (r e)"),
                                                  ALU.add)
                else:
                    ins = nc.vector.tensor_copy(lv, ps_small[:, 0:R * E])
                chain.link(ins)
                alone(dve, env["dve_passed"])
                for r in range(R):
                    ins = nc.vector.max(best[:, r, :], logit[:, r, :])
                chain.link(ins)
                alone(dve, env["dve_passed"])
                for r in range(R):
                    ins = nc.vector.max_index(best_at[:, r, :], best[:, r, :], logit[:, r, :])
                nc.vector.tensor_tensor(gap[:, :], best[:, :, 0], best[:, :, 1], ALU.subtract).then_inc(gap_ready, 1)

            def weights(pair, half):
                b = 2 * pair + half
                dve.wait_ge(gap_ready, b + 1)
                chain.link(nc.vector.tensor_copy(at_f[:, :, :], best_at[:, :, 0:2]))
                dve.wait_ge(tanh_ready, b + 1)
                nc.vector.tensor_scalar(weight[:, 0, :], tanh_gap[:, :], 0.5, 0.5, ALU.mult, ALU.add)
                nc.vector.tensor_scalar(weight[:, 1, :], tanh_gap[:, :], -0.5, 0.5, ALU.mult, ALU.add)
                for k in range(2):
                    ins = nc.vector.tensor_tensor(hot[:, k, :, :], iota[:, :, :],
                                                  at_f[:, :, k:k + 1].to_broadcast([P, R, E]), ALU.is_equal)
                chain.link(ins)
                for k in range(2):
                    ins = nc.vector.tensor_tensor(hot[:, k, :, :], hot[:, k, :, :],
                                                  weight[:, k, :].unsqueeze(2).to_broadcast([P, R, E]), ALU.mult)
                chain.link(ins)
                nc.vector.tensor_tensor(comb[:, :, :], hot[:, 0, :, :], hot[:, 1, :, :], ALU.add).then_inc(comb_ready, 1)

            def split_comb(pair, half):
                b = 2 * pair + half
                dve.wait_ge(combT_ready, b + 1)
                wait(dve, w_ready, (b - 1) * E)
                chain.link(nc.vector.tensor_copy(comb_T[0:E, half, :], ps_small[0:E, :]))
                nc.vector.tensor_tensor(comb_T[32:32 + E, half, :], ps_small[0:E, :], comb_T[0:E, half, :].bitcast(F32),
                                        ALU.subtract).then_inc(combT_split, 1)

            def high_part(pair, half, g):
                n = (2 * pair + half) * NG + g
                dve.wait_ge(gelu_done, n + 1)
                wait(dve, y_chunk, n - HR + 1)
                nc.vector.tensor_copy(hh[:, g % HR, :], h[:, g % HB, :]).then_inc(high_done, 1)

            def low_part(n, g):
                dve.wait_ge(high_done, n + 1)
                nc.vector.tensor_tensor(hl[:, g % HR, :], h[:, g % HB, :], hh[:, g % HR, :].bitcast(F32), ALU.subtract)\
                  .then_inc(h_split, 1)

            def combine(n, e):
                dve.wait_ge(y_chunk, (n + 1) * HC)
                dve.wait_ge(w_copied, n + 1)
                wait(dve, added, n - 1)
                nc.vector.scalar_tensor_tensor(scaled_y[:, e % 2, :], ps_y[e % 2][:, :], b2_sb[:, e:e + 1],
                                               w_rows[:, e % 2, :], ALU.add, ALU.mult).then_inc(y_scaled, 1)

            def update(pair, half):
                b = 2 * pair + half
                dve.wait_ge(out_ready, b + 1)
                nc.vector.tensor_tensor(X[:, bass.ts(b, N)], X[:, bass.ts(b, N)], ps_out[:, :], ALU.add)\
                  .then_inc(x_done, 1)

            graph_stats(0, 0)
            graph_stats(0, 1)
            for half in range(2):
                normalize(0, half)
                if own_ln:
                    graph_stats2(0, half)
                    normalize2(0, half)
            split_x(0, 0)
            top_two(0, 0)
            weights(0, 0)
            split_comb(0, 0)
            chain.end_prologue()
            chain.per_pair = 2 + (2 if own_ln else 0) + 2 * (1 + 2 + 3 + 1)

            def body(pair):
                last_pair = isinstance(pair, int) and pair == PAIRS - 1
                chain.pair(pair)
                for half in range(2):
                    first, last, nxt, prev = steps(pair, half)
                    for g in range(NG):
                        if split_h:
                            high_part(pair, half, g)
                            if not (first and g == 0):
                                low_part((2 * pair + half) * NG + g - 1, (g - 1) % NG)
                        else:
                            dve.wait_ge(gelu_done, (2 * pair + half) * NG + g + 1)
                        done = g - LATE + 1
                        if done % HC == 0 and not (first and done <= 0):
                            combine((2 * pair + half) * E + done // HC - 1, (done // HC - 1) % E)
                        if g == S_UPDATE and not first:
                            update(*prev)
                        if not last:
                            if g == S_TRANSPOSE:
                                split_x(*nxt)
                            if g == S_TOP:
                                top_two(*nxt)
                            if g == S_COMBINE_W:
                                weights(*nxt)
                            if g == S_COMB_SPLIT:
                                split_comb(*nxt)
                        if g == S_STATS and not last_pair:
                            graph_stats(pair + 1, half)
                        if g == S_NORM and not last_pair:
                            normalize(pair + 1, half)
                            if own_ln:
                                graph_stats2(pair + 1, half)
                        if g == S_NORM2 and own_ln and not last_pair:
                            normalize2(pair + 1, half)
                if not last_pair:
                    chain.end_pair()
            pairs(dve, body)
            if split_h:
                low_part(B * NG - 1, NG - 1)
            for done in range(NG - LATE + 1, NG + 1):
                if done % HC == 0:
                    combine((B - 1) * E + done // HC - 1, done // HC - 1)
            update(PAIRS - 1, 1)
            dve.wait_ge(x_done, B)

        @block.tensor
        def _(pe):
            def transposes(pair, half):
                b = 2 * pair + half
                pe.wait_ge(xn_ready, b + 1)
                for r in range(R):
                    ins = nc.tensor.transpose(ps_xT[:, r * P:(r + 1) * P], xn[:, half, r, :], ident[:, :])
                if own_ln:
                    pe.wait_ge(xn2_ready, b + 1)
                    wait(pe, x_done, b - 2)
                    for r in range(R):
                        ins = nc.tensor.transpose(ps_out[:, r * P:(r + 1) * P], xn2[:, half, r, :], ident[:, :])
                ins.then_inc(xT_ready, 1)

            def logits(pair, half):
                b = 2 * pair + half
                pe.wait_ge(xT_copied, (b + 1) * (2 if own_ln else 1))
                wait(pe, combT_split, b)
                for r in range(R):
                    ins = nc.tensor.matmul(ps_small[:, r * E:(r + 1) * E], xT[:, r * P:(r + 1) * P], wr_sb[:, :],
                                           start=True, stop=True)
                ins.then_inc(logits_ready, 1)

            def transpose_comb(pair, half):
                pe.wait_ge(comb_ready, 2 * pair + half + 1)
                for r in range(R):
                    ins = nc.tensor.transpose(ps_small[0:E, r * P:(r + 1) * P], comb[:, r, :], ident[:, :])
                ins.then_inc(combT_ready, 1)

            def first_product(pair, half, g):
                n = (2 * pair + half) * NG + g
                if g == 0:
                    pe.wait_ge(x_split, 2 * pair + half + 1)
                wait(pe, gelu_done, n - 1)
                e, c = g // HC, g % HC
                cols = slice(c * P, (c + 1) * P)
                nc.tensor.matmul(ps_h[g % 2][:, :], w1h[:, e, cols], xh[:, half, :], start=True, stop=False)
                nc.tensor.matmul(ps_h[g % 2][:, :], w1h[:, e, cols], xl[:, half, :], start=False, stop=False)
                nc.tensor.matmul(ps_h[g % 2][:, :], w1l[:, e, cols], xh[:, half, :], start=False, stop=True)\
                  .then_inc(h_ready, 1)

            def second_product(n, g, half):
                e, c = g // HC, g % HC
                slot = g % HR
                y = ps_y[e % 2]
                if split_h:
                    pe.wait_ge(h_split, n + 1)
                    nc.tensor.matmul(y[:, :], w2h[:, e, c, :], hh[:, slot, :], start=c == 0, stop=False)
                    nc.tensor.matmul(y[:, :], w2h[:, e, c, :], hl[:, slot, :], start=False, stop=False)
                    nc.tensor.matmul(y[:, :], w2l[:, e, c, :], hh[:, slot, :], start=False, stop=c == HC - 1)\
                      .then_inc(y_chunk, 1)
                else:
                    pe.wait_ge(gelu_done, n + 1)
                    nc.tensor.matmul(y[:, :], w2h[:, e, c, :], h[:, slot, :], start=c == 0, stop=c == HC - 1)\
                      .then_inc(y_chunk, 1)

            def lagged(pair, half, g):
                b = 2 * pair + half
                lg = g - LAG
                n = b * NG + lg
                if lg < 0:
                    lg, lb, lh = lg + NG, b - 1, 1 - half
                else:
                    lb, lh = b, half
                e = lg // HC
                if lg % HC == 0:
                    if e == 0:
                        pe.wait_ge(combT_split, lb + 1)
                    en = lb * E + e
                    wait(pe, w_copied, en)
                    nc.tensor.matmul(ps_w[:, :], sel[:, e:e + 1].to_broadcast([64, P]), comb_T[:, lh, :], start=True, stop=True)\
                      .then_inc(w_ready, 1)
                    wait(pe, y_scaled, en - 1)
                second_product(n, lg, lh)

            def transpose_out(pair, half):
                b = 2 * pair + half
                pe.wait_ge(added, (b + 1) * E)
                wait(pe, x_done, b)
                for r in range(R):
                    ins = nc.tensor.transpose(ps_out[:, r * P:(r + 1) * P], acc[:, half, r * P:(r + 1) * P], ident[:, :])
                ins.then_inc(out_ready, 1)

            transposes(0, 0)
            logits(0, 0)
            transpose_comb(0, 0)

            def body(pair):
                for half in range(2):
                    first, last, nxt, prev = steps(pair, half)
                    for g in range(NG):
                        first_product(pair, half, g)
                        if not (first and g < LAG):
                            lagged(pair, half, g)
                        if g == S_OUT and not first:
                            transpose_out(*prev)
                        if not last:
                            if g == S_TRANSPOSE:
                                transposes(*nxt)
                            if g == S_LOGITS:
                                logits(*nxt)
                            if g == S_COMB_T:
                                transpose_comb(*nxt)
            pairs(pe, body)
            for g in range(LAG):
                lagged(PAIRS, 0, g)
            transpose_out(PAIRS - 1, 1)


def mamba_layer(nc, env, name, w_in, conv_w, conv_b, dt_bias, a_log, d_skip, norm_w, w_out_t, w_lin, b_lin):
    X, ident = env["X"], env["ident"]
    INNER, STATE, HEADS, HEAD, TAPS = 256, 64, 4, 64, 4
    XBC = INNER + 2 * STATE
    CC = XBC // P
    RMS_EPS = 1e-5
    PAD = 4
    RH = R * HEADS
    ctx = ExitStack()
    with ctx:
        def sb(n, shape, dt=F32):
            return ctx.enter_context(nc.sbuf_tensor(f"{name}_{n}", shape, dt))

        def pb(n):
            return ctx.enter_context(nc.psum_tensor(f"{name}_{n}", [P, 512], F32))

        sem = layer_semaphores(nc, ctx, name)

        wch, wcl = sb("wch", [P, TAPS, XBC], F32R), sb("wcl", [P, TAPS, XBC], F32R)
        wz, wdt_sb = sb("wz", [P, INNER]), sb("wdt", [P, HEADS])
        wo = sb("wo", [P, 2, D])
        half_cb = sb("half_cb", [P, CC])
        dtb, a_neg = sb("dtb", [P, R, HEADS]), sb("a_neg", [P, R, HEADS])
        d_row = sb("d_row", [P, HEADS, HEAD])
        b_row = sb("b_row", [P, R, D])
        rms_eps = sb("rms_eps", [P, 1])
        ones, tri, strict = sb("ones", [P, P]), sb("tri", [P, P]), sb("strict", [P, P])
        xh, xl = sb("xh", [P, PAD + N], F32R), sb("xl", [P, PAD + N], F32R)

        with ExitStack() as setup:
            def ssb(n, shape, dt=F32):
                return setup.enter_context(nc.sbuf_tensor(f"{name}_{n}", shape, dt))

            w_xbc, cw_row, w_tap = ssb("w_xbc", [P, XBC]), ssb("cw_row", [P, TAPS, XBC]), ssb("w_tap", [P, TAPS, XBC])
            wot, wlin, nw = ssb("wot", [P, INNER]), ssb("wlin", [P, D]), ssb("nw", [P, 2])
            d_in, cb_in = ssb("d_in", [P, HEADS]), ssb("cb_in", [P, CC])
            zeros = ssb("zeros", [P, PAD])
            ps_w = setup.enter_context(nc.psum_tensor(f"{name}_ps_w", [P, 512], F32))
            loaded, masks, prep, wo_mm, a_exp = [sem(n) for n in ("loaded", "masks", "prep", "wo_mm", "a_exp")]
            loads = [(w_xbc[:, :], w_in[:, INNER:INNER + XBC]), (wz[:, :], w_in[:, 0:INNER]),
                     (wdt_sb[:, :], w_in[:, INNER + XBC:]), (wot[:, :], w_out_t), (wlin[:, :], w_lin),
                     (nw[:, :], norm_w), (cb_in[:, :], conv_b), (d_in[:, :], d_skip.partition_broadcast(P))]
            loads += [(cw_row[:, k, :], conv_w[k].partition_broadcast(P)) for k in range(TAPS)]
            for r in range(R):
                loads += [(dtb[:, r, :], dt_bias.partition_broadcast(P)), (a_neg[:, r, :], a_log.partition_broadcast(P)),
                          (b_row[:, r, :], b_lin.partition_broadcast(P))]
            with nc.Block() as block:
                @block.sync
                def _(sp):
                    for dst, src in loads:
                        sp.dma_start(dst, src).then_inc(loaded, 16)

                @block.gpsimd
                def _(pool):
                    nc.gpsimd.memset(zeros[:, :], 0.0)
                    nc.gpsimd.memset(rms_eps[:, :], RMS_EPS * INNER)
                    nc.gpsimd.memset(ones[:, :], 1.0).then_inc(masks, 1)
                    pool.wait_ge(masks, 1)
                    nc.gpsimd.affine_select(out=tri[:, :], in_=ones[:, :], compare_op=ALU.is_ge, fill=0.0,
                                            base=0, pattern=[[1, P]], channel_multiplier=-1).then_inc(masks, 1)

                @block.scalar
                def _(act):
                    act.wait_ge(loaded, 16 * len(loads))
                    nc.scalar.activation(a_neg[:, :, :], a_neg[:, :, :], ACT.Exp).then_inc(a_exp, 1)
                    nc.scalar.mul(half_cb[:, :], cb_in[:, :], 0.5)

                @block.tensor
                def _(pe):
                    pe.wait_ge(loaded, 16 * len(loads))
                    for k in range(2):
                        ins = nc.tensor.matmul(ps_w[:, k * D:(k + 1) * D], wot[:, k * P:(k + 1) * P], wlin[:, :],
                                               start=True, stop=True)
                    ins.then_inc(wo_mm, 1)

                @block.vector
                def _(dve):
                    dve.wait_ge(masks, 2)
                    nc.vector.tensor_tensor(strict[:, :], tri[:, :], ident[:, :], ALU.subtract)
                    nc.vector.tensor_copy(xh[:, 0:PAD], zeros[:, :])
                    nc.vector.tensor_copy(xl[:, 0:PAD], zeros[:, :])
                    dve.wait_ge(loaded, 16 * len(loads))
                    for k in range(TAPS):
                        ins = nc.vector.tensor_tensor(w_tap[:, k, :], w_xbc[:, :], cw_row[:, k, :], ALU.mult)
                    ins.then_inc(prep, 1)
                    dve.wait_ge(prep, 1)
                    nc.vector.tensor_copy(wch[:, :, :], w_tap[:, :, :]).then_inc(prep, 1)
                    dve.wait_ge(prep, 2)
                    nc.vector.tensor_tensor(wcl[:, :, :], w_tap[:, :, :], wch[:, :, :].bitcast(F32), ALU.subtract)
                    nc.vector.tensor_copy(d_row[:, :, :], d_in[:, :].unsqueeze(2).to_broadcast([P, HEADS, HEAD]))
                    dve.wait_ge(wo_mm, 1)
                    for k in range(2):
                        nc.vector.tensor_scalar(wo[:, k, :], ps_w[:, k * D:(k + 1) * D], nw[:, k:k + 1], float(INNER) ** 0.5,
                                                ALU.mult, ALU.mult)
                    dve.wait_ge(a_exp, 1)
                    nc.vector.tensor_scalar(a_neg[:, :, :], a_neg[:, :, :], -1.0, None, ALU.mult)

        stats, aggr, rstd = sb("stats", [P, 2, R, 6]), sb("aggr", [P, 2, R, 2]), sb("rstd", [P, 2, R])
        xn = sb("xn", [P, 2, R, P])
        xT = sb("xT", [P, N])
        th, hv = sb("th", [P, 2, N]), sb("hv", [P, 2, N])
        xc = sb("xc", [P, 2, 2, N])
        BT, CT = sb("BT", [STATE, 2, N]), sb("CT", [STATE, 2, N])
        zg = sb("zg", [P, 2, R, INNER])
        dt_raw, dt_abs, dt_exp, dt_ln = [sb(n, [P, RH]) for n in ("dt_raw", "dt_abs", "dt_exp", "dt_ln")]
        dt, dA = sb("dt", [P, 2, RH]), sb("dA", [P, 2, RH])
        acum, exp_acum = sb("acum", [P, 2, RH]), sb("exp_acum", [P, 2, RH])
        rest, exp_rest = sb("rest", [P, RH]), sb("exp_rest", [P, RH])
        exp_total, dt_rest = sb("exp_total", [P, 2, RH]), sb("dt_rest", [P, 2, RH])
        diff, ediff = sb("diff", [P, HEADS, P]), sb("ediff", [P, HEADS, P])
        cb_m = sb("cb_m", [P, P])
        mix = sb("mix", [P, 2, HEADS, P])
        xB = sb("xB", [P, 2, INNER + STATE])
        xdt, xrest, xD = sb("xdt", [P, 2, INNER]), sb("xrest", [P, 2, INNER]), sb("xD", [P, 2, INNER])
        state, decayed = sb("state", [STATE, INNER]), sb("decayed", [STATE, INNER])
        y_part, y, gated = sb("y_part", [P, INNER]), sb("y", [P, INNER]), sb("gated", [P, 2, INNER])
        squares = sb("squares", [P, 2, INNER])
        sumsq, rms = sb("sumsq", [P, 2]), sb("rms", [P, 2])
        gT = sb("gT", [P, 2, INNER])
        minus_half1 = env["minus_half"][:, 0:1]

        ps_f = [pb("ps_f0"), pb("ps_f1")]
        ps_bc, ps_c1, ps_c2, ps_s, ps_small, ps_c3 = [pb(n) for n in ("ps_bc", "ps_c1", "ps_c2", "ps_s", "ps_small", "ps_c3")]

        (stats_ready, rstd_ready, xn_ready, f_ready, f_read, x_split, conv_act, silu_done, dtm_ready, dt_pre, dt_ln_done, dA_ready,
         cum_ready, cum_act, cum_dve, rest_exp, front_done, c1_ready, c1_copied, diff_ready, ediff_ready, mix_ready,
         c2_ready, state_done, decay_done, gated_ready, sq_done, rms_ready, gT_ready, gT_copied, o_ready, x_done, xD_ready,
         z_act, zg_ready, dve_chain, pool_chain) = [sem(n) for n in (
             "stats_ready rstd_ready xn_ready f_ready f_read x_split conv_act silu_done dtm_ready dt_pre dt_ln_done dA_ready "
             "cum_ready cum_act cum_dve rest_exp front_done c1_ready c1_copied diff_ready ediff_ready mix_ready "
             "c2_ready state_done decay_done gated_ready sq_done rms_ready gT_ready gT_copied o_ready x_done xD_ready "
             "z_act zg_ready dve_chain pool_chain").split()]
        FU = 1 + CC + 2

        block = ctx.enter_context(nc.Block())

        PREP_AT, PROJECT_AT, UPDATE_AT = 2, -1, -2
        STATS_AT, NORM_AT, XT_AT, CONV_AT, SUMS_AT, Z_AT = 8, 6, 5, (5, 4, 3), 3, 2
        SILU_AT, DT_AT, DT2_AT, CUM2_AT, ZG_AT, BIAS_AT = (4, 3, 2), 4, 3, 2, 1, 6

        def tile_at(pair, half, r, ahead):
            turn, rest = divmod(half * R + r + ahead, 2 * R)
            if isinstance(pair, int) and not 0 <= pair + turn < PAIRS:
                return None
            b = 2 * (pair + turn) + rest // R
            return b * R + rest % R, b, rest // R, rest % R

        def graph_at(pair, half, r, ahead):
            t = tile_at(pair, half, r, ahead)
            return t[1:3] if t and t[3] == 0 else None

        def walk(eng, step, chain=None):
            def turn(pair):
                if chain:
                    chain.pair(pair)
                for k in range(2 * R):
                    step(pair, k // R, k % R)
            for k in range(-STATS_AT, 0):
                step(0, 0, k)
            if chain:
                chain.end_prologue()
            turn(0)
            with eng.Fori(1, PAIRS - 1) as pair:
                turn(pair)
                if chain:
                    chain.end_pair()
            turn(PAIRS - 1)
            for k in range(-UPDATE_AT):
                step(PAIRS, 0, k)

        @block.gpsimd
        def _(pool):
            chain = Chain(pool, pool_chain, 0)

            def rstd_of(b, half):
                pool.wait_ge(stats_ready, b + 1)
                chain.link(nc.gpsimd.tensor_tensor(rstd[:, half, :], aggr[:, half, :, 1], env["eps"][:, :], ALU.add))
                nc.gpsimd.tensor_tensor(rstd[:, half, :], rstd[:, half, :], env["minus_half"][:, :], ALU.pow)\
                  .then_inc(rstd_ready, 1)

            def add_bias(b, half):
                pool.wait_ge(xn_ready, b + 1)
                alone(pool, env["pool_passed"])
                chain.link(nc.gpsimd.tensor_tensor(X[:, bass.ts(b, N)], X[:, bass.ts(b, N)],
                                                   b_row[:, :, :].rearrange("p r d -> p (r d)"), ALU.add))

            def skip(n, s):
                pool.wait_ge(c1_copied, n + 1)
                wait(pool, gated_ready, n - 1)
                nc.gpsimd.tensor_tensor(xD[:, s, :], xB[:, s, 0:INNER], d_row[:, :, :].rearrange("p h c -> p (h c)"), ALU.mult)\
                    .then_inc(xD_ready, 1)

            def rms_of(n, s):
                pool.wait_ge(sq_done, n + 1)
                chain.link(nc.gpsimd.tensor_tensor(rms[:, s:s + 1], sumsq[:, s:s + 1], rms_eps[:, :], ALU.add))
                nc.gpsimd.tensor_tensor(rms[:, s:s + 1], rms[:, s:s + 1], minus_half1, ALU.pow).then_inc(rms_ready, 1)

            chain.per_pair = 2 * 2 + 2 * R

            def step(pair, half, r):
                if b := graph_at(pair, half, r, STATS_AT):
                    rstd_of(*b)
                if t := tile_at(pair, half, r, PREP_AT):
                    skip(t[0], t[3] % 2)
                if t := tile_at(pair, half, r, 0):
                    rms_of(t[0], t[3] % 2)
                if b := graph_at(pair, half, r, BIAS_AT):
                    add_bias(*b)
            walk(pool, step, chain)


        @block.scalar
        def _(act):
            def copy_xT(b):
                act.wait_ge(f_ready, b * FU + 1)
                wait(act, x_split, b)
                wait(act, f_ready, (b - 1) * FU + FU)
                nc.scalar.copy(xT[:, :], ps_f[0][:, :]).then_inc(f_read, 1)

            def conv_act_of(b, c):
                u = 1 + c
                act.wait_ge(f_ready, b * FU + u + 1)
                wait(act, silu_done, b * CC + c - 1 if c >= 2 else b * CC)
                if c < 2:
                    wait(act, zg_ready, b * 2)
                nc.scalar.activation(th[:, c % 2, :], ps_f[u % 2][:, :], ACT.Tanh, bias=half_cb[:, c:c + 1], scale=0.5)
                nc.scalar.activation(hv[:, c % 2, :], ps_f[u % 2][:, :], ACT.Identity, bias=half_cb[:, c:c + 1], scale=0.5)\
                    .then_inc(f_read, 1)

            def z_act_of(b, k):
                u = 1 + CC + k
                act.wait_ge(f_ready, b * FU + u + 1)
                wait(act, silu_done, (b + 1) * CC)
                s = (k + 1) % 2
                nc.scalar.activation(th[:, s, :], ps_f[u % 2][:, :], ACT.Tanh, scale=0.5)
                nc.scalar.activation(hv[:, s, :], ps_f[u % 2][:, :], ACT.Identity, scale=0.5).then_inc(f_read, 1)

            def dt_act(b):
                act.wait_ge(dt_pre, b + 1)
                nc.scalar.activation(dt_abs[:, :], dt_raw[:, :], ACT.Abs).then_inc(dt_ln_done, 1)
                act.wait_ge(dt_ln_done, 3 * b + 1)
                nc.scalar.activation(dt_exp[:, :], dt_abs[:, :], ACT.Exp, scale=-1.0).then_inc(dt_ln_done, 1)
                act.wait_ge(dt_ln_done, 3 * b + 2)
                nc.scalar.activation(dt_ln[:, :], dt_exp[:, :], ACT.Ln, bias=1.0).then_inc(dt_ln_done, 1)

            def cum_act_of(b, half):
                act.wait_ge(cum_dve, b + 1)
                nc.scalar.activation(exp_acum[:, half, :], acum[:, half, :], ACT.Exp)
                nc.scalar.activation(exp_total[:, half, :], ps_small[:, 2 * RH:3 * RH], ACT.Exp)
                nc.scalar.activation(exp_rest[:, :], rest[:, :], ACT.Exp).then_inc(rest_exp, 1)

            def exp_diff(n):
                act.wait_ge(diff_ready, n + 1)
                wait(act, mix_ready, n)
                nc.scalar.activation(ediff[:, :, :], diff[:, :, :], ACT.Exp).then_inc(ediff_ready, 1)

            def copy_c1(n, s):
                act.wait_ge(c1_ready, n + 1)
                wait(act, c2_ready, n - 1)
                wait(act, diff_ready, n - 1)
                wait(act, xD_ready, n - 1)
                nc.scalar.copy(xB[:, s, :], ps_c1[:, P:P + INNER + STATE]).then_inc(c1_copied, 1)

            def square(n, s):
                act.wait_ge(gated_ready, n + 1)
                wait(act, rms_ready, n - 1)
                nc.scalar.activation(squares[:, s, :], gated[:, s, :], ACT.Square, accum_out=sumsq[:, s:s + 1]).then_inc(sq_done, 1)

            def copy_gT(n, s):
                act.wait_ge(gT_ready, n + 1)
                nc.scalar.copy(gT[:, s, :], ps_c3[:, 0:INNER]).then_inc(gT_copied, 1)

            def step(pair, half, r):
                if b := graph_at(pair, half, r, XT_AT):
                    copy_xT(b[0])
                for c in range(CC):
                    if b := graph_at(pair, half, r, SILU_AT[c]):
                        conv_act_of(b[0], c)
                if t := tile_at(pair, half, r, PREP_AT):
                    copy_c1(t[0], t[3] % 2)
                if t := tile_at(pair, half, r, PROJECT_AT):
                    copy_gT(t[0], t[3] % 2)
                if t := tile_at(pair, half, r, PREP_AT):
                    exp_diff(t[0])
                if b := graph_at(pair, half, r, DT_AT):
                    dt_act(b[0])
                if t := tile_at(pair, half, r, 0):
                    square(t[0], t[3] % 2)
                if b := graph_at(pair, half, r, SUMS_AT):
                    cum_act_of(*b)
                if b := graph_at(pair, half, r, Z_AT):
                    z_act_of(b[0], 0)
                    z_act_of(b[0], 1)
            walk(act, step)

        @block.vector
        def _(dve):
            chain = Chain(dve, dve_chain, 0)

            def graph_stats(b, half):
                wait(dve, xn_ready, b - 1)
                for r in range(R):
                    ins = nc.vector.bn_stats(stats[:, half, r, :], X[:, bass.ds(b * N + r * D, D)])
                chain.link(ins)
                alone(dve, env["dve_passed"])
                for r in range(R):
                    ins = nc.vector.bn_aggr(aggr[:, half, r, :], stats[:, half, r, :])
                ins.then_inc(stats_ready, 1)

            def normalize(b, half):
                dve.wait_ge(rstd_ready, b + 1)
                wait(dve, f_ready, FU * (b - 2) + 1)
                for r in range(R):
                    ins = nc.vector.tensor_scalar(xn[:, half, r, :], X[:, bass.ds(b * N + r * D, D)],
                                                  aggr[:, half, r, 0:1], rstd[:, half, r:r + 1], ALU.subtract, ALU.mult)
                ins.then_inc(xn_ready, 1)

            def split_x(b):
                dve.wait_ge(f_read, b * FU + 1)
                wait(dve, f_ready, (b - 1) * FU + 1 + CC)
                chain.link(nc.vector.tensor_copy(xh[:, PAD:], xT[:, :]))
                nc.vector.tensor_tensor(xl[:, PAD:], xT[:, :], xh[:, PAD:].bitcast(F32), ALU.subtract).then_inc(x_split, 1)

            def silu(b, half, c):
                dve.wait_ge(f_read, b * FU + 1 + c + 1)
                wait(dve, c1_ready, (b - 1) * R)
                if c < 2:
                    nc.vector.scalar_tensor_tensor(xc[:, half, c, :], th[:, c % 2, :], 1.0, hv[:, c % 2, :], ALU.add, ALU.mult)\
                        .then_inc(silu_done, 1)
                else:
                    wait(dve, c2_ready, (b - 1) * R)
                    nc.vector.scalar_tensor_tensor(BT[:, half, :], th[0:STATE, 0, :], 1.0, hv[0:STATE, 0, :], ALU.add, ALU.mult)
                    nc.vector.scalar_tensor_tensor(CT[:, half, :], th[STATE:, 0, :], 1.0, hv[STATE:, 0, :], ALU.add, ALU.mult)\
                        .then_inc(silu_done, 1)

            def z_silu(b, half, k):
                dve.wait_ge(f_read, b * FU + 1 + CC + k + 1)
                s = (k + 1) % 2
                nc.vector.scalar_tensor_tensor(zg[:, half, 2 * k:2 * k + 2, :].rearrange("p r c -> p (r c)"), th[:, s, :], 1.0,
                                               hv[:, s, :], ALU.add, ALU.mult).then_inc(zg_ready, 1)

            def dt_first(b):
                dve.wait_ge(dtm_ready, b + 1)
                nc.vector.tensor_tensor(dt_raw[:, :], ps_small[:, 0:RH], dtb[:, :, :].rearrange("p r h -> p (r h)"), ALU.add)\
                    .then_inc(dt_pre, 1)

            def dt_second(b, half):
                dve.wait_ge(dt_ln_done, 3 * b + 3)
                dve.wait_ge(dt_pre, b + 1)
                wait(dve, c1_ready, (b - 1) * R)
                chain.link(nc.vector.scalar_tensor_tensor(dt[:, half, :], dt_raw[:, :], 0.0, dt_ln[:, :], ALU.max, ALU.add))
                nc.vector.tensor_tensor(dA[:, half, :], dt[:, half, :], a_neg[:, :, :].rearrange("p r h -> p (r h)"), ALU.mult)\
                    .then_inc(dA_ready, 1)

            def cum_first(b, half):
                dve.wait_ge(cum_ready, b + 1)
                chain.link(nc.vector.tensor_copy(acum[:, half, :], ps_small[:, RH:2 * RH]))
                wait(dve, rest_exp, b)
                nc.vector.tensor_tensor(rest[:, :], ps_small[:, 2 * RH:3 * RH], acum[:, half, :], ALU.subtract)\
                    .then_inc(cum_dve, 1)

            def cum_second(b, half):
                dve.wait_ge(rest_exp, b + 1)
                nc.vector.tensor_tensor(dt_rest[:, half, :], exp_rest[:, :], dt[:, half, :], ALU.mult).then_inc(front_done, 1)

            def by_head(v, half, r):
                return v[:, half, r * HEADS:(r + 1) * HEADS].unsqueeze(2).to_broadcast([P, HEADS, HEAD])

            def decays(n, b, half, r):
                dve.wait_ge(c1_ready, n + 1)
                wait(dve, ediff_ready, n)
                dve.wait_ge(front_done, b + 1)
                for h in range(HEADS):
                    ins = nc.vector.scalar_tensor_tensor(diff[:, h, :], ps_bc[:, h * P:(h + 1) * P],
                                                         acum[:, half, r * HEADS + h:r * HEADS + h + 1], strict[:, :],
                                                         ALU.subtract, ALU.mult)
                ins.then_inc(diff_ready, 1)

            def mixing(n, half, r):
                s = r % 2
                dve.wait_ge(c1_copied, n + 1)
                wait(dve, mix_ready, n)
                chain.link(nc.vector.tensor_tensor(cb_m[:, :], ps_c1[:, 0:P], tri[:, :], ALU.mult))
                wait(dve, c2_ready, n - 1)
                x_v = xB[:, s, 0:INNER].rearrange("p (h c) -> p h c", c=HEAD)
                nc.vector.tensor_tensor(xdt[:, s, :].rearrange("p (h c) -> p h c", c=HEAD), x_v, by_head(dt, half, r), ALU.mult)
                nc.vector.tensor_tensor(xrest[:, s, :].rearrange("p (h c) -> p h c", c=HEAD), x_v, by_head(dt_rest, half, r),
                                        ALU.mult)
                dve.wait_ge(ediff_ready, n + 1)
                nc.vector.scalar_tensor_tensor(mix[:, s, :, :], ediff[:, :, :], 1.0, cb_m[:, :].unsqueeze(1).to_broadcast([P, HEADS, P]),
                                               ALU.min, ALU.mult).then_inc(mix_ready, 1)

            def chunk_second(n, half, r):
                s = r % 2
                dve.wait_ge(c2_ready, n + 1)
                if r == 0:
                    nc.vector.tensor_copy(state[:, :], ps_s[0:STATE, 0:INNER]).then_inc(state_done, 1)
                else:
                    chain.link(nc.vector.tensor_tensor(
                        decayed[:, :].rearrange("p (h c) -> p h c", c=HEAD), state[:, :].rearrange("p (h c) -> p h c", c=HEAD),
                        exp_total[0:STATE, half, r * HEADS:(r + 1) * HEADS].unsqueeze(2).to_broadcast([STATE, HEADS, HEAD]),
                        ALU.mult))
                    nc.vector.tensor_tensor(state[:, :], decayed[:, :], ps_s[0:STATE, 0:INNER], ALU.add).then_inc(state_done, 1)
                dve.wait_ge(xD_ready, n + 1)
                if r == 0:
                    chain.link(nc.vector.tensor_tensor(y[:, :], ps_c2[:, 0:INNER], xD[:, s, :], ALU.add))
                else:
                    for h in range(HEADS):
                        cols = slice(h * HEAD, (h + 1) * HEAD)
                        ins = nc.vector.scalar_tensor_tensor(y_part[:, cols], ps_c2[:, INNER + h * HEAD:INNER + (h + 1) * HEAD],
                                                             exp_acum[:, half, r * HEADS + h:r * HEADS + h + 1], xD[:, s, cols],
                                                             ALU.mult, ALU.add)
                    chain.link(ins)
                    chain.link(nc.vector.tensor_tensor(y[:, :], y_part[:, :], ps_c2[:, 0:INNER], ALU.add))
                wait(dve, gT_ready, n - 1)
                wait(dve, sq_done, n - 1)
                nc.vector.tensor_tensor(gated[:, s, :], y[:, :], zg[:, half, r, :], ALU.mult).then_inc(gated_ready, 1)

            def update(n, col, s):
                dve.wait_ge(o_ready, n + 1)
                dve.wait_ge(rms_ready, n + 1)
                nc.vector.scalar_tensor_tensor(X[:, bass.ds(col, D)], ps_c3[:, INNER:INNER + D], rms[:, s:s + 1],
                                               X[:, bass.ds(col, D)], ALU.mult, ALU.add).then_inc(x_done, 1)

            chain.per_pair = 2 * (1 + 1 + 1 + 1 + R + 1 + 3 * (R - 1))

            def step(pair, half, r):
                if b := graph_at(pair, half, r, STATS_AT):
                    graph_stats(*b)
                if b := graph_at(pair, half, r, XT_AT):
                    split_x(b[0])
                if b := graph_at(pair, half, r, DT_AT):
                    dt_first(b[0])
                if b := graph_at(pair, half, r, DT2_AT):
                    dt_second(*b)
                if b := graph_at(pair, half, r, CUM2_AT):
                    cum_second(*b)
                if b := graph_at(pair, half, r, ZG_AT):
                    z_silu(*b, 0)
                    z_silu(*b, 1)
                if t := tile_at(pair, half, r, UPDATE_AT):
                    update(t[0], t[0] * D, t[3] % 2)
                if t := tile_at(pair, half, r, 0):
                    chunk_second(t[0], *t[2:])
                for c in range(CC):
                    if b := graph_at(pair, half, r, SILU_AT[c]):
                        silu(*b, c)
                if t := tile_at(pair, half, r, PREP_AT):
                    decays(*t)
                if b := graph_at(pair, half, r, NORM_AT):
                    normalize(*b)
                if t := tile_at(pair, half, r, PREP_AT):
                    mixing(t[0], *t[2:])
                if b := graph_at(pair, half, r, SUMS_AT):
                    cum_first(*b)
            walk(dve, step, chain)
            dve.wait_ge(x_done, B * R)

        @block.tensor
        def _(pe):
            def transposes(b, half):
                pe.wait_ge(xn_ready, b + 1)
                wait(pe, f_read, b * FU - 1)
                for r in range(R):
                    ins = nc.tensor.transpose(ps_f[0][:, r * P:(r + 1) * P], xn[:, half, r, :], ident[:, :])
                ins.then_inc(f_ready, 1)

            def conv(b, c):
                u = 1 + c
                if c == 0:
                    pe.wait_ge(x_split, b + 1)
                wait(pe, f_read, b * FU + u - 1)
                cols = slice(c * P, (c + 1) * P)
                for k in range(TAPS):
                    shift = slice(PAD - (TAPS - 1) + k, PAD - (TAPS - 1) + k + N)
                    nc.tensor.matmul(ps_f[u % 2][:, :], wch[:, k, cols], xh[:, shift], start=k == 0, stop=False)
                    nc.tensor.matmul(ps_f[u % 2][:, :], wch[:, k, cols], xl[:, shift], start=False, stop=False)
                    ins = nc.tensor.matmul(ps_f[u % 2][:, :], wcl[:, k, cols], xh[:, shift], start=False, stop=k == TAPS - 1)
                ins.then_inc(f_ready, 1)

            def z_of(b, k):
                u = 1 + CC + k
                wait(pe, f_read, b * FU + u - 1)
                for j in range(2):
                    r = 2 * k + j
                    ins = nc.tensor.matmul(ps_f[u % 2][:, j * INNER:(j + 1) * INNER], xT[:, r * P:(r + 1) * P], wz[:, :],
                                           start=True, stop=True)
                ins.then_inc(f_ready, 1)

            def dt_of(b):
                wait(pe, rest_exp, b)
                for r in range(R):
                    ins = nc.tensor.matmul(ps_small[:, r * HEADS:(r + 1) * HEADS], xT[:, r * P:(r + 1) * P], wdt_sb[:, :],
                                           start=True, stop=True)
                ins.then_inc(dtm_ready, 1)

            def sums(b, half):
                pe.wait_ge(dA_ready, b + 1)
                nc.tensor.matmul(ps_small[:, RH:2 * RH], tri[:, :], dA[:, half, :], start=True, stop=True)
                nc.tensor.matmul(ps_small[:, 2 * RH:3 * RH], ones[:, :], dA[:, half, :], start=True, stop=True)\
                    .then_inc(cum_ready, 1)

            def chunk_prep(n, b, half, r):
                wait(pe, diff_ready, n)
                wait(pe, c1_copied, n)
                wait(pe, mix_ready, n)
                if r == 0:
                    pe.wait_ge(silu_done, (b + 1) * CC)
                for h in range(HEADS):
                    col = r * HEADS + h
                    nc.tensor.matmul(ps_bc[:, h * P:(h + 1) * P], dA[:, half, col:col + 1].to_broadcast([P, P]), tri[:, :],
                                     start=True, stop=True)
                tile = slice(r * P, (r + 1) * P)
                nc.tensor.matmul(ps_c1[:, 0:P], BT[:, half, tile], CT[:, half, tile], start=True, stop=True)
                for k in range(2):
                    nc.tensor.transpose(ps_c1[:, P + k * P:P + (k + 1) * P], xc[:, half, k, tile], ident[:, :])
                nc.tensor.transpose(ps_c1[:, P + INNER:P + INNER + STATE], BT[:, half, tile], ident[0:STATE, 0:STATE])\
                    .then_inc(c1_ready, 1)

            def chunk_products(n, half, r):
                s = r % 2
                pe.wait_ge(mix_ready, n + 1)
                wait(pe, gated_ready, n)
                wait(pe, state_done, n)
                for h in range(HEADS):
                    nc.tensor.matmul(ps_c2[:, h * HEAD:(h + 1) * HEAD], mix[:, s, h, :], xdt[:, s, h * HEAD:(h + 1) * HEAD],
                                     start=True, stop=True)
                if r > 0:
                    nc.tensor.matmul(ps_c2[:, INNER:2 * INNER], CT[:, half, r * P:(r + 1) * P], state[:, :],
                                     start=True, stop=True)
                nc.tensor.matmul(ps_s[0:STATE, 0:INNER], xB[:, s, INNER:INNER + STATE], xrest[:, s, :],
                                 start=True, stop=True).then_inc(c2_ready, 1)

            def transpose_gated(n, s):
                pe.wait_ge(gated_ready, n + 1)
                wait(pe, x_done, n)
                for k in range(2):
                    ins = nc.tensor.transpose(ps_c3[:, k * P:(k + 1) * P], gated[:, s, k * P:(k + 1) * P], ident[:, :])
                ins.then_inc(gT_ready, 1)

            def project(n, s):
                pe.wait_ge(gT_copied, n + 1)
                for k in range(2):
                    ins = nc.tensor.matmul(ps_c3[:, INNER:INNER + D], gT[:, s, k * P:(k + 1) * P], wo[:, k, :],
                                           start=k == 0, stop=k == 1)
                ins.then_inc(o_ready, 1)

            def step(pair, half, r):
                if b := graph_at(pair, half, r, XT_AT):
                    transposes(*b)
                if t := tile_at(pair, half, r, 0):
                    chunk_products(t[0], *t[2:])
                if t := tile_at(pair, half, r, PREP_AT):
                    chunk_prep(*t)
                if t := tile_at(pair, half, r, PROJECT_AT):
                    transpose_gated(t[0], t[3] % 2)
                if b := graph_at(pair, half, r, SUMS_AT):
                    sums(*b)
                for c in range(CC):
                    if b := graph_at(pair, half, r, CONV_AT[c]):
                        conv(b[0], c)
                        if c == 0:
                            dt_of(b[0])
                if b := graph_at(pair, half, r, Z_AT):
                    z_of(b[0], 0)
                    z_of(b[0], 1)
                if t := tile_at(pair, half, r, PROJECT_AT):
                    project(t[0], t[3] % 2)
            walk(pe, step)


@contextmanager
def expert_weights(nc, name, w1, w2, hidden):
    with nc.semaphore(f"{name}_raw_loaded") as loaded, nc.sbuf_tensor(f"{name}_raw", [P, E, 2, hidden], F32) as raw:
        loads = []
        for e in range(E):
            loads.append((raw[:, e, 0, :], w1[e]))
            loads.append((raw[:, e, 1, :].rearrange("p (c d) -> p c d", d=D), w2[e].rearrange("(c p) d -> p c d", p=P)))
        yield raw, loads, loaded


def build(nc, a, out, layers=range(8), only_load=None):
    ctx = ExitStack()
    with ctx:
        X = ctx.enter_context(nc.sbuf_tensor("X", [P, B * N], F32))
        ident = ctx.enter_context(nc.sbuf_tensor("ident", [P, P], F32))
        minus_half = ctx.enter_context(nc.sbuf_tensor("minus_half", [P, R], F32))
        ident_zero, ident_done = (ctx.enter_context(nc.semaphore(n)) for n in ("ident_zero", "ident_done"))
        dve_passed, pool_passed = (ctx.enter_context(nc.semaphore(n)) for n in ("dve_passed", "pool_passed"))
        out_stored = ctx.enter_context(nc.semaphore("out_stored"))
        mask_dram = nc.dram_tensor("mask_dram", [B, P, R * N], BF16, kind="Internal").ap()
        eps = ctx.enter_context(nc.sbuf_tensor("eps", [P, R], F32))
        env = {"X": X, "ident": ident, "minus_half": minus_half, "eps": eps, "mask_dram": mask_dram,
               "dve_passed": dve_passed, "pool_passed": pool_passed}

        with nc.Block() as block:
            @block.gpsimd
            def _(pool):
                nc.gpsimd.memset(minus_half[:, :], -0.5)
                nc.gpsimd.memset(eps[:, :], LN_EPS)
                nc.gpsimd.memset(ident[:, :], 0.0).then_inc(ident_zero, 1)
                pool.wait_ge(ident_zero, 1)
                nc.gpsimd.affine_select(out=ident[:, :], in_=ident[:, :], compare_op=ALU.not_equal, fill=1.0,
                                        base=0, pattern=[[-1, P]], channel_multiplier=1).then_inc(ident_done, 1)
                pool.wait_ge(ident_done, 1)

        if 0 not in layers:
            only_load(nc, env, a)
        else:
            gnn_layer(nc, env, "g0", a["L0_gnn_W"], a["L0_gnn_Wt"], a["L0_gnn_A"], 1, elu=True,
                      node_mask=True, load=(a["x"], a["adj"], a["nodemask"]))
        if 1 in layers:
            f = {k: a[f"L0_ffn_{k}"] for k in ("W_in", "conv_w", "conv_b", "dt_bias", "A_log", "D", "norm_w", "W_out_t",
                                               "W_lin", "b_lin")}
            mamba_layer(nc, env, "f0", f["W_in"], f["conv_w"], f["conv_b"], f["dt_bias"], f["A_log"], f["D"],
                        f["norm_w"], f["W_out_t"], f["W_lin"], f["b_lin"])
        with expert_weights(nc, "f1", a["L1_ffn_w1"], a["L1_ffn_w2"], 128) as (raw, loads, loaded):
            if 2 in layers:
                gnn_layer(nc, env, "g1", a["L1_gnn_W"], a["L1_gnn_Wt"], a["L1_gnn_A"], 1, prefetch=(loads, loaded))
            if 3 in layers:
                moe_layer(nc, env, "f1", raw, loaded, a["L1_ffn_b1"], a["L1_ffn_b2"],
                          a["L1_ffn_router_w"], None, 128, keep_tokens=True, split_h=False)
        with expert_weights(nc, "f2", a["L2_ffn_W1"], a["L2_ffn_W2"], 512) as (raw, loads, loaded):
            if 4 in layers:
                gnn_layer(nc, env, "g2", a["L2_gnn_W"], a["L2_gnn_Wt"], a["L2_gnn_A"], 1, elu=True, prefetch=(loads, loaded))
            if 5 in layers:
                moe_layer(nc, env, "f2", raw, loaded, a["L2_ffn_b1"], a["L2_ffn_b2"],
                          a["L2_ffn_Wg"], a["L2_ffn_bg"], 512)
        with expert_weights(nc, "f3", a["L3_ffn_W1"], a["L3_ffn_W2"], 512) as (raw, loads, loaded):
            if 6 in layers:
                gnn_layer(nc, env, "g3", a["L3_gnn_W"], a["L3_gnn_Wt"], a["L3_gnn_A"], 4, bias=a["L3_gnn_b"],
                          prefetch=(loads, loaded))
            if 7 in layers:
                moe_layer(nc, env, "f3", raw, loaded, a["L3_ffn_b1"], a["L3_ffn_b2"],
                          a["L3_ffn_Wr"], a["L3_ffn_br"], 512, own_ln=(a["L3_ffn_ln_g"], a["L3_ffn_ln_b"]))

        with nc.Block() as block:
            @block.sync
            def _(sp):
                out_v = out.rearrange("b (r p) d -> p (b r) d", p=P)
                sp.dma_start(out_v, X[:, :].rearrange("p (t d) -> p t d", d=D)).then_inc(out_stored, 16)
                sp.wait_ge(out_stored, 16)


def _layout(inputs):
    arrays = {k: np.ascontiguousarray(v) for k, v in inputs.items()}
    arrays["nodemask"] = np.ascontiguousarray(inputs["nodemask"].reshape(B * R, P).T)
    for l in range(4):
        w, a = arrays.pop(f"L{l}_gnn_W"), arrays.pop(f"L{l}_gnn_a")
        if l >= 2:
            w = w.T
        arrays[f"L{l}_gnn_W"], arrays[f"L{l}_gnn_Wt"] = np.ascontiguousarray(w), np.ascontiguousarray(w.T)
        heads = a.shape[0] if l == 3 else 1
        a = a.reshape(heads, 2, D // heads)
        cols = np.zeros((D, P), a.dtype)
        for h in range(heads):
            for q in range(4):
                cols[h * (D // heads):(h + 1) * (D // heads), 32 * q + h] = a[h, q // 2]
        arrays[f"L{l}_gnn_A"] = cols
    for name in ("L0_ffn_conv_b", "L0_ffn_norm_w"):
        arrays[name] = np.ascontiguousarray(arrays[name].reshape(-1, P).T)
    arrays["L0_ffn_conv_w"] = np.ascontiguousarray(arrays["L0_ffn_conv_w"].T)
    arrays["L0_ffn_W_out_t"] = np.ascontiguousarray(arrays.pop("L0_ffn_W_out").T)
    arrays["L1_ffn_router_w"] = np.ascontiguousarray(arrays["L1_ffn_router_w"].T)
    for l in (1, 2, 3):
        name = f"L{l}_ffn_b1"
        arrays[name] = np.ascontiguousarray(arrays[name].reshape(-1, P).T)
        arrays[f"L{l}_ffn_b2"] = np.ascontiguousarray(arrays[f"L{l}_ffn_b2"].T)
    for name in ("L3_ffn_ln_g", "L3_ffn_ln_b"):
        arrays[name] = np.ascontiguousarray(arrays[name].T)
    return arrays


def kernel(**inputs):
    import concourse.bacc as bacc
    from concourse.bass_utils import run_bass_kernel_spmd

    arrays = {f"in_{k}": v for k, v in _layout(inputs).items()}
    nc = bacc.Bacc("TRN2", target_bir_lowering=False, num_devices=1)
    aps = {k[3:]: nc.dram_tensor(k, v.shape, mybir.dt.from_np(v.dtype), kind="ExternalInput").ap()
           for k, v in arrays.items()}
    out = nc.dram_tensor("out", [B, N, D], F32, kind="ExternalOutput").ap()
    build(nc, aps, out)
    r = run_bass_kernel_spmd(nc, [arrays], core_ids=[0])
    return r.results[0]["out"]
```
